# Optimizing a Trainium2 kernel written in Bass

```python
import numpy as np
import jax
import jax.numpy as jnp

def _softmax(x, axis=-1):
    return jax.nn.softmax(x, axis=axis)

def _gelu(x):
    return jax.nn.gelu(x, approximate=True)

def _silu(x):
    return jax.nn.silu(x)

def _sigmoid(x):
    return jax.nn.sigmoid(x)

def _layernorm(x, axis=-1, eps=1e-05):
    m = jnp.mean(x, axis=axis, keepdims=True)
    v = jnp.var(x, axis=axis, keepdims=True)
    return (x - m) / jnp.sqrt(v + eps)

def _scatter_add(tgt, idx, src, axis=0):
    return tgt.at[idx].add(src)

def _segment_sum(src, seg, n):
    return jax.ops.segment_sum(src, seg, n)
kernel_name = 'mk_decoder_preln_d1_seqx_r8_c47a27'

def setup_inputs(seed: int=0):
    np.random.seed(seed)
    _w = jnp.asarray

    def _rec_inputs():
        import jax
        import jax.numpy as jnp
        _rk = jax.random.key(seed)
        x = -0.0002928 + 1 * jax.random.normal(jax.random.fold_in(_rk, 1), (4, 256, 256), jnp.float32)
        _lenS = 256 - jax.random.randint(jax.random.fold_in(_rk, 7), (4,), 0, max(1, 256 // 4) + 1, jnp.int32)
        _lenS2 = 1601 - jax.random.randint(jax.random.fold_in(_rk, 8), (4,), 0, max(1, 1601 // 4) + 1, jnp.int32)
        _ctx_512P = jax.random.normal(jax.random.fold_in(_rk, 11), (4, 16, 64), jnp.float32)
        _ctx_512c = jax.random.dirichlet(jax.random.fold_in(_rk, 511), 0.3 * jnp.ones((16,), jnp.float32), (4, 1601))
        _ctx_512t = jnp.einsum('bsk,bkd->bsd', _ctx_512c, _ctx_512P)
        _ctx_512t = _ctx_512t * jax.lax.rsqrt(jnp.mean(jnp.square(_ctx_512t)) + 1e-12) * 0.953939
        ctx_512 = 0.000227908 + 0.99994 * (_ctx_512t + 0.3 * jax.random.normal(jax.random.fold_in(_rk, 611), (4, 1601, 64), jnp.float32))
        return (x, ctx_512)
    x, ctx_512 = _rec_inputs()

    def _L0_attn_setup():
        import jax, jax.numpy as jnp
        import numpy as np
        B, S, H = (4, 256, 256)
        key = jax.random.key(seed)
        k1, k2, k3 = jax.random.split(key, 3)
        xav_qkv = float(np.sqrt(6.0 / (H + 3 * H)))
        xav_out = float(np.sqrt(6.0 / (H + H)))
        return {'hidden_states': jax.random.normal(k1, (B, S, H), dtype=jnp.float32), 'w_qkv': jax.random.uniform(k2, (3 * H, H), minval=-xav_qkv, maxval=xav_qkv, dtype=jnp.float32), 'b_qkv': jnp.zeros((3 * H,), dtype=jnp.float32), 'w_out': jax.random.uniform(k3, (H, H), minval=-xav_out, maxval=xav_out, dtype=jnp.float32), 'b_out': jnp.zeros((H,), dtype=jnp.float32)}
    _L0_attn_all = _L0_attn_setup()
    _L0_attn_in = {k: v for k, v in _L0_attn_all.items() if k in ('w_qkv', 'b_qkv', 'w_out', 'b_out')}
    del _L0_attn_all

    def _L0_xattn_setup():
        import jax, jax.numpy as jnp
        import numpy as np
        B, S, L = (2, 128, 128)
        DIM_Q, H, K, D_C, D_CQ, R = (256, 16, 128, 64, 192, 64)

        def _rope_tables(seq_len, dim, dtype):
            inv_freq = 1.0 / 10000.0 ** (jnp.arange(0, dim, 2, dtype=dtype) / dim)
            t = jnp.arange(seq_len, dtype=dtype)
            freqs = t[:, None] * inv_freq[None, :]
            sin = jnp.repeat(jnp.sin(freqs), 2, axis=-1)
            cos = jnp.repeat(jnp.cos(freqs), 2, axis=-1)
            return (sin, cos)

        def _rotate_half(x):
            h = x.shape[-1] // 2
            return jnp.concatenate([-x[..., h:], x[..., :h]], axis=-1)
        key = jax.random.key(seed)
        ks = jax.random.split(key, 8)
        s_in = 1.0 / np.sqrt(DIM_Q)
        s_k = 1.0 / np.sqrt(K)
        s_cq = 1.0 / np.sqrt(D_CQ)
        s_c = 1.0 / np.sqrt(D_C)
        return {'hidden_q': jax.random.normal(ks[0], (B, S, DIM_Q), jnp.float32), 'kv_c': jax.random.normal(ks[1], (B, L, D_C), jnp.float32), 'Wq': jax.random.normal(ks[2], (H * K, DIM_Q), jnp.float32) * s_in, 'w_kc_q': jax.random.normal(ks[3], (H, K, D_CQ), jnp.float32) * s_k, 'w_kc_kv': jax.random.normal(ks[4], (H, K, D_C), jnp.float32) * s_k, 'W_qr': jax.random.normal(ks[5], (H, D_CQ, R), jnp.float32) * s_cq / np.sqrt(R), 'W_kr': jax.random.normal(ks[6], (H, D_C, R), jnp.float32) * s_c, 'Wo': jax.random.normal(ks[7], (DIM_Q, H * K), jnp.float32) * s_k}
    _L0_xattn_all = _L0_xattn_setup()
    _L0_xattn_in = {k: v for k, v in _L0_xattn_all.items() if k in ('Wq', 'w_kc_q', 'w_kc_kv', 'W_qr', 'W_kr', 'Wo')}
    del _L0_xattn_all

    def _L0_ffn_setup():
        import jax, jax.numpy as jnp
        import numpy as np
        H = 256
        I = 176
        E = 16
        K = 2
        SI = I * 2

        def _swiglu(gu, inter):
            g, u = (gu[..., :inter], gu[..., inter:])
            return jax.nn.silu(g) * u
        key = jax.random.key(seed)
        ks = jax.random.split(key, 6)
        s = 0.02
        hidden_states = jax.random.normal(ks[0], (1, 128, H), dtype=jnp.float32)
        gate_w = jax.random.normal(ks[1], (E, H), dtype=jnp.float32) * s
        w_gate_up = jax.random.normal(ks[2], (E, H, 2 * I), dtype=jnp.float32) * s
        w_down = jax.random.normal(ks[3], (E, I, H), dtype=jnp.float32) * s
        shared_gate_up = jax.random.normal(ks[4], (H, 2 * SI), dtype=jnp.float32) * s
        shared_down = jax.random.normal(ks[5], (SI, H), dtype=jnp.float32) * s
        return {'hidden_states': hidden_states, 'gate_w': gate_w, 'w_gate_up': w_gate_up, 'w_down': w_down, 'shared_gate_up': shared_gate_up, 'shared_down': shared_down}
    _L0_ffn_all = _L0_ffn_setup()
    _L0_ffn_in = {k: v for k, v in _L0_ffn_all.items() if k in ('gate_w', 'w_gate_up', 'w_down', 'shared_gate_up', 'shared_down')}
    del _L0_ffn_all
    return {'x': x, 'ctx_512': ctx_512, 'L0_attn_w_qkv': _L0_attn_in['w_qkv'], 'L0_attn_b_qkv': _L0_attn_in['b_qkv'], 'L0_attn_w_out': _L0_attn_in['w_out'], 'L0_attn_b_out': _L0_attn_in['b_out'], 'L0_xattn_Wq': _L0_xattn_in['Wq'], 'L0_xattn_w_kc_q': _L0_xattn_in['w_kc_q'], 'L0_xattn_w_kc_kv': _L0_xattn_in['w_kc_kv'], 'L0_xattn_W_qr': _L0_xattn_in['W_qr'], 'L0_xattn_W_kr': _L0_xattn_in['W_kr'], 'L0_xattn_Wo': _L0_xattn_in['Wo'], 'L0_ffn_gate_w': _L0_ffn_in['gate_w'], 'L0_ffn_w_gate_up': _L0_ffn_in['w_gate_up'], 'L0_ffn_w_down': _L0_ffn_in['w_down'], 'L0_ffn_shared_gate_up': _L0_ffn_in['shared_gate_up'], 'L0_ffn_shared_down': _L0_ffn_in['shared_down']}

def reference(x, ctx_512, L0_attn_w_qkv, L0_attn_b_qkv, L0_attn_w_out, L0_attn_b_out, L0_xattn_Wq, L0_xattn_w_kc_q, L0_xattn_w_kc_kv, L0_xattn_W_qr, L0_xattn_W_kr, L0_xattn_Wo, L0_ffn_gate_w, L0_ffn_w_gate_up, L0_ffn_w_down, L0_ffn_shared_gate_up, L0_ffn_shared_down):
    import jax
    import jax.numpy as jnp

    def _L0_attn_ref(hidden_states, w_qkv, b_qkv, w_out, b_out):
        import jax, jax.numpy as jnp
        import numpy as np
        B, S, H = (4, 256, 256)
        Bc, Sc, Hc = hidden_states.shape
        scaling = jnp.sqrt(jnp.asarray(Hc, hidden_states.dtype))
        qkv = jnp.einsum('bsh,oh->bso', hidden_states, w_qkv) + b_qkv
        q, k, v = jnp.split(qkv, 3, axis=-1)
        scores = jnp.einsum('bqh,bkh->bqk', q, k) / scaling
        probs = jax.nn.softmax(scores, axis=-1)
        context = jnp.einsum('bqk,bkh->bqh', probs, v)
        out = jnp.einsum('bsh,oh->bso', context, w_out) + b_out
        return out

    def _L0_xattn_ref(hidden_q, kv_c, Wq, w_kc_q, w_kc_kv, W_qr, W_kr, Wo):
        import jax, jax.numpy as jnp
        import numpy as np
        B, S, L = (2, 128, 128)
        DIM_Q, H, K, D_C, D_CQ, R = (256, 16, 128, 64, 192, 64)

        def _rope_tables(seq_len, dim, dtype):
            inv_freq = 1.0 / 10000.0 ** (jnp.arange(0, dim, 2, dtype=dtype) / dim)
            t = jnp.arange(seq_len, dtype=dtype)
            freqs = t[:, None] * inv_freq[None, :]
            sin = jnp.repeat(jnp.sin(freqs), 2, axis=-1)
            cos = jnp.repeat(jnp.cos(freqs), 2, axis=-1)
            return (sin, cos)

        def _rotate_half(x):
            h = x.shape[-1] // 2
            return jnp.concatenate([-x[..., h:], x[..., :h]], axis=-1)
        b, s, _ = hidden_q.shape
        l = kv_c.shape[1]
        q_hk = (hidden_q @ Wq.T).reshape(b, s, H, K)
        q_big = jnp.einsum('bshk,hkq->bshq', q_hk, w_kc_q)
        sin, cos = _rope_tables(l, D_C, kv_c.dtype)
        kv_rope = kv_c * cos[None] + _rotate_half(kv_c) * sin[None]
        q_r = jnp.einsum('bshq,hqr->bhsr', q_big, W_qr)
        k_r = jnp.einsum('bld,hdr->bhlr', kv_rope, W_kr)
        scores = jnp.einsum('bhsr,bhlr->bhsl', q_r, k_r)
        attn = jax.nn.softmax(scores, axis=-1)
        ctx_c = jnp.einsum('bhsl,bld->bhsd', attn, kv_rope)
        ctx_lat = jnp.einsum('bhsd,hkd->bshk', ctx_c, w_kc_kv)
        out = ctx_lat.reshape(b, s, H * K) @ Wo.T
        return out

    def _L0_ffn_ref(hidden_states, gate_w, w_gate_up, w_down, shared_gate_up, shared_down):
        import jax, jax.numpy as jnp
        import numpy as np
        H = 256
        I = 176
        E = 16
        K = 2
        SI = I * 2

        def _swiglu(gu, inter):
            g, u = (gu[..., :inter], gu[..., inter:])
            return jax.nn.silu(g) * u
        orig_shape = hidden_states.shape
        x = hidden_states.reshape(-1, H)
        logits = jnp.einsum('th,eh->te', x, gate_w)
        scores = jax.nn.softmax(logits, axis=-1)
        topk_w, topk_idx = jax.lax.top_k(scores, K)
        combine = jnp.sum(jax.nn.one_hot(topk_idx, E, dtype=x.dtype) * topk_w[..., None], axis=1)
        gu = jnp.einsum('th,ehj->etj', x, w_gate_up)
        h = _swiglu(gu, I)
        y = jnp.einsum('eti,eih,te->th', h, w_down, combine)
        gu_s = x @ shared_gate_up
        y = y + _swiglu(gu_s, SI) @ shared_down
        return y.reshape(orig_shape)
    x = x + _L0_attn_ref(_layernorm(x, axis=-1), L0_attn_w_qkv, L0_attn_b_qkv, L0_attn_w_out, L0_attn_b_out)
    x = x + _L0_xattn_ref(_layernorm(x, axis=-1), ctx_512, L0_xattn_Wq, L0_xattn_w_kc_q, L0_xattn_w_kc_kv, L0_xattn_W_qr, L0_xattn_W_kr, L0_xattn_Wo)
    x = x + _L0_ffn_ref(_layernorm(x, axis=-1), L0_ffn_gate_w, L0_ffn_w_gate_up, L0_ffn_w_down, L0_ffn_shared_gate_up, L0_ffn_shared_down)
    return x

_drawn_inputs = setup_inputs


def setup_inputs(seed=0):
    import zlib

    import numpy as np

    out = dict(_drawn_inputs(seed))
    spreads = {'L0_attn_b_qkv': (0.0, 0.1), 'L0_attn_b_out': (0.0, 0.1)}
    factors = {'L0_ffn_gate_w': 8.0,
     'L0_ffn_w_gate_up': 8.0,
     'L0_ffn_w_down': 8.0,
     'L0_ffn_shared_gate_up': 3.83,
     'L0_ffn_shared_down': 3.844}
    for name, (base, spread) in spreads.items():
        noise = np.random.default_rng([zlib.crc32(name.encode()), seed]).standard_normal(out[name].shape)
        drawn = base * np.exp(spread * noise) if base else spread * noise
        out[name] = jnp.asarray(drawn.astype(out[name].dtype))
    for name, factor in factors.items():
        out[name] = (out[name] * factor).astype(out[name].dtype)
    return out
```

```python
from contextlib import ExitStack

import numpy as np

import concourse.bass as bass
from concourse import mybir
from concourse.alu_op_type import AluOpType as ALU

B, S, D = 4, 256, 256
L, DC = 1601, 64
H, HK, DQ, R = 16, 128, 192, 64
E, I = 16, 176
P = 128
T = B * S
TT = T // P
KD = D // P
KT = -(-L // P)
LAST = L - (KT - 1) * P
UNITS = 4
G = B * UNITS
C = 4 * S
QT = C // P
CW = 402
NCHUNK = QT * 2
SHARED = 2 * I
NF = -(-(E * I + SHARED) // P)
FW = 2 * KD * P + D + P
EPS = 1e-5
CROW = 32


def build(nc, x, ctxk, rope, wqkv, bqk, bvo, wout, wq, wkcq, wqr, wkr, wkckv, wo, gate, ffw, consts, out):
    f32, f32r = mybir.dt.float32, mybir.dt.float32r
    ACT, AX = mybir.ActivationFunctionType, mybir.AxisListType
    es = ExitStack()
    with es:
        def sb(name, shape, dt=f32):
            return es.enter_context(nc.sbuf_tensor(name, shape, dt))

        def sem(name):
            return es.enter_context(nc.semaphore(name))

        x_sb = sb("x_sb", [P, TT, D])
        hT = sb("hT", [P, KD, T])
        A_sb = sb("A_sb", [P, KD, UNITS * 256])
        Bo_sb = sb("Bo_sb", [P, 8, D])
        ident = sb("ident", [P, P])
        rank = sb("rank", [P, TT, E])
        ones64 = sb("ones64", [P, 64])
        bqk_sb = sb("bqk_sb", [P, 4])
        bvo_sb = sb("bvo_sb", [P, 2, D])
        gate_sb = sb("gate_sb", [P, KD * E])
        xn = sb("xn", [P, 4, D])
        stats = sb("stats", [P, 4, 6])
        mv = sb("mv", [P, 4, 2])
        lnw = sb("lnw", [P, 5, 4])
        smx = sb("smx", [P, 2, 4, 2])
        big = sb("big", [P, 25088])

        def part(lo, hi, rows=P, **dims):
            a = big[0:rows, lo:hi]
            return a.rearrange("p (a n) -> p a n", **dims) if dims else a

        wq_sb = part(0, 4096, a=H)
        wkcq_sb = part(4096, 7168, a=H)
        qkT = part(7168, 11264, a=4)
        wo_sb = part(7168, 11264, a=H)
        wqkv_sb = part(11264, 12800, a=KD)
        wout_sb = part(12800, 13312, a=KD)
        v_sb = part(13312, 15360, a=TT)
        pr = big[:, 15360:16384].rearrange("p (s q k) -> p s q k", s=2, q=2)
        prT = part(16384, 16896, a=2)
        cxT = big[:, 16896:17920].rearrange("p (s k n) -> p s k n", s=2, k=KD)
        wkr_sb = part(17920, 18944, R, a=H)
        wkckv_sb = part(18944, 19968, HK, a=H)
        wqr_sb = big[0:96, 19968:22016].rearrange("p (h b r) -> p h b r", h=H, b=2)
        DT = big[0:96, 22016:23040].rearrange("p (s b n) -> p s b n", s=2, b=2)
        ET = part(23040, 25088, R, a=8)
        ctxn = part(0, 8192, a=G)
        probs = part(8192, 12288, a=4)
        accD = part(12288, 14336, a=2)
        accP = big[:, 14336:15360]
        nctx = big[:, 15360:15872]
        est = big[:, 15872:16384]
        corr = big[:, 16384:16896]
        kraw = sb("kraw", [P, KT, DC])
        kcos = sb("kcos", [P, 2, KT, DC])
        kt2 = sb("kt2", [P, KT, DC])
        kvn = sb("kvn", [P, 2, KT, DC])
        mxp = sb("mxp", [P, QT, 2])
        mx = sb("mx", [P, QT])
        mrow = sb("mrow", [QT, 2, 2, P], f32r)
        arr = sb("arr", [P, 11264], f32r)
        Q1 = arr[:, 0:2048].rearrange("p (s n) -> p s n", s=2)
        Q2 = arr[:, 2048:4096].rearrange("p (s n) -> p s n", s=2)
        kcat = arr[:, 4096:7424].rearrange("p (s n) -> p s n", s=2)
        khs = arr[:, 7424:10752].rearrange("p (s n) -> p s n", s=2)
        xhi = arr[:, 0:2048].rearrange("p (k n) -> p k n", k=KD)
        xlo = arr[:, 2048:4096].rearrange("p (k n) -> p k n", k=KD)
        whi = arr[:, 4096:4096 + 2 * FW].rearrange("p (s n) -> p s n", s=2)
        wlo = arr[:, 4096 + 2 * FW:4096 + 4 * FW].rearrange("p (s n) -> p s n", s=2)
        hhi = arr[:, 7680:8704].rearrange("p (s n) -> p s n", s=2)
        hlo = arr[:, 8704:9728].rearrange("p (s n) -> p s n", s=2)
        cT = arr[0:64, 9728:10752]
        ghi = arr[:, 10752:10784]
        glo = arr[:, 10784:10816]
        wring = big[:, 8192:8192 + 3 * FW].rearrange("p (s n) -> p s n", s=3)
        silu = big[:, 12288:13312].rearrange("p (s n) -> p s n", s=2)
        hsu = big[:, 13312:14336].rearrange("p (s n) -> p s n", s=2)
        hful = big[:, 14336:15360].rearrange("p (s n) -> p s n", s=2)
        rt = big[:, 17000:17000 + 6 * TT * E].rearrange("p (a t e) -> p a t e", a=6, t=TT)
        rs = sb("rs", [P, 6, TT])
        comb = sb("comb", [P, TT, E + 1])

        ps = es.enter_context(nc.psum_tensor("ps", [P, 8, 512], f32))

        loads = {}

        def arrived(eng, name):
            eng.wait_ge(loads[name], 16)

        names = ["x0", "x1", "consts", "wqkv", "bias", "wout", "wkr", "wkckv", "wqr", "gate", "rope"]
        names += [f"wkcq{i}" for i in range(4)] + [f"wq{i}" for i in range(4)] + [f"wo{i}" for i in range(4)]
        for n in names:
            loads[n] = sem("ld_" + n)
        ld_ctx = sem("ld_ctx")
        ld_ffw = [sem(f"ld_ffw{i}") for i in range(3)]

        def head_jobs(h):
            return [("D", h), ("E", h)]

        self_jobs = [("S", 0), ("S", 1), ("T", 0), ("S", 2), ("C", 0), ("T", 1), ("O", 0), ("S", 3), ("C", 1), ("T", 2),
                     ("O", 1), ("LN2", 0), ("C", 2), ("T", 3), ("O", 2), ("C", 3), ("O", 3), ("LN2", 1)]
        jobs = [("LN1", 0), ("LN1", 1), ("LT1", 0), ("LT1", 1), ("LT1", 2), ("LT1", 3)]
        jobs += [("QK", m) for m in range(8)] + [("V", j) for j in range(4)]
        h = 0
        for j in self_jobs:
            jobs.append(j)
            if j[0] in "SCTO":
                jobs += head_jobs(h)
                h += 1
                if h % 4 == 0:
                    jobs.append(("A", h // 4 - 1))
        assert h == H
        jobs += [("W", u) for u in range(4)] + [("LT2", i) for i in range(4)] + [("K", i) for i in range(4)]
        evac_by = {"LT1": "act", "QK": "act", "V": "dve", "S": "act", "T": "act", "C": "dve", "O": "dve", "D": "act",
                   "E": "dve", "A": "dve", "W": "act", "LT2": "act", "K": "dve"}
        bank_jobs = [j for j in jobs if j[0][:2] != "LN"]
        bank_of, filled, done = {}, {}, {}
        count = {"act": 0, "dve": 0}
        for i, j in enumerate(bank_jobs):
            bank_of[j], filled[j] = i % 8, i + 1
            count[evac_by[j[0]]] += 1
            done[j] = count[evac_by[j[0]]]
        s_bank = sem("s_bank")
        s_evac = {"act": sem("s_evac_act"), "dve": sem("s_evac_dve")}

        def evacuated(eng, j):
            eng.wait_ge(s_evac[evac_by[j[0]]], done[j])

        s_link = sem("s_link")
        s_alink = sem("s_alink")
        s_ln_var = sem("s_ln_var")
        s_ln_est = sem("s_ln_est")
        s_xn = sem("s_xn")
        s_smax = sem("s_smax")
        s_probs = sem("s_probs")
        s_const = sem("s_const")
        s_rope = sem("s_rope")
        s_kraw = sem("s_kraw")
        s_plink = sem("s_plink")
        s_ktr = sem("s_ktr")
        s_khi = sem("s_khi")
        s_klo = sem("s_klo")
        s_qp = sem("s_qp")
        s_qhi = sem("s_qhi")
        s_qlo = sem("s_qlo")
        s_mch = sem("s_mch")
        s_mrd = sem("s_mrd")
        s_mx = sem("s_mx")
        s_mt = sem("s_mt")
        s_mrow = sem("s_mrow")
        s_mq = sem("s_mq")
        s_sc = sem("s_sc")
        s_exp = sem("s_exp")
        s_pv = sem("s_pv")
        s_addD = sem("s_addD")
        s_addP = sem("s_addP")
        s_acc = sem("s_acc")
        s_ctx = sem("s_ctx")
        s_sum = sem("s_sum")
        s_est = sem("s_est")
        s_rec = sem("s_rec")
        s_norm = sem("s_norm")
        s_o2 = sem("s_o2")
        s_x2 = sem("s_x2")
        s_l3 = sem("s_l3")
        s_xhi = sem("s_xhi")
        s_xlo = sem("s_xlo")
        s_gs = sem("s_gs")
        s_lg = sem("s_lg")
        s_rsub = sem("s_rsub")
        s_rexp = sem("s_rexp")
        s_comb = sem("s_comb")
        s_ct = sem("s_ct")
        s_cthi = sem("s_cthi")
        s_ctlo = sem("s_ctlo")
        s_c0 = sem("s_c0")
        s_whi = sem("s_whi")
        s_wlo = sem("s_wlo")
        s_g = sem("s_g")
        s_u = sem("s_u")
        s_silu = sem("s_silu")
        s_hu = sem("s_hu")
        s_hc = sem("s_hc")
        s_hhi = sem("s_hhi")
        s_hlo = sem("s_hlo")
        s_dn = sem("s_dn")
        s_fin = sem("s_fin")
        s_out = sem("s_out")

        NH = 2 * NF
        CHUNKS = (0, 2, 2, 1, 2, 1, 2, 1, 2, 1, 2, 0, 0)
        SLOTS = {0: (), 1: (1,), 2: (0, 2)}
        KPREP_AT = {5: 0, 7: 1, 9: 2, 10: 3}
        assert sum(CHUNKS) == NCHUNK

        def chunks_beside(kt):
            return range(sum(CHUNKS[:kt]), sum(CHUNKS[:kt + 1]))

        def kgroup(i):
            return range(4 * i, min(4 * i + 4, KT))

        def releasedD(kt):
            return max(1, kt // 2)

        def releasedP(kt):
            return max(1, (kt - 1) // 2)

        block = es.enter_context(nc.Block())

        @block.sync
        def _(sp):
            def load(name, dst, src):
                sp.dma_start(dst, src).then_inc(loads[name], 16)

            load("x0", x_sb[:, 0:4, :], x[:, 0:4, :])
            load("x1", x_sb[:, 4:8, :], x[:, 4:8, :])
            sp.dma_start(ident[:, :], consts[:, 0:P]).then_inc(loads["consts"], 16)
            sp.dma_start(rank[:, :, :], consts[:, P:2 * P].rearrange("p (t e) -> p t e", t=TT)).then_inc(loads["consts"], 16)
            load("wqkv", wqkv_sb[:, :, :], wqkv)
            sp.dma_start(bqk_sb[:, :], bqk).then_inc(loads["bias"], 16)
            sp.dma_start(bvo_sb[:, :, :], bvo).then_inc(loads["bias"], 16)
            load("wkcq0", wkcq_sb[:, 0:4, :], wkcq[:, 0:4, :])
            load("wq0", wq_sb[:, 0:4, :], wq[:, 0:4, :])
            load("wqr", wqr_sb[:, :, :, :], wqr)
            load("wout", wout_sb[:, :, :], wout)
            load("wkr", wkr_sb[:, :, :], wkr)
            for i in range(1, 4):
                hs = slice(4 * i, 4 * i + 4)
                load(f"wkcq{i}", wkcq_sb[:, hs, :], wkcq[:, hs, :])
                load(f"wq{i}", wq_sb[:, hs, :], wq[:, hs, :])
            sp.dma_start(kraw[:, :, :], ctxk[0]).then_inc(ld_ctx, 16)
            load("rope", kcos[:, :, :, :], rope)
            load("wkckv", wkckv_sb[:, :, :], wkckv)
            load("gate", gate_sb[:, :], gate)
            sp.wait_ge(s_bank, filled[("S", B - 1)])
            for i in range(4):
                hs = slice(4 * i, 4 * i + 4)
                load(f"wo{i}", wo_sb[:, hs, :], wo[:, hs, :])
            for g in range(-1, G - 1):
                if g >= 0 and g % UNITS == 0 and g // UNITS + 1 < B:
                    sp.wait_ge(s_kraw, g // UNITS + 1)
                    sp.dma_start(kraw[:, :, :], ctxk[g // UNITS + 1]).then_inc(ld_ctx, 16)
                n = g + 1
                sp.wait_ge(s_mrow, n + 1)
                if n >= 2:
                    sp.wait_ge(s_sc, 2 * KT * (n - 1))
                for half in range(2):
                    sp.dma_start(Q2[64 + half:65 + half, n % 2, :].rearrange("o (t q) -> o t q", t=QT).bitcast(f32),
                                 mrow[:, n % 2, half, :].bitcast(f32)).then_inc(s_mq, 16)
            for c in range(NF):
                if c == 0:
                    sp.wait_ge(s_pv, KT * G)
                    sp.wait_ge(s_acc, G)
                if c >= 3:
                    sp.wait_ge(s_whi, c - 2)
                    sp.wait_ge(s_wlo, c - 2)
                sp.dma_start(wring[:, c % 3, :], ffw[c]).then_inc(ld_ffw[c % 3], 16)
            for i in range(4):
                sp.wait_ge(s_fin, i + 1)
                sp.dma_start(out[:, 2 * i:2 * i + 2, :], x_sb[:, 2 * i:2 * i + 2, :]).then_inc(s_out, 16)
            sp.wait_ge(s_out, 64)

        @block.tensor
        def _(pe):
            mm = nc.tensor.matmul

            def fresh_bank(j):
                i = filled[j] - 1
                if i >= 8:
                    evacuated(pe, bank_jobs[i - 8])

            def key_transposes(out_bank, b, i):
                for n, kt in enumerate(kgroup(i)):
                    last = nc.tensor.transpose(ps[0:DC, out_bank, n * P:(n + 1) * P], kvn[:, b % 2, kt, :], ident[:, :])
                return last

            for kind, i in jobs:
                j = (kind, i)
                if kind[:2] == "LN":
                    continue
                bk = bank_of[j]
                fresh_bank(j)
                if kind in ("LT1", "LT2"):
                    k, half = i % 2, i // 2
                    if j == ("LT1", 0):
                        pe.wait_ge(loads["consts"], 32)
                    pe.wait_ge(s_xn, (half + 1) if kind == "LT1" else half + 3)
                    for t in range(4):
                        last = nc.tensor.transpose(ps[:, bk, t * P:(t + 1) * P], xn[:, t, k * P:(k + 1) * P], ident[:, :])
                elif kind == "QK":
                    m, half = i % 4, i // 4
                    if i == 0:
                        arrived(pe, "wqkv")
                    evacuated(pe, ("LT1", 2 * half + 1))
                    for k in range(KD):
                        last = mm(ps[:, bk, :], wqkv_sb[:, k, m * P:(m + 1) * P], hT[:, k, half * 512:half * 512 + 512],
                                  start=k == 0, stop=k == KD - 1)
                elif kind == "V":
                    for t in range(2):
                        tok = (2 * i + t) * P
                        for k in range(KD):
                            last = mm(ps[:, bk, t * D:(t + 1) * D], hT[:, k, tok:tok + P], wqkv_sb[:, k, 2 * D:3 * D],
                                      start=k == 0, stop=k == KD - 1)
                elif kind == "S":
                    evacuated(pe, ("QK", 4 * (i // 2) + 3))
                    for q in range(2):
                        tok = i * S + q * P
                        for k in range(KD):
                            last = mm(ps[:, bk, q * S:(q + 1) * S], qkT[:, k, tok:tok + P], qkT[:, KD + k, i * S:(i + 1) * S],
                                      start=k == 0, stop=k == KD - 1)
                elif kind == "T":
                    pe.wait_ge(s_probs, i + 1)
                    for k in range(2):
                        for q in range(2):
                            last = nc.tensor.transpose(ps[:, bk, k * S + q * P:k * S + (q + 1) * P],
                                                       pr[:, i % 2, q, k * P:(k + 1) * P], ident[:, :])
                elif kind == "C":
                    evacuated(pe, ("T", i))
                    evacuated(pe, ("V", i))
                    for m in range(KD):
                        for k in range(2):
                            last = mm(ps[:, bk, m * S:(m + 1) * S], v_sb[:, 2 * i + k, m * P:(m + 1) * P], prT[:, k, :],
                                      start=k == 0, stop=k == 1)
                elif kind == "O":
                    evacuated(pe, ("C", i))
                    if i == 0:
                        arrived(pe, "wout")
                    for t in range(2):
                        for k in range(KD):
                            last = mm(ps[:, bk, t * D:(t + 1) * D], cxT[:, i % 2, k, t * P:(t + 1) * P], wout_sb[:, k, :],
                                      start=k == 0, stop=k == KD - 1)
                elif kind == "D":
                    if i % 4 == 0:
                        arrived(pe, f"wkcq{i // 4}")
                        arrived(pe, f"wq{i // 4}")
                    for b in range(2):
                        last = mm(ps[0:96, bk, b * D:(b + 1) * D], wkcq_sb[:, i, 96 * b:96 * b + 96], wq_sb[:, i, :],
                                  start=True, stop=True)
                elif kind == "E":
                    if i == 0:
                        arrived(pe, "wqr")
                    evacuated(pe, ("D", i))
                    for b in range(2):
                        last = mm(ps[0:R, bk, 0:D], wqr_sb[:, i, b, :], DT[:, i % 2, b, :], start=b == 0, stop=b == 1)
                elif kind == "A":
                    if i == 0:
                        arrived(pe, "wkr")
                    evacuated(pe, ("E", 4 * i + 3))
                    for k in range(KD):
                        for r in range(2):
                            for t in range(2):
                                hh = 4 * i + 2 * r + t
                                at = k * 256 + t * P + r * 64
                                last = mm(ps[:, bk, at:at + 64], ET[:, hh % 8, k * P:(k + 1) * P], wkr_sb[:, hh, :],
                                          start=True, stop=True)
                elif kind == "W":
                    if i == 0:
                        arrived(pe, "wkckv")
                    arrived(pe, f"wo{i}")
                    for t in range(2):
                        for r in range(2):
                            hh = 4 * i + 2 * r + t
                            last = mm(ps[64 * r:64 * r + 64, bk, t * D:(t + 1) * D], wkckv_sb[:, hh, :], wo_sb[:, hh, :],
                                      start=True, stop=True)
                elif kind == "K":
                    if i == 0:
                        pe.wait_ge(s_rope, 1)
                    last = key_transposes(bk, 0, i)
                last.then_inc(s_bank, 1)

            pe.wait_ge(s_evac["act"], count["act"])
            pe.wait_ge(s_evac["dve"], count["dve"])

            def scores(g, kt, between):
                n, b, m = KT * g + kt, g // UNITS, P if kt < KT - 1 else LAST
                if kt == 0:
                    pe.wait_ge(s_qhi, g + 1)
                    pe.wait_ge(s_qlo, g + 1)
                for half in range(2):
                    cols = slice(half * 512, half * 512 + 512)
                    if n:
                        pe.wait_ge(s_exp, 2 * n - 1 + half)
                    mm(ps[0:m, half, :], kcat[:, b % 2, kt * P:kt * P + m], Q1[:, g % 2, cols], start=True, stop=False)
                    if kt == 0 and half == 0:
                        pe.wait_ge(s_mq, 32 * (g + 1))
                    mm(ps[0:m, half, :], khs[:, b % 2, kt * P:kt * P + m], Q2[:, g % 2, cols],
                       start=False, stop=True).then_inc(s_sc, 1)
                    between(half)

            def context(n, between=lambda slot: None):
                g, kt = n // KT, n % KT
                m = P if kt < KT - 1 else LAST
                if kt == 0 and g:
                    pe.wait_ge(s_ctx, g)
                for r in range(2):
                    pe.wait_ge(s_exp, 2 * n + r + 1)
                    last = mm(ps[64 * r:64 * r + 64, 2, :], kvn[0:m, (g // UNITS) % 2, kt, :],
                              probs[0:m, n % 4, r * 512:r * 512 + 512], start=kt == 0, stop=kt == KT - 1)
                    if r == 0:
                        between(2)
                last.then_inc(s_pv, 1)
                between(3)

            def project_queries(g):
                b, u = g // UNITS, g % UNITS
                if g >= 1:
                    pe.wait_ge(s_mrd, NCHUNK * g)
                if g == 0:
                    evacuated(pe, ("LT2", 3))
                if g == 1:
                    pe.wait_ge(s_qhi, 1)
                    pe.wait_ge(s_qlo, 1)
                for t in range(2):
                    for k in range(KD):
                        last = mm(ps[:, 4, t * S:(t + 1) * S], A_sb[:, k, u * 256 + t * P:u * 256 + (t + 1) * P],
                                  hT[:, k, b * S:(b + 1) * S], start=k == 0, stop=k == KD - 1)
                last.then_inc(s_qp, 1)

            def max_chunk(g, i):
                c = NCHUNK * g + i
                if i == 0:
                    pe.wait_ge(s_qhi, g + 1)
                    pe.wait_ge(s_qlo, g + 1)
                if i >= 2 or g:
                    pe.wait_ge(s_mrd, c - 1)
                t, half = divmod(i, 2)
                for q in range(2):
                    at = (2 * half + q) * CW
                    last = mm(ps[:, 4 + 2 * (c % 2) + q, 0:CW], Q1[:, g % 2, t * P:(t + 1) * P],
                              kcat[:, (g // UNITS) % 2, at:at + CW], start=True, stop=True)
                last.then_inc(s_mch, 1)

            def transpose_max(g):
                pe.wait_ge(s_mx, g + 1)
                nc.tensor.transpose(ps[0:QT, 3, 0:P], mx[:, :], ident[:, :]).then_inc(s_mt, 1)

            def add_up(g):
                pe.wait_ge(s_acc, g + 1)
                if g + 1 < G:
                    pe.wait_ge(s_mrow, g + 2)
                for r in range(2):
                    last = mm(ps[64 * r:64 * r + 64, 3, :], ones64[:, :], accD[:, g % 2, r * 512:r * 512 + 512],
                              start=True, stop=True)
                last.then_inc(s_sum, 1)

            project_queries(0)
            for i in range(NCHUNK):
                max_chunk(0, i)
            transpose_max(0)
            project_queries(1)
            for g in range(G):
                for kt in range(KT):
                    def between(slot, g=g, kt=kt):
                        if g + 1 < G and slot in SLOTS[CHUNKS[kt]]:
                            max_chunk(g + 1, chunks_beside(kt)[SLOTS[CHUNKS[kt]].index(slot)])

                    scores(g, kt, between)
                    if kt == KT - 1 and g + 2 < G:
                        project_queries(g + 2)
                    if KT * g + kt > 0:
                        context(KT * g + kt - 1, between)
                    if kt == 2 and g:
                        add_up(g - 1)
                    if g % UNITS == 2 and g // UNITS + 1 < B and kt in KPREP_AT:
                        i = KPREP_AT[kt]
                        nb = g // UNITS + 1
                        if i == 0:
                            pe.wait_ge(s_rope, nb + 1)
                            pe.wait_ge(s_rec, g)
                        else:
                            pe.wait_ge(s_klo, 4 * (nb - 1) + i)
                        key_transposes(3, nb, i).then_inc(s_ktr, 1)
                    if g + 1 < G and kt == 11:
                        if g:
                            pe.wait_ge(s_rec, g)
                        if g % UNITS == 2 and g // UNITS + 1 < B:
                            pe.wait_ge(s_klo, 4 * (g // UNITS + 1))
                        transpose_max(g + 1)
            context(KT * G - 1)
            add_up(G - 1)

            for i in range(4):
                pe.wait_ge(s_norm, UNITS * (i + 1))
                if i == 0:
                    pe.wait_ge(s_exp, 2 * KT * G)
                    pe.wait_ge(s_ctx, G)
                    pe.wait_ge(s_rec, G)
                for t2 in range(2):
                    for p8 in range(8):
                        u, t = divmod(p8, 2)
                        last = mm(ps[:, i, t2 * D:(t2 + 1) * D], ctxn[:, UNITS * i + u, t * S + t2 * P:t * S + (t2 + 1) * P],
                                  Bo_sb[:, p8, :], start=p8 == 0, stop=p8 == 7)
                last.then_inc(s_o2, 1)
            for i in range(4):
                k, half = i % 2, i // 2
                pe.wait_ge(s_xn, 5 + half)
                for t in range(4):
                    last = nc.tensor.transpose(ps[:, 4 + i, t * P:(t + 1) * P], xn[:, t, k * P:(k + 1) * P], ident[:, :])
                last.then_inc(s_l3, 1)
            pe.wait_ge(s_xhi, 4)
            pe.wait_ge(s_xlo, 4)
            pe.wait_ge(s_gs, 2)
            pe.wait_ge(s_x2, 4)
            for t in range(TT):
                terms = [(a, w, k) for k in range(KD) for a, w in ((xhi, ghi), (xlo, ghi), (xhi, glo))]
                for n, (a, w, k) in enumerate(terms):
                    last = mm(ps[:, 7, t * E:(t + 1) * E], a[:, k, t * P:(t + 1) * P], w[:, k * E:(k + 1) * E],
                              start=n == 0, stop=n == len(terms) - 1)
            last.then_inc(s_lg, 1)

            def up(n):
                c, half = n // 2, n % 2
                tok = slice(half * 512, half * 512 + 512)
                if half == 0:
                    pe.wait_ge(s_whi, c + 1)
                    pe.wait_ge(s_wlo, c + 1)
                if n:
                    pe.wait_ge(s_silu, n)
                for gu in range(2):
                    if gu and n:
                        pe.wait_ge(s_hu, n)
                    terms = [(w, a, k) for k in range(KD) for w, a in ((whi, xhi), (whi, xlo), (wlo, xhi))]
                    for m, (w, a, k) in enumerate(terms):
                        at = (k * 2 + gu) * P
                        last = mm(ps[:, 4 + gu, :], w[:, c % 2, at:at + P], a[:, k, tok], start=m == 0, stop=m == len(terms) - 1)
                    if gu == 0:
                        last.then_inc(s_g, 1)
                if n == 0:
                    pe.wait_ge(s_cthi, 1)
                    pe.wait_ge(s_ctlo, 1)
                if n:
                    pe.wait_ge(s_hc, n)
                mm(ps[:, 6, :], whi[0:64, c % 2, FW - P:FW], cT[:, tok], start=True, stop=True).then_inc(s_u, 1)

            def down(n):
                c, half = n // 2, n % 2
                pe.wait_ge(s_hhi, n + 1)
                pe.wait_ge(s_hlo, n + 1)
                at = 2 * KD * P
                for t in range(4):
                    tile = 4 * half + t
                    o = ps[:, tile // 2, (tile % 2) * D:(tile % 2 + 1) * D]
                    for m, (a, w) in enumerate(((hhi, whi), (hhi, wlo), (hlo, whi))):
                        last = mm(o, a[:, n % 2, t * P:(t + 1) * P], w[:, c % 2, at:at + D],
                                  start=c == 0 and m == 0 and tile % 2 == 0, stop=c == NF - 1 and m == 2, skip_group_check=True)
                last.then_inc(s_dn, 1)

            def transpose_combine():
                pe.wait_ge(s_comb, 1)
                for t in range(TT):
                    last = nc.tensor.transpose(ps[0:E + 1, 6 + t // 4, (t % 4) * P:(t % 4 + 1) * P], comb[:, t, :], ident[:, :])
                last.then_inc(s_ct, 1)

            transpose_combine()
            for n in range(NH):
                up(n)
                if n:
                    down(n - 1)
            down(NH - 1)

        @block.scalar
        def _(act):
            acts = nc.scalar.activation
            chain = [0]
            nc.scalar.preload_act_table_set("natural_log_exp_and_others")

            def link(ins):
                chain[0] += 1
                ins.then_inc(s_alink, 1)
                act.wait_ge(s_alink, chain[0])

            def ln_estimate(n):
                act.wait_ge(s_ln_var, n + 1)
                link(acts(lnw[:, 1, :], lnw[:, 0, :], ACT.Ln))
                acts(lnw[:, 2, :], lnw[:, 1, :], ACT.Exp, scale=-0.5).then_inc(s_ln_est, 1)

            for kind, i in jobs:
                j = (kind, i)
                if kind in ("LN1", "LN2"):
                    ln_estimate(i + (2 if kind == "LN2" else 0))
                    continue
                if kind == "K":
                    act.wait_ge(s_bank, filled[j])
                    w = len(kgroup(i)) * P
                    if i == 0:
                        act.wait_ge(s_const, 1)
                    at = slice(4 * P * i, 4 * P * i + w)
                    acts(kcat[0:64, 0, at], ps[0:64, bank_of[j], 0:w], ACT.Copy).then_inc(s_khi, 1)
                    acts(khs[0:64, 0, at], ps[0:64, bank_of[j], 0:w], ACT.Copy).then_inc(s_khi, 1)
                    continue
                if evac_by[kind] != "act":
                    continue
                act.wait_ge(s_bank, filled[j])
                bk = ps[:, bank_of[j], :]
                if kind in ("LT1", "LT2"):
                    k, half = i % 2, i // 2
                    last = acts(hT[:, k, half * 512:half * 512 + 512], bk, ACT.Copy)
                elif kind == "QK":
                    m, half = i % 4, i // 4
                    if i == 0:
                        act.wait_ge(loads["bias"], 32)
                    last = acts(qkT[:, m, half * 512:half * 512 + 512], bk, ACT.Identity, bias=bqk_sb[:, m:m + 1])
                elif kind == "S":
                    act.wait_ge(s_smax, i + 1)
                    if i >= 2:
                        act.wait_ge(s_bank, filled[("T", i - 2)])
                    for q in range(2):
                        last = acts(pr[:, i % 2, q, :], bk[:, q * S:(q + 1) * S], ACT.Exp, scale=D ** -0.5,
                                    bias=smx[:, i % 2, 1, q:q + 1], accum_out=smx[:, i % 2, 2, q:q + 1])
                elif kind == "T":
                    if i:
                        act.wait_ge(s_bank, filled[("C", i - 1)])
                    last = acts(prT[:, :, :], bk.rearrange("p (k q) -> p k q", k=2), ACT.Copy)
                elif kind == "D":
                    if i >= 2:
                        act.wait_ge(s_bank, filled[("E", i - 2)])
                    last = acts(DT[:, i % 2, :, :], bk[0:96].rearrange("p (b n) -> p b n", b=2), ACT.Copy)
                elif kind == "W":
                    last = acts(Bo_sb[:, 2 * i:2 * i + 2, :], bk.rearrange("p (t n) -> p t n", t=2), ACT.Copy)
                last.then_inc(s_evac["act"], 1)

            def exponentials(g, kt):
                n, m = KT * g + kt, P if kt < KT - 1 else LAST
                if n >= 4:
                    act.wait_ge(s_pv, n - 3)
                    g4, kt4 = divmod(n - 4, KT)
                    if kt4 % 2 == 0:
                        act.wait_ge(s_addD, 6 * g4 + releasedD(kt4))
                    else:
                        act.wait_ge(s_addP, 5 * g4 + releasedP(kt4))
                for half in range(2):
                    act.wait_ge(s_sc, 2 * n + half + 1)
                    acts(probs[0:m, n % 4, half * 512:half * 512 + 512], ps[0:m, half, :], ACT.Exp).then_inc(s_exp, 1)

            def query_high(g):
                act.wait_ge(s_qp, g + 1)
                if g >= 2:
                    act.wait_ge(s_sc, 2 * KT * (g - 1))
                for r in range(2):
                    for dup in range(2):
                        last = acts(Q1[64 * dup:64 * dup + 64, g % 2, 512 * r:512 * r + 512], ps[64 * r:64 * r + 64, 4, :], ACT.Copy)
                last.then_inc(s_qhi, 1)

            def key_high(b, i):
                act.wait_ge(s_ktr, 4 * (b - 1) + i + 1)
                if i == 0 and b >= 2:
                    act.wait_ge(s_sc, 2 * KT * UNITS * (b - 1))
                w = len(kgroup(i)) * P
                at = slice(4 * P * i, 4 * P * i + w)
                acts(kcat[0:64, b % 2, at], ps[0:64, 3, 0:w], ACT.Copy).then_inc(s_khi, 1)
                acts(khs[0:64, b % 2, at], ps[0:64, 3, 0:w], ACT.Copy).then_inc(s_khi, 1)

            def read_context(g):
                act.wait_ge(s_pv, KT * (g + 1))
                if g:
                    act.wait_ge(s_norm, g)
                acts(nctx, ps[:, 2, :], ACT.Copy, scale=-1.0).then_inc(s_ctx, 1)

            def estimate(g):
                act.wait_ge(s_sum, g + 1)
                if g:
                    act.wait_ge(s_rec, g)
                link(acts(est, ps[:, 3, :], ACT.Ln))
                acts(est, est, ACT.Exp, scale=-1.0).then_inc(s_est, 1)

            query_high(0)
            query_high(1)
            for g in range(G):
                for kt in range(KT):
                    exponentials(g, kt)
                    if kt == 0 and g:
                        read_context(g - 1)
                    if kt == 3 and g:
                        estimate(g - 1)
                    if kt == KT - 1 and g + 2 < G:
                        query_high(g + 2)
                    if g % UNITS == 2 and g // UNITS + 1 < B and kt in KPREP_AT:
                        key_high(g // UNITS + 1, KPREP_AT[kt])
            read_context(G - 1)
            estimate(G - 1)

            for half in range(2):
                ln_estimate(4 + half)
            for i in range(4):
                k, half = i % 2, i // 2
                act.wait_ge(s_l3, i + 1)
                acts(xhi[:, k, half * 512:half * 512 + 512], ps[:, 4 + i, :], ACT.Copy).then_inc(s_xhi, 1)
            act.wait_ge(s_rsub, 1)
            acts(rt[:, 1, :, :], rt[:, 0, :, :], ACT.Exp).then_inc(s_rexp, 1)

            def weights_high(c):
                act.wait_ge(ld_ffw[c % 3], 16 * (c // 3 + 1))
                if c >= 2:
                    act.wait_ge(s_dn, 2 * (c - 1))
                acts(whi[:, c % 2, :], wring[:, c % 3, :], ACT.Copy).then_inc(s_whi, 1)

            weights_high(0)
            weights_high(1)
            act.wait_ge(s_ct, 1)
            act.wait_ge(s_c0, 1)
            acts(cT[0:E + 1, :].rearrange("p (b n) -> p b n", b=2), ps[0:E + 1, 6:8, :], ACT.Copy).then_inc(s_cthi, 1)
            for n in range(NH):
                act.wait_ge(s_g, n + 1)
                if n >= 2:
                    act.wait_ge(s_hu, n - 1)
                acts(silu[:, n % 2, :], ps[:, 4, :], ACT.Silu).then_inc(s_silu, 1)
                act.wait_ge(s_hc, n + 1)
                if n >= 2:
                    act.wait_ge(s_dn, n - 1)
                acts(hhi[:, n % 2, :], hful[:, n % 2, :], ACT.Copy).then_inc(s_hhi, 1)
                if n % 2 == 0 and n and n // 2 + 1 < NF:
                    weights_high(n // 2 + 1)

        @block.gpsimd
        def _(pool):
            chain = [0]

            def link(ins):
                chain[0] += 1
                ins.then_inc(s_plink, 1)
                pool.wait_ge(s_plink, chain[0])

            link(nc.gpsimd.memset(ones64[:, :], 1.0))
            link(nc.gpsimd.memset(Q2[64:128, :, :].bitcast(f32), 0.0))
            link(nc.gpsimd.memset(khs[64:128, :, :].bitcast(f32), 0.0))
            nc.gpsimd.memset(khs[64:66, :, :].bitcast(f32), 1.0).then_inc(s_const, 1)
            pool.wait_ge(s_const, 1)

            def rotate(b):
                if b == 0:
                    arrived(pool, "rope")
                pool.wait_ge(ld_ctx, 16 * (b + 1))
                if b >= 2:
                    pool.wait_ge(s_pv, KT * UNITS * (b - 1))
                    pool.wait_ge(s_klo, 4 * (b - 1))
                hd = DC // 2
                nc.gpsimd.tensor_tensor(kvn[:, b % 2, :, :], kraw[:, :, :], kcos[:, 0], ALU.mult)
                nc.gpsimd.tensor_tensor(kt2[:, :, 0:hd], kraw[:, :, hd:DC], kcos[:, 1, :, 0:hd], ALU.mult)
                ins = nc.gpsimd.tensor_tensor(kt2[:, :, hd:DC], kraw[:, :, 0:hd], kcos[:, 1, :, hd:DC], ALU.mult)
                ins.then_inc(s_kraw, 1)
                pool.wait_ge(s_kraw, b + 1)
                nc.gpsimd.tensor_tensor(kvn[:, b % 2, :, :], kvn[:, b % 2, :, :], kt2[:, :, :], ALU.add).then_inc(s_rope, 1)

            rotate(0)

            def add_odd(g, kt):
                n = KT * g + kt
                pool.wait_ge(s_exp, 2 * n + 2)
                if kt == 3:
                    if g:
                        pool.wait_ge(s_acc, g)
                    nc.gpsimd.tensor_tensor(accP, probs[:, (n - 2) % 4, :], probs[:, n % 4, :], ALU.add).then_inc(s_addP, 1)
                elif kt > 3:
                    pool.wait_ge(s_addP, 5 * g + releasedP(kt) - 1)
                    nc.gpsimd.tensor_tensor(accP, accP, probs[:, n % 4, :], ALU.add).then_inc(s_addP, 1)

            def norm(g):
                pool.wait_ge(s_rec, g + 1)
                pool.wait_ge(s_ctx, g + 1)
                nc.gpsimd.tensor_tensor(ctxn[:, g, :], corr, nctx, ALU.mult).then_inc(s_norm, 1)

            for g in range(G):
                for kt in range(1, KT, 2):
                    add_odd(g, kt)
                    if kt == 5 and g:
                        norm(g - 1)
                if g % UNITS == 0 and g // UNITS + 1 < B:
                    rotate(g // UNITS + 1)
            norm(G - 1)

            for c in range(NF):
                pool.wait_ge(ld_ffw[c % 3], 16 * (c // 3 + 1))
                pool.wait_ge(s_whi, c + 1)
                nc.gpsimd.tensor_tensor(wlo[:, c % 2, 0:FW - P], wring[:, c % 3, 0:FW - P],
                                        whi[:, c % 2, 0:FW - P].bitcast(f32), ALU.subtract).then_inc(s_wlo, 1)

        @block.vector
        def _(dve):
            V = nc.vector
            chain = [0]

            def link(ins):
                chain[0] += 1
                ins.then_inc(s_link, 1)
                dve.wait_ge(s_link, chain[0])

            def layer_norm(n, half):
                for t in range(4):
                    ins = V.bn_stats(stats[:, t, :], x_sb[:, 4 * half + t, :])
                link(ins)
                for t in range(4):
                    ins = V.bn_aggr(mv[:, t, :], stats[:, t, :])
                link(ins)
                V.tensor_scalar(lnw[:, 0, :], mv[:, :, 1], EPS, None, ALU.add).then_inc(s_ln_var, 1)
                dve.wait_ge(s_ln_est, n + 1)
                link(V.tensor_tensor(lnw[:, 3, :], lnw[:, 2, :], lnw[:, 2, :], ALU.mult))
                link(V.tensor_tensor(lnw[:, 3, :], lnw[:, 3, :], lnw[:, 0, :], ALU.mult))
                link(V.tensor_scalar(lnw[:, 3, :], lnw[:, 3, :], -0.5, 1.5, ALU.mult, ALU.add))
                link(V.tensor_tensor(lnw[:, 4, :], lnw[:, 3, :], lnw[:, 2, :], ALU.mult))
                if n in (1, 2, 3):
                    j = {1: ("LT1", 1), 2: ("LT1", 3), 3: ("LT2", 1)}[n]
                    dve.wait_ge(s_bank, filled[j])
                elif n == 4:
                    dve.wait_ge(s_bank, filled[("LT2", 3)])
                elif n == 5:
                    dve.wait_ge(s_l3, 2)
                for t in range(4):
                    ins = V.tensor_scalar(xn[:, t, :], x_sb[:, 4 * half + t, :], mv[:, t, 0:1], lnw[:, 4, t:t + 1],
                                          ALU.subtract, ALU.mult)
                ins.then_inc(s_xn, 1)

            for kind, i in jobs:
                j = (kind, i)
                if kind == "LN1":
                    arrived(dve, f"x{i}")
                    layer_norm(i, i)
                elif kind == "LN2":
                    layer_norm(2 + i, i)
                elif kind == "S":
                    dve.wait_ge(s_bank, filled[j])
                    if i >= 2:
                        dve.wait_ge(s_probs, i - 1)
                    link(V.reduce_max(smx[:, i % 2, 0, :], ps[:, bank_of[j], :].rearrange("p (q k) -> p q k", q=2), AX.X))
                    V.tensor_scalar(smx[:, i % 2, 1, :], smx[:, i % 2, 0, :], -D ** -0.5, None, ALU.mult).then_inc(s_smax, 1)
                elif kind == "T":
                    evacuated(dve, ("S", i))
                    link(V.reciprocal(smx[:, i % 2, 3, :], smx[:, i % 2, 2, :]))
                    for q in range(2):
                        ins = V.tensor_scalar(pr[:, i % 2, q, :], pr[:, i % 2, q, :], smx[:, i % 2, 3, q:q + 1], None, ALU.mult)
                    ins.then_inc(s_probs, 1)
                elif kind == "K":
                    w = len(kgroup(i)) * P
                    at = slice(4 * P * i, 4 * P * i + w)
                    dve.wait_ge(s_khi, 2 * (i + 1))
                    V.tensor_tensor(kcat[64:128, 0, at], ps[0:64, bank_of[j], 0:w], kcat[0:64, 0, at].bitcast(f32),
                                    ALU.subtract).then_inc(s_evac["dve"], 1)
                elif evac_by[kind] == "dve":
                    dve.wait_ge(s_bank, filled[j])
                    bk = ps[:, bank_of[j], :]
                    if kind == "V":
                        if i == 0:
                            dve.wait_ge(loads["bias"], 32)
                        ins = V.tensor_tensor(v_sb[:, 2 * i:2 * i + 2, :], bk.rearrange("p (t n) -> p t n", t=2),
                                              bvo_sb[:, 0:1, :].broadcast_to([P, 2, D]), ALU.add)
                    elif kind == "C":
                        if i >= 2:
                            dve.wait_ge(s_bank, filled[("O", i - 2)])
                        ins = V.tensor_copy(cxT[:, i % 2, :, :], bk.rearrange("p (k n) -> p k n", k=2))
                    elif kind == "O":
                        xt = x_sb[:, 2 * i:2 * i + 2, :]
                        link(V.tensor_tensor(xt, xt, bk.rearrange("p (t n) -> p t n", t=2), ALU.add))
                        ins = V.tensor_tensor(xt, xt, bvo_sb[:, 1:2, :].broadcast_to([P, 2, D]), ALU.add)
                    elif kind == "E":
                        if i >= 8:
                            dve.wait_ge(s_bank, filled[("A", i // 4 - 2)])
                        ins = V.tensor_copy(ET[:, i % 8, :], bk[0:R, 0:D])
                    elif kind == "A":
                        ins = V.tensor_copy(A_sb[:, :, i * 256:(i + 1) * 256], bk.rearrange("p (k n) -> p k n", k=2))
                    ins.then_inc(s_evac["dve"], 1)
                    if kind == "O":
                        evacuated(dve, j)

            def query_low(g):
                dve.wait_ge(s_qhi, g + 1)
                if g == 0:
                    dve.wait_ge(s_const, 1)
                for r in range(2):
                    last = V.tensor_tensor(Q2[0:64, g % 2, 512 * r:512 * r + 512], ps[64 * r:64 * r + 64, 4, :],
                                           Q1[0:64, g % 2, 512 * r:512 * r + 512].bitcast(f32), ALU.subtract)
                last.then_inc(s_qlo, 1)

            def key_low(b, i):
                dve.wait_ge(s_khi, 8 * b + 2 * (i + 1))
                w = len(kgroup(i)) * P
                at = slice(4 * P * i, 4 * P * i + w)
                V.tensor_tensor(kcat[64:128, b % 2, at], ps[0:64, 3, 0:w], kcat[0:64, b % 2, at].bitcast(f32),
                                ALU.subtract).then_inc(s_klo, 1)

            def max_chunk(g, i):
                dve.wait_ge(s_mch, NCHUNK * g + i + 1)
                if i == 0 and g:
                    dve.wait_ge(s_mx, g)
                t, half = divmod(i, 2)
                V.reduce_max(mxp[:, t, half:half + 1], ps[:, 4 + 2 * half:6 + 2 * half, 0:CW], AX.XY).then_inc(s_mrd, 1)

            def reduce_chunks(g):
                dve.wait_ge(s_mrd, NCHUNK * (g + 1))
                if g:
                    dve.wait_ge(s_mt, g)
                V.reduce_max(mx[:, :], mxp[:, :, :], AX.X).then_inc(s_mx, 1)

            def max_rows(g):
                dve.wait_ge(s_mt, g + 1)
                if g >= 2:
                    dve.wait_ge(s_mq, 32 * (g - 1))
                link(V.tensor_scalar(mrow[:, g % 2, 0, :], ps[0:QT, 3, 0:P], -1.0, None, ALU.mult))
                V.scalar_tensor_tensor(out=mrow[:, g % 2, 1, :], in0=ps[0:QT, 3, 0:P], scalar=-1.0,
                                       in1=mrow[:, g % 2, 0, :].bitcast(f32), op0=ALU.mult, op1=ALU.subtract).then_inc(s_mrow, 1)

            def add_even(g, kt):
                n, m = KT * g + kt, P if kt < KT - 1 else LAST
                if kt == 0:
                    return
                dve.wait_ge(s_exp, 2 * n + 2)
                a = accD[:, g % 2, :]
                if kt == 2:
                    if g >= 2:
                        dve.wait_ge(s_sum, g - 1)
                    V.tensor_tensor(a, probs[:, (n - 2) % 4, :], probs[:, n % 4, :], ALU.add).then_inc(s_addD, 1)
                else:
                    dve.wait_ge(s_addD, 6 * g + releasedD(kt) - 1)
                    V.tensor_tensor(a[0:m], a[0:m], probs[0:m, n % 4, :], ALU.add).then_inc(s_addD, 1)

            def combine(g):
                dve.wait_ge(s_addD, 6 * (g + 1))
                dve.wait_ge(s_addP, 5 * (g + 1))
                a = accD[:, g % 2, :]
                V.tensor_tensor(a, a, accP, ALU.add).then_inc(s_acc, 1)

            def reciprocal_sum(g):
                dve.wait_ge(s_est, g + 1)
                if g:
                    dve.wait_ge(s_norm, g)
                link(V.tensor_tensor(corr, est, ps[:, 3, :], ALU.mult))
                V.scalar_tensor_tensor(out=corr, in0=corr, scalar=-2.0, in1=est, op0=ALU.add, op1=ALU.mult).then_inc(s_rec, 1)

            query_low(0)
            for i in range(NCHUNK):
                max_chunk(0, i)
            reduce_chunks(0)
            max_rows(0)
            query_low(1)
            for g in range(G):
                for kt in range(KT):
                    if kt == 1 and g:
                        combine(g - 1)
                    if kt == 4 and g:
                        reciprocal_sum(g - 1)
                    todo = list(chunks_beside(kt)) if g + 1 < G else []
                    for i in todo[:1]:
                        max_chunk(g + 1, i)
                    if kt % 2 == 0:
                        add_even(g, kt)
                    for i in todo[1:]:
                        max_chunk(g + 1, i)
                    if kt == 10 and g + 1 < G:
                        reduce_chunks(g + 1)
                    if kt == 11 and g + 1 < G:
                        max_rows(g + 1)
                    if kt == KT - 1 and g + 2 < G:
                        query_low(g + 2)
                    if g % UNITS == 2 and g // UNITS + 1 < B and kt in KPREP_AT:
                        key_low(g // UNITS + 1, KPREP_AT[kt])
            combine(G - 1)
            reciprocal_sum(G - 1)

            arrived(dve, "gate")
            dve.wait_ge(s_sc, 2 * KT * G)
            V.tensor_copy(ghi, gate_sb[:, :]).then_inc(s_gs, 1)
            dve.wait_ge(s_gs, 1)
            V.tensor_tensor(glo, gate_sb[:, :], ghi.bitcast(f32), ALU.subtract).then_inc(s_gs, 1)
            V.memset(cT.bitcast(f32), 0.0).then_inc(s_c0, 1)
            for half in range(2):
                for i in (2 * half, 2 * half + 1):
                    dve.wait_ge(s_o2, i + 1)
                    xt = x_sb[:, 2 * i:2 * i + 2, :]
                    V.tensor_tensor(xt, xt, ps[:, i, :].rearrange("p (t n) -> p t n", t=2), ALU.add).then_inc(s_x2, 1)
                    dve.wait_ge(s_x2, i + 1)
                layer_norm(4 + half, half)
            for i in range(4):
                k, half = i % 2, i // 2
                at = slice(half * 512, half * 512 + 512)
                dve.wait_ge(s_xhi, i + 1)
                V.tensor_tensor(xlo[:, k, at], ps[:, 4 + i, :], xhi[:, k, at].bitcast(f32), ALU.subtract).then_inc(s_xlo, 1)

            def wide(a):
                return a.rearrange("p (t o) -> p t o", o=1).broadcast_to([P, TT, E])

            dve.wait_ge(s_lg, 1)
            lg = ps[:, 7, 0:TT * E].rearrange("p (t e) -> p t e", t=TT)
            link(V.reduce_max(rs[:, 0, :], lg, AX.X))
            V.tensor_tensor(rt[:, 0], lg, wide(rs[:, 0, :]), ALU.subtract).then_inc(s_rsub, 1)
            dve.wait_ge(s_rexp, 1)
            link(V.reduce_sum(rs[:, 1, :], rt[:, 1], AX.X))
            link(V.reciprocal(rs[:, 2, :], rs[:, 1, :]))
            link(V.tensor_tensor(rt[:, 1], rt[:, 1], wide(rs[:, 2, :]), ALU.mult))
            link(V.memset(rt[:, 5], 0.0))
            arrived2 = loads["consts"]
            dve.wait_ge(arrived2, 32)
            cur = rt[:, 1]
            for _ in range(2):
                link(V.reduce_max(rs[:, 3, :], cur, AX.X))
                link(V.tensor_tensor(rt[:, 3], cur, wide(rs[:, 3, :]), ALU.is_equal))
                link(V.tensor_tensor(rt[:, 3], rt[:, 3], rank[:, :, :], ALU.mult))
                link(V.reduce_max(rs[:, 4, :], rt[:, 3], AX.X))
                link(V.tensor_tensor(rt[:, 4], rt[:, 3], wide(rs[:, 4, :]), ALU.is_equal))
                link(V.tensor_tensor(rt[:, 5], rt[:, 5], rt[:, 4], ALU.add))
                link(V.scalar_tensor_tensor(out=rt[:, 2], in0=rt[:, 4], scalar=-4.0, in1=rt[:, 1], op0=ALU.mult, op1=ALU.add))
                cur = rt[:, 2]
            link(V.memset(comb[:, :, E:E + 1], 1.0))
            V.tensor_tensor(comb[:, :, 0:E], rt[:, 1], rt[:, 5], ALU.mult).then_inc(s_comb, 1)
            dve.wait_ge(s_cthi, 1)
            V.tensor_tensor(cT[CROW:CROW + E + 1, :].rearrange("p (b n) -> p b n", b=2), ps[0:E + 1, 6:8, :],
                            cT[0:E + 1, :].bitcast(f32).rearrange("p (b n) -> p b n", b=2), ALU.subtract).then_inc(s_ctlo, 1)

            for n in range(NH):
                dve.wait_ge(s_u, n + 1)
                dve.wait_ge(s_silu, n + 1)
                if n >= 2:
                    dve.wait_ge(s_hc, n - 1)
                V.tensor_tensor(hsu[:, n % 2, :], silu[:, n % 2, :], ps[:, 5, :], ALU.mult).then_inc(s_hu, 1)
                dve.wait_ge(s_hu, n + 1)
                if n >= 2:
                    dve.wait_ge(s_hhi, n - 1)
                    dve.wait_ge(s_hlo, n - 1)
                V.tensor_tensor(hful[:, n % 2, :], hsu[:, n % 2, :], ps[:, 6, :], ALU.mult).then_inc(s_hc, 1)
                dve.wait_ge(s_hhi, n + 1)
                if n >= 2:
                    dve.wait_ge(s_dn, n - 1)
                V.tensor_tensor(hlo[:, n % 2, :], hful[:, n % 2, :], hhi[:, n % 2, :].bitcast(f32), ALU.subtract).then_inc(s_hlo, 1)
            dve.wait_ge(s_dn, NH)
            for i in range(4):
                xt = x_sb[:, 2 * i:2 * i + 2, :]
                V.tensor_tensor(xt, xt, ps[:, i, :].rearrange("p (t n) -> p t n", t=2), ALU.add).then_inc(s_fin, 1)


def _tables():
    f = np.float32
    inv = (f(1.0) / f(10000.0) ** (np.arange(0, DC, 2, dtype=f) / f(DC))).astype(f)
    ang = np.arange(L, dtype=f)[:, None] * inv[None, :]
    sin = np.repeat(np.sin(ang), 2, axis=-1)
    cos = np.repeat(np.cos(ang), 2, axis=-1)
    sin[:, :DC // 2] = -sin[:, :DC // 2]
    sel = np.zeros((NF, P, P), f)
    for c in range(NF):
        for p in range(P):
            i = c * P + p
            e = min(i // I, E)
            sel[c, e, p] = 1.0
            sel[c, CROW + e, p] = 1.0
    rank = np.tile((E - np.arange(E)).astype(f), (P, TT))
    consts = np.concatenate([np.eye(P, dtype=f), rank], axis=1)
    return cos, sin, sel, consts


def _by_key(a):
    idx = np.minimum(np.arange(KT * P), L - 1)
    a = a[..., idx, :]
    a = a.reshape(*a.shape[:-2], KT, P, DC)
    return np.ascontiguousarray(np.swapaxes(a, -3, -2))


def _rows(a, n):
    return np.ascontiguousarray(a.reshape(n, P, -1).transpose(1, 0, 2))


def kernel(x, ctx_512, L0_attn_w_qkv, L0_attn_b_qkv, L0_attn_w_out, L0_attn_b_out, L0_xattn_Wq, L0_xattn_w_kc_q,
           L0_xattn_w_kc_kv, L0_xattn_W_qr, L0_xattn_W_kr, L0_xattn_Wo, L0_ffn_gate_w, L0_ffn_w_gate_up,
           L0_ffn_w_down, L0_ffn_shared_gate_up, L0_ffn_shared_down):
    import concourse.bacc as bacc
    from concourse.bass_utils import run_bass_kernel_spmd

    A = np.asarray
    cos, sin, sel, consts = _tables()
    gu = A(L0_ffn_w_gate_up)
    pad = NF * P - E * I - SHARED
    sgu, sdn = A(L0_ffn_shared_gate_up), A(L0_ffn_shared_down)

    def hidden(first, shared):
        a = np.concatenate([first.transpose(1, 0, 2).reshape(D, E * I), shared, np.zeros((D, pad), shared.dtype)], axis=1)
        return a.reshape(KD, P, NF, P).transpose(2, 1, 0, 3)

    gates = hidden(gu[:, :, :I], sgu[:, :SHARED])
    ups = hidden(gu[:, :, I:], sgu[:, SHARED:])
    gup = np.stack([gates, ups], axis=3).reshape(NF, P, 2 * KD * P)
    down = np.concatenate([A(L0_ffn_w_down).reshape(E * I, D), sdn, np.zeros((pad, D), sdn.dtype)]).reshape(NF, P, D)
    arrays = {
        "x": A(x).reshape(TT, P, D).transpose(1, 0, 2),
        "ctxk": _by_key(A(ctx_512)),
        "rope": np.stack([_by_key(cos), _by_key(sin)], axis=1),
        "wqkv": _rows(A(L0_attn_w_qkv).T, KD),
        "bqk": A(L0_attn_b_qkv)[:2 * D].reshape(4, P).T,
        "bvo": np.broadcast_to(np.stack([A(L0_attn_b_qkv)[2 * D:], A(L0_attn_b_out)])[None], (P, 2, D)),
        "wout": _rows(A(L0_attn_w_out).T, KD),
        "wq": A(L0_xattn_Wq).reshape(H, HK, D).transpose(1, 0, 2),
        "wkcq": A(L0_xattn_w_kc_q).transpose(1, 0, 2),
        "wqr": A(L0_xattn_W_qr).reshape(H, 2, 96, R).transpose(2, 0, 1, 3),
        "wkr": A(L0_xattn_W_kr).transpose(2, 0, 1),
        "wkckv": A(L0_xattn_w_kc_kv).transpose(1, 0, 2),
        "wo": A(L0_xattn_Wo).reshape(D, H, HK).transpose(2, 1, 0),
        "gate": A(L0_ffn_gate_w).T.reshape(KD, P, E).transpose(1, 0, 2).reshape(P, KD * E),
        "ffw": np.concatenate([gup, down, sel], axis=2),
        "consts": consts,
    }
    nc = bacc.Bacc("TRN2", target_bir_lowering=False, num_devices=1)
    feeds, args = {}, []
    for name, a in arrays.items():
        a = np.ascontiguousarray(a)
        feeds["in_" + name] = a
        args.append(nc.dram_tensor("in_" + name, a.shape, mybir.dt.from_np(a.dtype), kind="ExternalInput").ap())
    out = nc.dram_tensor("out_0", (P, TT, D), mybir.dt.float32, kind="ExternalOutput").ap()
    build(nc, *args, out)
    r = run_bass_kernel_spmd(nc, [feeds], core_ids=[0])
    return r.results[0]["out_0"].transpose(1, 0, 2).reshape(B, S, D)
```

```python
from contextlib import ExitStack

import numpy as np

import concourse.bass as bass
from concourse import mybir
from concourse.alu_op_type import AluOpType as ALU

B, S, D = 4, 256, 256
L, DC = 1601, 64
H, HK, DQ, R = 16, 128, 192, 64
E, I = 16, 176
P = 128
T = B * S
TT = T // P
KD = D // P
KT = -(-L // P)
LAST = L - (KT - 1) * P
UNITS = 4
G = B * UNITS
C = 4 * S
QT = C // P
CW = 402
NCHUNK = QT * 2
SHARED = 2 * I
NE = E * I // P
assert NE * P == E * I and NE % 2 == 0
NF = -(-(E * I + SHARED) // P)
FW = 2 * KD * P + D + P
EPS = 1e-5
CROW = 32
CROWS = CROW + E


def build(nc, x, ctxk, rope, wqkv, bqk, bvo, wout, wq, wkcq, wqr, wkr, wkckv, wo, gate, ffw, consts, out):
    f32, f32r = mybir.dt.float32, mybir.dt.float32r
    ACT, AX = mybir.ActivationFunctionType, mybir.AxisListType
    es = ExitStack()
    with es:
        def sb(name, shape, dt=f32):
            return es.enter_context(nc.sbuf_tensor(name, shape, dt))

        def sem(name):
            return es.enter_context(nc.semaphore(name))

        x_sb = sb("x_sb", [P, TT, D])
        hT = sb("hT", [P, KD, T])
        A_sb = sb("A_sb", [P, KD, UNITS * 256])
        Bo_sb = sb("Bo_sb", [P, 8, D])
        ident = sb("ident", [P, P])
        rank = sb("rank", [P, TT, E])
        ones64 = sb("ones64", [P, 64])
        bqk_sb = sb("bqk_sb", [P, 4])
        bvo_sb = sb("bvo_sb", [P, 2, D])
        gate_sb = sb("gate_sb", [P, KD * E])
        xn = sb("xn", [P, 2, 4, D])
        stats = sb("stats", [P, 4, 6])
        mv = sb("mv", [P, 4, 2])
        lnw = sb("lnw", [P, 5, 4])
        smx = sb("smx", [P, 2, 4, 2])
        big = sb("big", [P, 25088])

        def part(lo, hi, rows=P, **dims):
            a = big[0:rows, lo:hi]
            return a.rearrange("p (a n) -> p a n", **dims) if dims else a

        wq_sb = part(0, 4096, a=H)
        wkcq_sb = part(4096, 7168, a=H)
        qkT = part(7168, 11264, a=4)
        wo_sb = part(7168, 11264, a=H)
        wqkv_sb = part(11264, 12800, a=KD)
        wout_sb = part(12800, 13312, a=KD)
        v_sb = part(13312, 15360, a=TT)
        pr = big[:, 15360:16384].rearrange("p (s q k) -> p s q k", s=2, q=2)
        prT = part(16384, 16896, a=2)
        cxT = big[:, 16896:17920].rearrange("p (s k n) -> p s k n", s=2, k=KD)
        wkr_sb = part(17920, 18432, a=H // 2)
        wkckv_sb = part(18944, 19968, HK, a=H)
        wqr_sb = big[0:96, 19968:22016].rearrange("p (h b r) -> p h b r", h=H, b=2)
        DT = big[0:96, 22016:24064].rearrange("p (s b n) -> p s b n", s=4, b=2)
        ET = part(24064, 25088, a=4)
        ctxn = part(0, 8192, a=G)
        probs = part(8192, 12288, a=4)
        accD = part(12288, 14336, a=2)
        accP = big[:, 14336:15360]
        nctx = big[:, 15360:15872]
        est = big[:, 15872:16384]
        corr = big[:, 16384:16896]
        kraw = sb("kraw", [P, KT, DC])
        kcos = sb("kcos", [P, 2, KT, DC])
        kt2 = sb("kt2", [P, KT, DC])
        kvn = sb("kvn", [P, 2, KT, DC])
        mxp = sb("mxp", [P, QT, 2])
        mx = sb("mx", [P, QT])
        mrow = sb("mrow", [QT, 2, 2, P], f32r)
        arr = sb("arr", [P, 11264], f32r)
        Q1 = arr[:, 0:2048].rearrange("p (s n) -> p s n", s=2)
        Q2 = arr[:, 2048:4096].rearrange("p (s n) -> p s n", s=2)
        kcat = arr[:, 4096:7424].rearrange("p (s n) -> p s n", s=2)
        khs = arr[:, 7424:10752].rearrange("p (s n) -> p s n", s=2)
        xhi = arr[:, 0:2048].rearrange("p (k n) -> p k n", k=KD)
        xlo = arr[:, 2048:4096].rearrange("p (k n) -> p k n", k=KD)
        whi = arr[:, 4096:4096 + 2 * FW].rearrange("p (s n) -> p s n", s=2)
        wlo = arr[:, 4096 + 2 * FW:4096 + 4 * FW].rearrange("p (s n) -> p s n", s=2)
        hhi = arr[:, 7680:8704].rearrange("p (s n) -> p s n", s=2)
        hlo = arr[:, 8704:9728].rearrange("p (s n) -> p s n", s=2)
        cT = arr[0:CROWS, 9728:10752]
        comb = arr[:, 10816:10816 + TT * CROWS].rearrange("p (t e) -> p t e", t=TT)
        ghi = arr[:, 10752:10784]
        glo = arr[:, 10784:10816]
        wring = part(8192, 8192 + 2 * FW, a=2)
        silu = big[:, 12288:13312].rearrange("p (s n) -> p s n", s=2)
        hsu = part(19000, 21048, a=4)
        hful = big[:, 14336:15360].rearrange("p (s n) -> p s n", s=2)
        rt = big[:, 17000:17000 + 6 * TT * E].rearrange("p (a t e) -> p a t e", a=6, t=TT)
        rs = sb("rs", [P, 6, TT])
        cmb = part(18000, 18000 + TT * E, a=TT)
        lgT = part(21100, 21100 + T, E)

        ps = es.enter_context(nc.psum_tensor("ps", [P, 8, 512], f32))

        loads = {}

        def arrived(eng, name):
            eng.wait_ge(loads[name], 16)

        names = ["x0", "x1", "consts", "wqkv", "bias", "wout", "wkr", "wkckv", "wqr", "gate", "rope"]
        names += [f"wkcq{i}" for i in range(4)] + [f"wq{i}" for i in range(4)] + [f"wo{i}" for i in range(4)]
        for n in names:
            loads[n] = sem("ld_" + n)
        ld_ctx = sem("ld_ctx")
        ld_ffw = [sem(f"ld_ffw{i}") for i in range(2)]

        early = """LN1.0 LE1.0 D.0 LT1.0 LT1.1 D.1 LN1.1 D.2 LE1.1 D.3 QK.0 QK.1 QK.2 QK.3 LT1.2 V.0 LT1.3 S.0 V.1 S.1
                   QK.4 QK.5 T.0 QK.6 T.1 C.0 QK.7 C.1 V.2 O.0 S.2 O.1 S.3 V.3 T.2 E.0 T.3 C.2 E.1 D.4 C.3 D.5 O.2
                   D.6 O.3 LN2.0 E.2 D.7 E.3 LE2.0 K.0 K.1 K.2 K.3 A.0 A.1"""
        late = """LT2.0 LT2.1 D.8 QP.0 A.2 D.9 M.0 A.3 M.1 E.4 M.2 D.10 M.3 D.11 M.4 E.5 M.5 D.12 M.6 LN2.1 A.4 A.5
                  LE2.1 D.13 E.6 M.7 D.14 M.8 LT2.2 M.9 LT2.3 D.15 M.10 E.7 M.11 A.6 M.12 M.13 A.7 M.14 W.0 M.15 MX.0
                  W.1 W.2 MT.0 MR.0 QP.1 W.3"""
        early, late = ([(a, int(b)) for a, b in (w.split(".") for w in text.split())] for text in (early, late))
        jobs = early + late
        OTHER = ("LN1", "LN2", "LE1", "LE2", "QP", "M", "MX", "MT", "MR")
        evac_by = {"LT1": "act", "QK": "act", "V": "dve", "S": "act", "T": "act", "C": "dve", "O": "dve", "D": "act",
                   "E": "act", "A": "act", "W": "act", "LT2": "act", "K": "dve"}
        bank_jobs = [j for j in jobs if j[0] not in OTHER]
        bank_of, filled, done, before, user = {}, {}, {}, {}, {}
        count = {"act": 0, "dve": 0}
        for i, j in enumerate(bank_jobs):
            bank_of[j] = i % 8 if j in early else i % 3
            filled[j], before[j] = i + 1, user.get(bank_of[j])
            user[bank_of[j]] = j
            if j in early:
                early_user = dict(user)
            count[evac_by[j[0]]] += 1
            done[j] = count[evac_by[j[0]]]
        s_bank = sem("s_bank")
        s_evac = {"act": sem("s_evac_act"), "dve": sem("s_evac_dve")}

        def evacuated(eng, j):
            eng.wait_ge(s_evac[evac_by[j[0]]], done[j])

        s_link = sem("s_link")
        s_alink = sem("s_alink")
        s_ln_var = sem("s_ln_var")
        s_ln_est = sem("s_ln_est")
        s_xn = sem("s_xn")
        s_smax = sem("s_smax")
        s_probs = sem("s_probs")
        s_const = sem("s_const")
        s_rope = sem("s_rope")
        s_kraw = sem("s_kraw")
        s_plink = sem("s_plink")
        s_ktr = sem("s_ktr")
        s_khi = sem("s_khi")
        s_klo = sem("s_klo")
        s_qp = sem("s_qp")
        s_qhi = sem("s_qhi")
        s_qlo = sem("s_qlo")
        s_mch = sem("s_mch")
        s_mrd = sem("s_mrd")
        s_mx = sem("s_mx")
        s_mt = sem("s_mt")
        s_mrow = sem("s_mrow")
        s_mq = sem("s_mq")
        s_sc = sem("s_sc")
        s_exp = sem("s_exp")
        s_pv = sem("s_pv")
        s_addD = sem("s_addD")
        s_addP = sem("s_addP")
        s_acc = sem("s_acc")
        s_ctx = sem("s_ctx")
        s_sum = sem("s_sum")
        s_est = sem("s_est")
        s_rec = sem("s_rec")
        s_norm = sem("s_norm")
        s_o2 = sem("s_o2")
        s_x2 = sem("s_x2")
        s_l3 = sem("s_l3")
        s_xhi = sem("s_xhi")
        s_xlo = sem("s_xlo")
        s_gs = sem("s_gs")
        s_lg = sem("s_lg")
        s_lgs = sem("s_lgs")
        s_lgt = sem("s_lgt")
        s_rsub = sem("s_rsub")
        s_rexp = sem("s_rexp")
        s_comb = sem("s_comb")
        s_ct = sem("s_ct")
        s_ctc = sem("s_ctc")
        s_whi = sem("s_whi")
        s_wlo = sem("s_wlo")
        s_g = sem("s_g")
        s_u = sem("s_u")
        s_c = sem("s_c")
        s_silu = sem("s_silu")
        s_hu = sem("s_hu")
        s_hc = sem("s_hc")
        s_hhi = sem("s_hhi")
        s_hlo = sem("s_hlo")
        s_dn = sem("s_dn")
        s_fin = sem("s_fin")
        s_out = sem("s_out")

        NH = 2 * NF
        FIRST = range(4)
        PAIRS = NE // 2 - 1
        TAIL = [(2 * c + h, c, h) for c in range(NE, NF) for h in range(2)]
        CHUNKS = (0, 2, 2, 1, 2, 1, 2, 1, 2, 1, 2, 0, 0)
        SLOTS = {0: (), 1: (1,), 2: (0, 2)}
        KPREP_AT = {(1, 7): 0, (1, 9): 1, (2, 7): 2, (2, 9): 3}
        assert sum(CHUNKS) == NCHUNK

        def chunks_beside(kt):
            return range(sum(CHUNKS[:kt]), sum(CHUNKS[:kt + 1]))

        def prepares_keys(g, kt):
            return g // UNITS + 1 < B and (g % UNITS, kt) in KPREP_AT

        def kgroup(i):
            return range(4 * i, min(4 * i + 4, KT))

        def releasedD(kt):
            return max(1, kt // 2)

        def releasedP(kt):
            return max(1, (kt - 1) // 2)

        block = es.enter_context(nc.Block())

        @block.sync
        def _(sp):
            def load(name, dst, src):
                sp.dma_start(dst, src).then_inc(loads[name], 16)

            load("x0", x_sb[:, 0:4, :], x[:, 0:4, :])
            sp.dma_start(ident[:, :], consts[:, 0:P]).then_inc(loads["consts"], 16)
            sp.dma_start(rank[:, :, :], consts[:, P:2 * P].rearrange("p (t e) -> p t e", t=TT)).then_inc(loads["consts"], 16)
            load("wkcq0", wkcq_sb[:, 0:4, :], wkcq[:, 0:4, :])
            load("wq0", wq_sb[:, 0:4, :], wq[:, 0:4, :])
            load("wqkv", wqkv_sb[:, :, :], wqkv)
            load("x1", x_sb[:, 4:8, :], x[:, 4:8, :])
            sp.dma_start(bqk_sb[:, :], bqk).then_inc(loads["bias"], 16)
            sp.dma_start(bvo_sb[:, :, :], bvo).then_inc(loads["bias"], 16)
            load("wqr", wqr_sb[:, :, :, :], wqr)
            load("wout", wout_sb[:, :, :], wout)
            load("wkr", wkr_sb[:, :, :], wkr)
            for i in range(1, 4):
                hs = slice(4 * i, 4 * i + 4)
                load(f"wkcq{i}", wkcq_sb[:, hs, :], wkcq[:, hs, :])
                load(f"wq{i}", wq_sb[:, hs, :], wq[:, hs, :])
            sp.dma_start(kraw[:, :, :], ctxk[0]).then_inc(ld_ctx, 16)
            load("rope", kcos[:, :, :, :], rope)
            load("wkckv", wkckv_sb[:, :, :], wkckv)
            load("gate", gate_sb[:, :], gate)
            sp.wait_ge(s_bank, filled[("S", B - 1)])
            for i in range(4):
                hs = slice(4 * i, 4 * i + 4)
                load(f"wo{i}", wo_sb[:, hs, :], wo[:, hs, :])
            for g in range(-1, G - 1):
                if g >= 0 and g % UNITS == 0 and g // UNITS + 1 < B:
                    sp.wait_ge(s_kraw, g // UNITS + 1)
                    sp.dma_start(kraw[:, :, :], ctxk[g // UNITS + 1]).then_inc(ld_ctx, 16)
                n = g + 1
                sp.wait_ge(s_mrow, n + 1)
                if n >= 2:
                    sp.wait_ge(s_sc, 2 * KT * (n - 1))
                for half in range(2):
                    sp.dma_start(Q2[64 + half:65 + half, n % 2, :].rearrange("o (t q) -> o t q", t=QT).bitcast(f32),
                                 mrow[:, n % 2, half, :].bitcast(f32)).then_inc(s_mq, 16)
            sp.wait_ge(s_pv, KT * G)
            sp.wait_ge(s_acc, G)

            def load_chunk(c, slot, recycled=True):
                if recycled:
                    sp.wait_ge(s_whi, c - 1)
                    sp.wait_ge(s_wlo, c - 1)
                sp.dma_start(wring[:, slot, :], ffw[bass.ds(c, 1)].rearrange("o p n -> p (o n)")).then_inc(ld_ffw[slot], 16)

            load_chunk(0, 0, False)
            load_chunk(1, 1, False)
            with sp.Fori(0, PAIRS + 1) as i:
                for slot in range(2):
                    load_chunk(i * 2 + 2 + slot, slot)
            load_chunk(NF - 1, 0)
            for i in range(4):
                sp.wait_ge(s_fin, i + 1)
                sp.dma_start(out[:, 2 * i:2 * i + 2, :], x_sb[:, 2 * i:2 * i + 2, :]).then_inc(s_out, 16)
            sp.wait_ge(s_out, 64)

        @block.tensor
        def _(pe):
            mm = nc.tensor.matmul

            def fresh_bank(j):
                if before[j]:
                    evacuated(pe, before[j])

            def key_transposes(out_bank, b, i):
                for n, kt in enumerate(kgroup(i)):
                    last = nc.tensor.transpose(ps[0:DC, out_bank, n * P:(n + 1) * P], kvn[:, b % 2, kt, :], ident[:, :])
                return last

            def scores(g, kt, between):
                n, b, m = KT * g + kt, g // UNITS, P if kt < KT - 1 else LAST
                if kt == 0:
                    pe.wait_ge(s_qlo, 2 * g + 2)
                for half in range(2):
                    cols = slice(half * 512, half * 512 + 512)
                    if n:
                        pe.wait_ge(s_exp, 2 * n - 1 + half)
                    mm(ps[0:m, half, :], kcat[:, b % 2, kt * P:kt * P + m], Q1[:, g % 2, cols], start=True, stop=False)
                    if kt == 0 and half == 0:
                        pe.wait_ge(s_mq, 32 * (g + 1))
                    mm(ps[0:m, half, :], khs[:, b % 2, kt * P:kt * P + m], Q2[:, g % 2, cols],
                       start=False, stop=True).then_inc(s_sc, 1)
                    between(half)

            def context(n, between=lambda slot: None):
                g, kt = n // KT, n % KT
                m = P if kt < KT - 1 else LAST
                if kt == 0 and g:
                    pe.wait_ge(s_ctx, g)
                for r in range(2):
                    pe.wait_ge(s_exp, 2 * n + r + 1)
                    last = mm(ps[64 * r:64 * r + 64, 2, :], kvn[0:m, (g // UNITS) % 2, kt, :],
                              probs[0:m, n % 4, r * 512:r * 512 + 512], start=kt == 0, stop=kt == KT - 1)
                    if r == 0:
                        between(2)
                last.then_inc(s_pv, 1)
                between(3)

            def project_queries(g):
                b, u = g // UNITS, g % UNITS
                if g >= 1:
                    pe.wait_ge(s_mrd, NCHUNK * g)
                if g == 0:
                    evacuated(pe, ("LT2", 1))
                    for bank in range(3, 8):
                        evacuated(pe, early_user[bank])
                if g == 1:
                    pe.wait_ge(s_qlo, 2)
                for t in range(2):
                    for k in range(KD):
                        last = mm(ps[:, 6, t * S:(t + 1) * S], A_sb[:, k, u * 256 + t * P:u * 256 + (t + 1) * P],
                                  hT[:, k, b * S:(b + 1) * S], start=k == 0, stop=k == KD - 1)
                last.then_inc(s_qp, 1)

            def max_chunk(g, i):
                c = NCHUNK * g + i
                if i == 0:
                    pe.wait_ge(s_qlo, 2 * g + 1)
                if i == 1:
                    pe.wait_ge(s_qlo, 2 * g + 2)
                if i >= 2 or g:
                    pe.wait_ge(s_mrd, c - 1)
                t, half = divmod(i, 2)
                for q in range(2):
                    at = (2 * half + q) * CW
                    last = mm(ps[:, 4 + 2 * (c % 2) + q, 0:CW], Q1[:, g % 2, t * P:(t + 1) * P],
                              kcat[:, (g // UNITS) % 2, at:at + CW], start=True, stop=True)
                last.then_inc(s_mch, 1)

            def transpose_max(g):
                pe.wait_ge(s_mx, g + 1)
                nc.tensor.transpose(ps[0:QT, 3, 0:P], mx[:, :], ident[:, :]).then_inc(s_mt, 1)

            def add_up(g):
                pe.wait_ge(s_acc, g + 1)
                if g + 1 < G:
                    pe.wait_ge(s_mrow, g + 2)
                for r in range(2):
                    last = mm(ps[64 * r:64 * r + 64, 3, :], ones64[:, :], accD[:, g % 2, r * 512:r * 512 + 512],
                              start=True, stop=True)
                last.then_inc(s_sum, 1)

            for kind, i in jobs:
                j = (kind, i)
                if kind == "QP":
                    evacuated(pe, ("A", 2 * i + 1))
                    project_queries(i)
                elif kind == "M":
                    max_chunk(0, i)
                elif kind == "MT":
                    transpose_max(0)
                if kind in OTHER:
                    continue
                bk = bank_of[j]
                fresh_bank(j)
                if kind in ("LT1", "LT2"):
                    k, half = i % 2, i // 2
                    if j == ("LT1", 0):
                        pe.wait_ge(loads["consts"], 32)
                    pe.wait_ge(s_xn, (half + 1) if kind == "LT1" else half + 3)
                    for t in range(4):
                        last = nc.tensor.transpose(ps[:, bk, t * P:(t + 1) * P], xn[:, half, t, k * P:(k + 1) * P], ident[:, :])
                elif kind == "QK":
                    m, half = i % 4, i // 4
                    if i == 0:
                        arrived(pe, "wqkv")
                    evacuated(pe, ("LT1", 2 * half + 1))
                    for k in range(KD):
                        last = mm(ps[:, bk, :], wqkv_sb[:, k, m * P:(m + 1) * P], hT[:, k, half * 512:half * 512 + 512],
                                  start=k == 0, stop=k == KD - 1)
                elif kind == "V":
                    for t in range(2):
                        tok = (2 * i + t) * P
                        for k in range(KD):
                            last = mm(ps[:, bk, t * D:(t + 1) * D], hT[:, k, tok:tok + P], wqkv_sb[:, k, 2 * D:3 * D],
                                      start=k == 0, stop=k == KD - 1)
                elif kind == "S":
                    evacuated(pe, ("QK", 4 * (i // 2) + 3))
                    for q in range(2):
                        tok = i * S + q * P
                        for k in range(KD):
                            last = mm(ps[:, bk, q * S:(q + 1) * S], qkT[:, k, tok:tok + P], qkT[:, KD + k, i * S:(i + 1) * S],
                                      start=k == 0, stop=k == KD - 1)
                elif kind == "T":
                    pe.wait_ge(s_probs, i + 1)
                    for k in range(2):
                        for q in range(2):
                            last = nc.tensor.transpose(ps[:, bk, k * S + q * P:k * S + (q + 1) * P],
                                                       pr[:, i % 2, q, k * P:(k + 1) * P], ident[:, :])
                elif kind == "C":
                    evacuated(pe, ("T", i))
                    evacuated(pe, ("V", i))
                    for m in range(KD):
                        for k in range(2):
                            last = mm(ps[:, bk, m * S:(m + 1) * S], v_sb[:, 2 * i + k, m * P:(m + 1) * P], prT[:, k, :],
                                      start=k == 0, stop=k == 1)
                elif kind == "O":
                    evacuated(pe, ("C", i))
                    if i == 0:
                        arrived(pe, "wout")
                    for t in range(2):
                        for k in range(KD):
                            last = mm(ps[:, bk, t * D:(t + 1) * D], cxT[:, i % 2, k, t * P:(t + 1) * P], wout_sb[:, k, :],
                                      start=k == 0, stop=k == KD - 1)
                elif kind == "D":
                    if i % 4 == 0:
                        arrived(pe, f"wkcq{i // 4}")
                        arrived(pe, f"wq{i // 4}")
                    for b in range(2):
                        last = mm(ps[0:96, bk, b * D:(b + 1) * D], wkcq_sb[:, i, 96 * b:96 * b + 96], wq_sb[:, i, :],
                                  start=True, stop=True)
                elif kind == "E":
                    if i == 0:
                        arrived(pe, "wqr")
                    evacuated(pe, ("D", 2 * i + 1))
                    for b in range(2):
                        for r in range(2):
                            last = mm(ps[R * r:R * r + R, bk, 0:D], wqr_sb[:, 2 * i + r, b, :], DT[:, (2 * i + r) % 4, b, :],
                                      start=b == 0, stop=b == 1)
                elif kind == "A":
                    if i == 0:
                        arrived(pe, "wkr")
                    u, t = divmod(i, 2)
                    evacuated(pe, ("E", 2 * u + 1))
                    rows = slice(R * t, R * t + R)
                    for k in range(KD):
                        for r in range(2):
                            last = mm(ps[:, bk, k * P + r * DC:k * P + (r + 1) * DC], ET[rows, (2 * u + r) % 4, k * P:(k + 1) * P],
                                      wkr_sb[rows, 2 * u + r, :], start=True, stop=True)
                elif kind == "W":
                    if i == 0:
                        arrived(pe, "wkckv")
                    arrived(pe, f"wo{i}")
                    for t in range(2):
                        for r in range(2):
                            hh = 4 * i + 2 * r + t
                            last = mm(ps[64 * r:64 * r + 64, bk, t * D:(t + 1) * D], wkckv_sb[:, hh, :], wo_sb[:, hh, :],
                                      start=True, stop=True)
                elif kind == "K":
                    if i == 0:
                        pe.wait_ge(s_rope, 1)
                    last = key_transposes(bk, 0, i)
                last.then_inc(s_bank, 1)

            pe.wait_ge(s_evac["act"], count["act"])
            pe.wait_ge(s_evac["dve"], count["dve"])

            for g in range(G):
                for kt in range(KT):
                    def between(slot, g=g, kt=kt):
                        if g + 1 < G and slot in SLOTS[CHUNKS[kt]]:
                            max_chunk(g + 1, chunks_beside(kt)[SLOTS[CHUNKS[kt]].index(slot)])

                    scores(g, kt, between)
                    if kt == KT - 1 and g + 2 < G:
                        project_queries(g + 2)
                    if KT * g + kt > 0:
                        context(KT * g + kt - 1, between)
                    if kt == 2 and g:
                        add_up(g - 1)
                    if prepares_keys(g, kt):
                        i = KPREP_AT[g % UNITS, kt]
                        nb = g // UNITS + 1
                        if i == 0:
                            pe.wait_ge(s_rope, nb + 1)
                        pe.wait_ge(s_rec, g)
                        if i:
                            pe.wait_ge(s_klo, 4 * (nb - 1) + i)
                        key_transposes(3, nb, i).then_inc(s_ktr, 1)
                    if g + 1 < G and kt == 11:
                        if g:
                            pe.wait_ge(s_rec, g)
                        if g % UNITS in (1, 2) and g // UNITS + 1 < B:
                            pe.wait_ge(s_klo, 4 * (g // UNITS) + 2 * (g % UNITS))
                        transpose_max(g + 1)
            context(KT * G - 1)

            def project_context(i):
                pe.wait_ge(s_norm, UNITS * (i + 1))
                for t2 in range(2):
                    for p8 in range(8):
                        u, t = divmod(p8, 2)
                        last = mm(ps[:, i, t2 * D:(t2 + 1) * D], ctxn[:, UNITS * i + u, t * S + t2 * P:t * S + (t2 + 1) * P],
                                  Bo_sb[:, p8, :], start=p8 == 0, stop=p8 == 7)
                last.then_inc(s_o2, 1)

            def transpose_tokens(half):
                pe.wait_ge(s_xn, 5 + half)
                if half:
                    pe.wait_ge(s_x2, 4)
                for k in range(KD):
                    for t in range(4):
                        last = nc.tensor.transpose(ps[:, (4, 2)[half] + k, t * P:(t + 1) * P], xn[:, half, t, k * P:(k + 1) * P],
                                                   ident[:, :])
                    last.then_inc(s_l3, 1)

            def router(half):
                pe.wait_ge(s_xhi, 2 * half + 2)
                pe.wait_ge(s_xlo, 2 * half + 2)
                pe.wait_ge(s_gs, 2)
                terms = [(w, a, k) for k in range(KD) for w, a in ((ghi, xhi), (ghi, xlo), (glo, xhi))]
                for n, (w, a, k) in enumerate(terms):
                    last = mm(ps[0:E, 6 + half, :], w[:, k * E:(k + 1) * E], a[:, k, half * 512:half * 512 + 512],
                              start=n == 0, stop=n == len(terms) - 1)
                last.then_inc(s_lg, 1)

            def gate_up(n, slot, half, first=False):
                tok = slice(half * 512, half * 512 + 512)
                for gu in range(2):
                    if not first:
                        pe.wait_ge((s_silu, s_hu)[gu], n)
                    terms = [(w, a, k) for k in range(KD) for w, a in ((whi, xhi), (whi, xlo), (wlo, xhi))]
                    for m, (w, a, k) in enumerate(terms):
                        at = (k * 2 + gu) * P
                        last = mm(ps[:, 4 + gu, :], w[:, slot, at:at + P], a[:, k, tok], start=m == 0, stop=m == len(terms) - 1)
                    last.then_inc((s_g, s_u)[gu], 1)

            def combine_rows(n, slot, half, parity, first=False):
                if not first:
                    pe.wait_ge(s_hc, n - 1)
                mm(ps[:, 6 + parity, :], whi[0:CROWS, slot, FW - P:FW], cT[:, half * 512:half * 512 + 512],
                   start=True, stop=True).then_inc(s_c, 1)

            def down(n, slot, half, parity, first=False, final=False):
                pe.wait_ge(s_hhi, n + 1)
                pe.wait_ge(s_hlo, n + 1)
                at = 2 * KD * P
                for t in range(4):
                    tile = 4 * half + t
                    o = ps[:, tile // 2, (tile % 2) * D:(tile % 2 + 1) * D]
                    for m, (a, w) in enumerate(((hhi, whi), (hhi, wlo), (hlo, whi))):
                        last = mm(o, a[:, parity, t * P:(t + 1) * P], w[:, slot, at:at + D],
                                  start=first and m == 0 and tile % 2 == 0, stop=final and m == 2, skip_group_check=True)
                last.then_inc(s_dn, 1)

            pe.wait_ge(s_exp, 2 * KT * G)
            project_context(0)
            add_up(G - 1)
            project_context(1)
            pe.wait_ge(s_ctx, G)
            project_context(2)
            transpose_tokens(0)
            pe.wait_ge(s_rec, G)
            project_context(3)
            pe.wait_ge(s_xhi, 2)
            pe.wait_ge(s_xlo, 2)
            pe.wait_ge(s_whi, 1)
            pe.wait_ge(s_wlo, 1)
            gate_up(0, 0, 0, first=True)
            router(0)
            transpose_tokens(1)
            router(1)
            gate_up(1, 0, 1)
            pe.wait_ge(s_lgs, 2)
            for t in range(TT):
                last = nc.tensor.transpose(ps[:, 0, t * E:(t + 1) * E], lgT[:, t * P:(t + 1) * P], ident[0:E, 0:E])
            last.then_inc(s_lgt, 1)
            pe.wait_ge(s_whi, 2)
            pe.wait_ge(s_wlo, 2)
            gate_up(2, 1, 0)
            gate_up(3, 1, 1)
            pe.wait_ge(s_comb, 1)
            for half in range(2):
                for t in range(4):
                    last = nc.tensor.transpose(ps[0:CROWS, half, t * P:(t + 1) * P], comb[:, 4 * half + t, :].bitcast(f32), ident[:, :])
                last.then_inc(s_ct, 1)
            for half in range(2):
                pe.wait_ge(s_ctc, half + 1)
                combine_rows(half, 0, half, half, first=True)
            for n in range(2):
                down(n, 0, n, n, first=True)
                combine_rows(n + 2, 1, n, n)
            down(2, 1, 0, 0)

            def half_chunks(c, slot, combined=True):
                for half in range(2):
                    n = c * 2 + half
                    if half == 0:
                        pe.wait_ge(s_whi, c + 1)
                        pe.wait_ge(s_wlo, c + 1)
                    gate_up(n, slot, half)
                    if combined:
                        combine_rows(n, slot, half, half)
                    down(n - 1, slot if half else 1 - slot, 1 - half, 1 - half)

            with pe.Fori(0, PAIRS) as i:
                for slot in range(2):
                    half_chunks(i * 2 + 2 + slot, slot)
            for c in range(NE, NF):
                half_chunks(c, c % 2, combined=False)
            down(NH - 1, (NF - 1) % 2, 1, 1, final=True)

        @block.scalar
        def _(act):
            acts = nc.scalar.activation
            chain = [0]
            nc.scalar.preload_act_table_set("natural_log_exp_and_others")

            def link(ins):
                chain[0] += 1
                ins.then_inc(s_alink, 1)
                act.wait_ge(s_alink, chain[0])

            def ln_estimate(n):
                act.wait_ge(s_ln_var, n + 1)
                link(acts(lnw[:, 1, :], lnw[:, 0, :], ACT.Ln))
                acts(lnw[:, 2, :], lnw[:, 1, :], ACT.Exp, scale=-0.5).then_inc(s_ln_est, 1)

            def exponentials(g, kt):
                n, m = KT * g + kt, P if kt < KT - 1 else LAST
                if n >= 4:
                    act.wait_ge(s_pv, n - 3)
                    g4, kt4 = divmod(n - 4, KT)
                    if kt4 % 2 == 0:
                        act.wait_ge(s_addD, 6 * g4 + releasedD(kt4))
                    else:
                        act.wait_ge(s_addP, 5 * g4 + releasedP(kt4))
                for half in range(2):
                    act.wait_ge(s_sc, 2 * n + half + 1)
                    acts(probs[0:m, n % 4, half * 512:half * 512 + 512], ps[0:m, half, :], ACT.Exp).then_inc(s_exp, 1)

            def query_high(g):
                act.wait_ge(s_qp, g + 1)
                if g >= 2:
                    act.wait_ge(s_sc, 2 * KT * (g - 1))
                for r in range(2):
                    last = acts(Q1[0:64, g % 2, 512 * r:512 * r + 512], ps[64 * r:64 * r + 64, 6, :], ACT.Copy)
                last.then_inc(s_qhi, 1)

            def key_high(b, i):
                act.wait_ge(s_ktr, 4 * (b - 1) + i + 1)
                if i == 0 and b >= 2:
                    act.wait_ge(s_sc, 2 * KT * UNITS * (b - 1))
                w = len(kgroup(i)) * P
                at = slice(4 * P * i, 4 * P * i + w)
                acts(kcat[0:64, b % 2, at], ps[0:64, 3, 0:w], ACT.Copy).then_inc(s_khi, 1)
                acts(khs[0:64, b % 2, at], ps[0:64, 3, 0:w], ACT.Copy).then_inc(s_khi, 1)

            def read_context(g):
                act.wait_ge(s_pv, KT * (g + 1))
                if g:
                    act.wait_ge(s_norm, g)
                acts(nctx, ps[:, 2, :], ACT.Copy, scale=-1.0).then_inc(s_ctx, 1)

            def estimate(g):
                act.wait_ge(s_sum, g + 1)
                if g:
                    act.wait_ge(s_rec, g)
                link(acts(est, ps[:, 3, :], ACT.Ln))
                acts(est, est, ACT.Exp, scale=-1.0).then_inc(s_est, 1)

            for kind, i in jobs:
                j = (kind, i)
                if kind in ("LE1", "LE2"):
                    ln_estimate(i + (2 if kind == "LE2" else 0))
                    continue
                if kind == "QP":
                    query_high(i)
                if kind in OTHER:
                    continue
                if kind == "K":
                    act.wait_ge(s_bank, filled[j])
                    w = len(kgroup(i)) * P
                    if i == 0:
                        act.wait_ge(s_const, 1)
                    at = slice(4 * P * i, 4 * P * i + w)
                    acts(kcat[0:64, 0, at], ps[0:64, bank_of[j], 0:w], ACT.Copy).then_inc(s_khi, 1)
                    acts(khs[0:64, 0, at], ps[0:64, bank_of[j], 0:w], ACT.Copy).then_inc(s_khi, 1)
                    continue
                if evac_by[kind] != "act":
                    continue
                act.wait_ge(s_bank, filled[j])
                bk = ps[:, bank_of[j], :]
                if kind in ("LT1", "LT2"):
                    k, half = i % 2, i // 2
                    last = acts(hT[:, k, half * 512:half * 512 + 512], bk, ACT.Copy)
                elif kind == "QK":
                    m, half = i % 4, i // 4
                    if i == 0:
                        act.wait_ge(loads["bias"], 32)
                    last = acts(qkT[:, m, half * 512:half * 512 + 512], bk, ACT.Identity, bias=bqk_sb[:, m:m + 1])
                elif kind == "S":
                    act.wait_ge(s_smax, i + 1)
                    if i >= 2:
                        act.wait_ge(s_bank, filled[("T", i - 2)])
                    for q in range(2):
                        last = acts(pr[:, i % 2, q, :], bk[:, q * S:(q + 1) * S], ACT.Exp, scale=D ** -0.5,
                                    bias=smx[:, i % 2, 1, q:q + 1], accum_out=smx[:, i % 2, 2, q:q + 1])
                elif kind == "T":
                    if i:
                        act.wait_ge(s_bank, filled[("C", i - 1)])
                    last = acts(prT[:, :, :], bk.rearrange("p (k q) -> p k q", k=2), ACT.Copy)
                elif kind == "D":
                    if i >= 4:
                        act.wait_ge(s_bank, filled[("E", i // 2 - 2)])
                    last = acts(DT[:, i % 4, :, :], bk[0:96].rearrange("p (b n) -> p b n", b=2), ACT.Copy)
                elif kind == "E":
                    if i >= 4:
                        act.wait_ge(s_bank, filled[("A", 2 * (i // 2 - 2) + 1)])
                    last = acts(ET[:, i % 4, :], bk[:, 0:D], ACT.Copy)
                elif kind == "A":
                    last = acts(A_sb[:, :, i * P:(i + 1) * P], bk[:, 0:2 * P].rearrange("p (k n) -> p k n", k=2), ACT.Copy)
                elif kind == "W":
                    last = acts(Bo_sb[:, 2 * i:2 * i + 2, :], bk.rearrange("p (t n) -> p t n", t=2), ACT.Copy)
                last.then_inc(s_evac["act"], 1)

            for g in range(G):
                for kt in range(KT):
                    exponentials(g, kt)
                    if kt == 0 and g:
                        read_context(g - 1)
                    if kt == 3 and g:
                        estimate(g - 1)
                    if kt == KT - 1 and g + 2 < G:
                        query_high(g + 2)
                    if prepares_keys(g, kt):
                        key_high(g // UNITS + 1, KPREP_AT[g % UNITS, kt])
            read_context(G - 1)
            estimate(G - 1)

            def tokens_high(half):
                for k in range(KD):
                    act.wait_ge(s_l3, 2 * half + k + 1)
                    acts(xhi[:, k, half * 512:half * 512 + 512], ps[:, (4, 2)[half] + k, :], ACT.Copy).then_inc(s_xhi, 1)

            def weights_high(c, slot, turn):
                act.wait_ge(ld_ffw[slot], (turn + 1) * 16)
                acts(whi[:, slot, :], wring[:, slot, :], ACT.Copy).then_inc(s_whi, 1)

            def silu_of(n, parity, first=False):
                act.wait_ge(s_g, n + 1)
                if not first:
                    act.wait_ge(s_hu, n - 1)
                acts(silu[:, parity, :], ps[:, 4, :], ACT.Silu).then_inc(s_silu, 1)

            def hidden_high(n, parity, first=False, combined=True):
                act.wait_ge(s_hc if combined else s_hu, n + 1)
                if not first:
                    act.wait_ge(s_dn, n - 1)
                acts(hhi[:, parity, :], hful[:, parity, :], ACT.Copy).then_inc(s_hhi, 1)

            ln_estimate(4)
            tokens_high(0)
            weights_high(0, 0, 0)
            weights_high(1, 1, 0)
            ln_estimate(5)
            silu_of(0, 0, first=True)
            tokens_high(1)
            for half in range(2):
                act.wait_ge(s_lg, half + 1)
                acts(lgT[:, half * 512:half * 512 + 512], ps[0:E, 6 + half, :], ACT.Copy).then_inc(s_lgs, 1)
            silu_of(1, 1, first=True)
            act.wait_ge(s_rsub, 1)
            acts(rt[:, 1, :, :], rt[:, 0, :, :], ACT.Exp).then_inc(s_rexp, 1)
            silu_of(2, 0)
            silu_of(3, 1)
            for half in range(2):
                act.wait_ge(s_ct, half + 1)
                acts(cT[:, half * 512:half * 512 + 512], ps[0:CROWS, half, :], ACT.Copy).then_inc(s_ctc, 1)
            for n in FIRST:
                hidden_high(n, n % 2, first=n < 2)
                if n == 2:
                    act.wait_ge(s_dn, 2)
                    weights_high(2, 0, 1)

            def half_chunks_act(c, slot, turn, combined=True, last=False):
                for half in range(2):
                    n = c * 2 + half
                    silu_of(n, half)
                    hidden_high(n, half, combined=combined)
                    if half == 0 and not last:
                        act.wait_ge(s_dn, c * 2)
                        weights_high(c + 1, 1 - slot, turn + slot)

            with act.Fori(0, PAIRS) as i:
                for slot in range(2):
                    half_chunks_act(i * 2 + 2 + slot, slot, i + 1)
            for c in range(NE, NF):
                half_chunks_act(c, c % 2, c // 2, combined=False, last=c == NF - 1)

        @block.gpsimd
        def _(pool):
            chain = [0]

            def link(ins):
                chain[0] += 1
                ins.then_inc(s_plink, 1)
                pool.wait_ge(s_plink, chain[0])

            link(nc.gpsimd.memset(ones64[:, :], 1.0))
            link(nc.gpsimd.memset(Q2[64:128, :, :].bitcast(f32), 0.0))
            link(nc.gpsimd.memset(khs[64:128, :, :].bitcast(f32), 0.0))
            nc.gpsimd.memset(khs[64:66, :, :].bitcast(f32), 1.0).then_inc(s_const, 1)
            pool.wait_ge(s_const, 1)

            def rotate(b):
                if b == 0:
                    arrived(pool, "rope")
                pool.wait_ge(ld_ctx, 16 * (b + 1))
                if b >= 2:
                    pool.wait_ge(s_pv, KT * UNITS * (b - 1))
                    pool.wait_ge(s_klo, 4 * (b - 1))
                hd = DC // 2
                nc.gpsimd.tensor_tensor(kvn[:, b % 2, :, :], kraw[:, :, :], kcos[:, 0], ALU.mult)
                nc.gpsimd.tensor_tensor(kt2[:, :, 0:hd], kraw[:, :, hd:DC], kcos[:, 1, :, 0:hd], ALU.mult)
                ins = nc.gpsimd.tensor_tensor(kt2[:, :, hd:DC], kraw[:, :, 0:hd], kcos[:, 1, :, hd:DC], ALU.mult)
                ins.then_inc(s_kraw, 1)
                pool.wait_ge(s_kraw, b + 1)
                nc.gpsimd.tensor_tensor(kvn[:, b % 2, :, :], kvn[:, b % 2, :, :], kt2[:, :, :], ALU.add).then_inc(s_rope, 1)

            rotate(0)

            def add_odd(g, kt):
                n = KT * g + kt
                pool.wait_ge(s_exp, 2 * n + 2)
                if kt == 3:
                    if g:
                        pool.wait_ge(s_acc, g)
                    nc.gpsimd.tensor_tensor(accP, probs[:, (n - 2) % 4, :], probs[:, n % 4, :], ALU.add).then_inc(s_addP, 1)
                elif kt > 3:
                    pool.wait_ge(s_addP, 5 * g + releasedP(kt) - 1)
                    nc.gpsimd.tensor_tensor(accP, accP, probs[:, n % 4, :], ALU.add).then_inc(s_addP, 1)

            def combine(g):
                pool.wait_ge(s_addD, 6 * (g + 1))
                pool.wait_ge(s_addP, 5 * (g + 1))
                a = accD[:, g % 2, :]
                nc.gpsimd.tensor_tensor(a, a, accP, ALU.add).then_inc(s_acc, 1)

            def norm(g):
                pool.wait_ge(s_rec, g + 1)
                pool.wait_ge(s_ctx, g + 1)
                nc.gpsimd.tensor_tensor(ctxn[:, g, :], corr, nctx, ALU.mult).then_inc(s_norm, 1)

            for g in range(G):
                if g:
                    combine(g - 1)
                for kt in range(1, KT, 2):
                    add_odd(g, kt)
                    if kt == 5 and g:
                        norm(g - 1)
                if g % UNITS == 0 and g // UNITS + 1 < B:
                    rotate(g // UNITS + 1)
            norm(G - 1)

            def weights_low(c, slot, turn):
                pool.wait_ge(ld_ffw[slot], (turn + 1) * 16)
                pool.wait_ge(s_whi, c + 1)
                nc.gpsimd.tensor_tensor(wlo[:, slot, 0:FW - P], wring[:, slot, 0:FW - P],
                                        whi[:, slot, 0:FW - P].bitcast(f32), ALU.subtract).then_inc(s_wlo, 1)

            weights_low(0, 0, 0)
            weights_low(1, 1, 0)
            with pool.Fori(0, PAIRS + 1) as i:
                for slot in range(2):
                    weights_low(i * 2 + 2 + slot, slot, i + 1)
            weights_low(NF - 1, 0, NF // 2)

        @block.vector
        def _(dve):
            V = nc.vector
            chain = [0]

            def link(ins):
                chain[0] += 1
                ins.then_inc(s_link, 1)
                dve.wait_ge(s_link, chain[0])

            def layer_norm(n, half):
                for t in range(4):
                    ins = V.bn_stats(stats[:, t, :], x_sb[:, 4 * half + t, :])
                link(ins)
                for t in range(4):
                    ins = V.bn_aggr(mv[:, t, :], stats[:, t, :])
                link(ins)
                V.tensor_scalar(lnw[:, 0, :], mv[:, :, 1], EPS, None, ALU.add).then_inc(s_ln_var, 1)
                dve.wait_ge(s_ln_est, n + 1)
                link(V.tensor_tensor(lnw[:, 3, :], lnw[:, 2, :], lnw[:, 2, :], ALU.mult))
                link(V.tensor_tensor(lnw[:, 3, :], lnw[:, 3, :], lnw[:, 0, :], ALU.mult))
                link(V.tensor_scalar(lnw[:, 3, :], lnw[:, 3, :], -0.5, 1.5, ALU.mult, ALU.add))
                link(V.tensor_tensor(lnw[:, 4, :], lnw[:, 3, :], lnw[:, 2, :], ALU.mult))
                if n >= 2:
                    dve.wait_ge(s_bank, filled[("LT1" if n < 4 else "LT2", 2 * half + 1)])
                for t in range(4):
                    ins = V.tensor_scalar(xn[:, half, t, :], x_sb[:, 4 * half + t, :], mv[:, t, 0:1], lnw[:, 4, t:t + 1],
                                          ALU.subtract, ALU.mult)
                ins.then_inc(s_xn, 1)

            def query_low(g):
                dve.wait_ge(s_qhi, g + 1)
                if g == 0:
                    dve.wait_ge(s_const, 1)
                V.tensor_copy(Q1[64:128, g % 2, :], Q1[0:64, g % 2, :].bitcast(f32)).then_inc(s_qlo, 1)
                for r in range(2):
                    last = V.tensor_tensor(Q2[0:64, g % 2, 512 * r:512 * r + 512], ps[64 * r:64 * r + 64, 6, :],
                                           Q1[0:64, g % 2, 512 * r:512 * r + 512].bitcast(f32), ALU.subtract)
                last.then_inc(s_qlo, 1)

            def key_low(b, i):
                dve.wait_ge(s_khi, 8 * b + 2 * (i + 1))
                w = len(kgroup(i)) * P
                at = slice(4 * P * i, 4 * P * i + w)
                V.tensor_tensor(kcat[64:128, b % 2, at], ps[0:64, 3, 0:w], kcat[0:64, b % 2, at].bitcast(f32),
                                ALU.subtract).then_inc(s_klo, 1)

            def max_chunk(g, i):
                dve.wait_ge(s_mch, NCHUNK * g + i + 1)
                if i == 0 and g:
                    dve.wait_ge(s_mx, g)
                t, half = divmod(i, 2)
                V.reduce_max(mxp[:, t, half:half + 1], ps[:, 4 + 2 * half:6 + 2 * half, 0:CW], AX.XY).then_inc(s_mrd, 1)

            def reduce_chunks(g):
                dve.wait_ge(s_mrd, NCHUNK * (g + 1))
                if g:
                    dve.wait_ge(s_mt, g)
                V.reduce_max(mx[:, :], mxp[:, :, :], AX.X).then_inc(s_mx, 1)

            def max_rows(g):
                dve.wait_ge(s_mt, g + 1)
                if g >= 2:
                    dve.wait_ge(s_mq, 32 * (g - 1))
                link(V.tensor_scalar(mrow[:, g % 2, 0, :], ps[0:QT, 3, 0:P], -1.0, None, ALU.mult))
                V.scalar_tensor_tensor(out=mrow[:, g % 2, 1, :], in0=ps[0:QT, 3, 0:P], scalar=-1.0,
                                       in1=mrow[:, g % 2, 0, :].bitcast(f32), op0=ALU.mult, op1=ALU.subtract).then_inc(s_mrow, 1)

            def add_even(g, kt):
                n, m = KT * g + kt, P if kt < KT - 1 else LAST
                if kt == 0:
                    return
                dve.wait_ge(s_exp, 2 * n + 2)
                a = accD[:, g % 2, :]
                if kt == 2:
                    if g >= 2:
                        dve.wait_ge(s_sum, g - 1)
                    V.tensor_tensor(a, probs[:, (n - 2) % 4, :], probs[:, n % 4, :], ALU.add).then_inc(s_addD, 1)
                else:
                    dve.wait_ge(s_addD, 6 * g + releasedD(kt) - 1)
                    V.tensor_tensor(a[0:m], a[0:m], probs[0:m, n % 4, :], ALU.add).then_inc(s_addD, 1)

            def reciprocal_sum(g):
                dve.wait_ge(s_est, g + 1)
                if g:
                    dve.wait_ge(s_norm, g)
                link(V.tensor_tensor(corr, est, ps[:, 3, :], ALU.mult))
                V.scalar_tensor_tensor(out=corr, in0=corr, scalar=-2.0, in1=est, op0=ALU.add, op1=ALU.mult).then_inc(s_rec, 1)

            for kind, i in jobs:
                j = (kind, i)
                if kind == "LN1":
                    arrived(dve, f"x{i}")
                    layer_norm(i, i)
                elif kind == "LN2":
                    layer_norm(2 + i, i)
                elif kind == "QP":
                    query_low(i)
                elif kind == "M":
                    max_chunk(0, i)
                elif kind == "MX":
                    reduce_chunks(0)
                elif kind == "MR":
                    max_rows(0)
                elif kind in ("MT", "LE1", "LE2"):
                    pass
                elif kind == "S":
                    dve.wait_ge(s_bank, filled[j])
                    if i >= 2:
                        dve.wait_ge(s_probs, i - 1)
                    link(V.reduce_max(smx[:, i % 2, 0, :], ps[:, bank_of[j], :].rearrange("p (q k) -> p q k", q=2), AX.X))
                    V.tensor_scalar(smx[:, i % 2, 1, :], smx[:, i % 2, 0, :], -D ** -0.5, None, ALU.mult).then_inc(s_smax, 1)
                elif kind == "T":
                    evacuated(dve, ("S", i))
                    link(V.reciprocal(smx[:, i % 2, 3, :], smx[:, i % 2, 2, :]))
                    for q in range(2):
                        ins = V.tensor_scalar(pr[:, i % 2, q, :], pr[:, i % 2, q, :], smx[:, i % 2, 3, q:q + 1], None, ALU.mult)
                    ins.then_inc(s_probs, 1)
                elif kind == "K":
                    w = len(kgroup(i)) * P
                    at = slice(4 * P * i, 4 * P * i + w)
                    dve.wait_ge(s_khi, 2 * (i + 1))
                    V.tensor_tensor(kcat[64:128, 0, at], ps[0:64, bank_of[j], 0:w], kcat[0:64, 0, at].bitcast(f32),
                                    ALU.subtract).then_inc(s_evac["dve"], 1)
                elif evac_by[kind] == "dve":
                    dve.wait_ge(s_bank, filled[j])
                    bk = ps[:, bank_of[j], :]
                    if kind == "V":
                        if i == 0:
                            dve.wait_ge(loads["bias"], 32)
                        ins = V.tensor_tensor(v_sb[:, 2 * i:2 * i + 2, :], bk.rearrange("p (t n) -> p t n", t=2),
                                              bvo_sb[:, 0:1, :].broadcast_to([P, 2, D]), ALU.add)
                    elif kind == "C":
                        if i >= 2:
                            dve.wait_ge(s_bank, filled[("O", i - 2)])
                        ins = V.tensor_copy(cxT[:, i % 2, :, :], bk.rearrange("p (k n) -> p k n", k=2))
                    elif kind == "O":
                        xt = x_sb[:, 2 * i:2 * i + 2, :]
                        link(V.tensor_tensor(xt, xt, bk.rearrange("p (t n) -> p t n", t=2), ALU.add))
                        ins = V.tensor_tensor(xt, xt, bvo_sb[:, 1:2, :].broadcast_to([P, 2, D]), ALU.add)
                    ins.then_inc(s_evac["dve"], 1)
                    if kind == "O":
                        evacuated(dve, j)

            for g in range(G):
                for kt in range(KT):
                    if kt == 4 and g:
                        reciprocal_sum(g - 1)
                    todo = list(chunks_beside(kt)) if g + 1 < G else []
                    for i in todo[:1]:
                        max_chunk(g + 1, i)
                    if kt % 2 == 0:
                        add_even(g, kt)
                    for i in todo[1:]:
                        max_chunk(g + 1, i)
                    if kt == 10 and g + 1 < G:
                        reduce_chunks(g + 1)
                    if kt == 11 and g + 1 < G:
                        max_rows(g + 1)
                    if kt == KT - 1 and g + 2 < G:
                        query_low(g + 2)
                    if prepares_keys(g, kt):
                        key_low(g // UNITS + 1, KPREP_AT[g % UNITS, kt])
            dve.wait_ge(s_addD, 6 * G)
            dve.wait_ge(s_addP, 5 * G)
            V.tensor_tensor(accD[:, (G - 1) % 2, :], accD[:, (G - 1) % 2, :], accP, ALU.add).then_inc(s_acc, 1)

            arrived(dve, "gate")
            dve.wait_ge(s_sc, 2 * KT * G)
            V.tensor_copy(ghi, gate_sb[:, :]).then_inc(s_gs, 1)
            dve.wait_ge(s_gs, 1)
            V.tensor_tensor(glo, gate_sb[:, :], ghi.bitcast(f32), ALU.subtract).then_inc(s_gs, 1)
            link(V.memset(comb.bitcast(f32), 0.0))

            def residual(i):
                dve.wait_ge(s_o2, i + 1)
                xt = x_sb[:, 2 * i:2 * i + 2, :]
                V.tensor_tensor(xt, xt, ps[:, i, :].rearrange("p (t n) -> p t n", t=2), ALU.add).then_inc(s_x2, 1)

            def tokens_low(half):
                at = slice(half * 512, half * 512 + 512)
                for k in range(KD):
                    dve.wait_ge(s_xhi, 2 * half + k + 1)
                    V.tensor_tensor(xlo[:, k, at], ps[:, (4, 2)[half] + k, :], xhi[:, k, at].bitcast(f32),
                                    ALU.subtract).then_inc(s_xlo, 1)

            def silu_up(n, parity, slot4, first=False, shared=False):
                dve.wait_ge(s_u, n + 1)
                dve.wait_ge(s_silu, n + 1)
                if shared:
                    dve.wait_ge(s_hhi, n - 1)
                    dve.wait_ge(s_hlo, n - 1)
                elif not first:
                    dve.wait_ge(s_hc, n - 3)
                dst = hful[:, parity, :] if shared else hsu[:, slot4, :]
                V.tensor_tensor(dst, silu[:, parity, :], ps[:, 5, :], ALU.mult).then_inc(s_hu, 1)

            def weigh(n, parity, slot4, first=False):
                dve.wait_ge(s_c, n + 1)
                dve.wait_ge(s_hu, n + 1)
                if not first:
                    dve.wait_ge(s_hhi, n - 1)
                    dve.wait_ge(s_hlo, n - 1)
                V.tensor_tensor(hful[:, parity, :], hsu[:, slot4, :], ps[:, 6 + parity, :], ALU.mult).then_inc(s_hc, 1)

            def hidden_low(n, parity, first=False):
                dve.wait_ge(s_hhi, n + 1)
                if not first:
                    dve.wait_ge(s_dn, n - 1)
                V.tensor_tensor(hlo[:, parity, :], hful[:, parity, :], hhi[:, parity, :].bitcast(f32),
                                ALU.subtract).then_inc(s_hlo, 1)

            residual(0)
            reciprocal_sum(G - 1)
            residual(1)
            dve.wait_ge(s_x2, 2)
            layer_norm(4, 0)
            tokens_low(0)
            residual(2)
            residual(3)
            dve.wait_ge(s_x2, 4)
            layer_norm(5, 1)
            silu_up(0, 0, 0, first=True)
            tokens_low(1)
            silu_up(1, 1, 1, first=True)

            def wide(a):
                return a.rearrange("p (t o) -> p t o", o=1).broadcast_to([P, TT, E])

            dve.wait_ge(s_lgt, 1)
            lg = ps[:, 0, 0:TT * E].rearrange("p (t e) -> p t e", t=TT)
            link(V.reduce_max(rs[:, 0, :], lg, AX.X))
            V.tensor_tensor(rt[:, 0], lg, wide(rs[:, 0, :]), ALU.subtract).then_inc(s_rsub, 1)
            V.memset(rt[:, 5], 0.0)
            dve.wait_ge(s_rexp, 1)
            link(V.reduce_sum(rs[:, 1, :], rt[:, 1], AX.X))
            link(V.reciprocal(rs[:, 2, :], rs[:, 1, :]))
            link(V.tensor_tensor(rt[:, 1], rt[:, 1], wide(rs[:, 2, :]), ALU.mult))
            dve.wait_ge(loads["consts"], 32)
            cur = rt[:, 1]
            for turn in range(2):
                link(V.reduce_max(rs[:, 3, :], cur, AX.X))
                link(V.tensor_tensor(rt[:, 3], cur, wide(rs[:, 3, :]), ALU.is_equal))
                link(V.tensor_tensor(rt[:, 3], rt[:, 3], rank[:, :, :], ALU.mult))
                link(V.reduce_max(rs[:, 4, :], rt[:, 3], AX.X))
                link(V.tensor_tensor(rt[:, 4], rt[:, 3], wide(rs[:, 4, :]), ALU.is_equal))
                ins = V.tensor_tensor(rt[:, 5], rt[:, 5], rt[:, 4], ALU.add)
                if turn == 0:
                    silu_up(2, 0, 2, first=True)
                    ins = V.scalar_tensor_tensor(out=rt[:, 2], in0=rt[:, 4], scalar=-4.0, in1=rt[:, 1], op0=ALU.mult, op1=ALU.add)
                link(ins)
                cur = rt[:, 2]
            link(V.tensor_tensor(cmb[:, :, :], rt[:, 1], rt[:, 5], ALU.mult))
            link(V.tensor_copy(comb[:, :, 0:E], cmb[:, :, :]))
            V.tensor_tensor(comb[:, :, CROW:CROWS], cmb[:, :, :], comb[:, :, 0:E].bitcast(f32), ALU.subtract).then_inc(s_comb, 1)
            silu_up(3, 1, 3, first=True)
            for n in FIRST:
                weigh(n, n % 2, n, first=n < 2)
                hidden_low(n, n % 2, first=n < 2)
            with dve.Fori(0, PAIRS) as i:
                for slot in range(2):
                    for half in range(2):
                        n = i * 4 + (4 + 2 * slot + half)
                        silu_up(n, half, 2 * slot + half)
                        weigh(n, half, 2 * slot + half)
                        hidden_low(n, half)
            for n, c, half in TAIL:
                silu_up(n, half, None, shared=True)
                dve.wait_ge(s_hu, n + 1)
                hidden_low(n, half)
            for i in range(4):
                dve.wait_ge(s_dn, NH - 1 + i // 2)
                xt = x_sb[:, 2 * i:2 * i + 2, :]
                V.tensor_tensor(xt, xt, ps[:, i, :].rearrange("p (t n) -> p t n", t=2), ALU.add).then_inc(s_fin, 1)


def _tables():
    f = np.float32
    inv = (f(1.0) / f(10000.0) ** (np.arange(0, DC, 2, dtype=f) / f(DC))).astype(f)
    ang = np.arange(L, dtype=f)[:, None] * inv[None, :]
    sin = np.repeat(np.sin(ang), 2, axis=-1)
    cos = np.repeat(np.cos(ang), 2, axis=-1)
    sin[:, :DC // 2] = -sin[:, :DC // 2]
    sel = np.zeros((NF, P, P), f)
    for c in range(NF):
        for p in range(P):
            i = c * P + p
            e = i // I
            if c < NE:
                sel[c, e, p] = sel[c, CROW + e, p] = 1.0
    rank = np.tile((E - np.arange(E)).astype(f), (P, TT))
    consts = np.concatenate([np.eye(P, dtype=f), rank], axis=1)
    return cos, sin, sel, consts


def _by_key(a):
    idx = np.minimum(np.arange(KT * P), L - 1)
    a = a[..., idx, :]
    a = a.reshape(*a.shape[:-2], KT, P, DC)
    return np.ascontiguousarray(np.swapaxes(a, -3, -2))


def _rows(a, n):
    return np.ascontiguousarray(a.reshape(n, P, -1).transpose(1, 0, 2))


def kernel(x, ctx_512, L0_attn_w_qkv, L0_attn_b_qkv, L0_attn_w_out, L0_attn_b_out, L0_xattn_Wq, L0_xattn_w_kc_q,
           L0_xattn_w_kc_kv, L0_xattn_W_qr, L0_xattn_W_kr, L0_xattn_Wo, L0_ffn_gate_w, L0_ffn_w_gate_up,
           L0_ffn_w_down, L0_ffn_shared_gate_up, L0_ffn_shared_down):
    import concourse.bacc as bacc
    from concourse.bass_utils import run_bass_kernel_spmd

    A = np.asarray
    cos, sin, sel, consts = _tables()
    gu = A(L0_ffn_w_gate_up)
    pad = NF * P - E * I - SHARED
    sgu, sdn = A(L0_ffn_shared_gate_up), A(L0_ffn_shared_down)

    def hidden(first, shared):
        a = np.concatenate([first.transpose(1, 0, 2).reshape(D, E * I), shared, np.zeros((D, pad), shared.dtype)], axis=1)
        return a.reshape(KD, P, NF, P).transpose(2, 1, 0, 3)

    gates = hidden(gu[:, :, :I], sgu[:, :SHARED])
    ups = hidden(gu[:, :, I:], sgu[:, SHARED:])
    gup = np.stack([gates, ups], axis=3).reshape(NF, P, 2 * KD * P)
    down = np.concatenate([A(L0_ffn_w_down).reshape(E * I, D), sdn, np.zeros((pad, D), sdn.dtype)]).reshape(NF, P, D)
    arrays = {
        "x": A(x).reshape(TT, P, D).transpose(1, 0, 2),
        "ctxk": _by_key(A(ctx_512)),
        "rope": np.stack([_by_key(cos), _by_key(sin)], axis=1),
        "wqkv": _rows(A(L0_attn_w_qkv).T, KD),
        "bqk": A(L0_attn_b_qkv)[:2 * D].reshape(4, P).T,
        "bvo": np.broadcast_to(np.stack([A(L0_attn_b_qkv)[2 * D:], A(L0_attn_b_out)])[None], (P, 2, D)),
        "wout": _rows(A(L0_attn_w_out).T, KD),
        "wq": A(L0_xattn_Wq).reshape(H, HK, D).transpose(1, 0, 2),
        "wkcq": A(L0_xattn_w_kc_q).transpose(1, 0, 2),
        "wqr": A(L0_xattn_W_qr).reshape(H, 2, 96, R).transpose(2, 0, 1, 3),
        "wkr": A(L0_xattn_W_kr).reshape(H // 2, 2, DC, R).transpose(1, 3, 0, 2).reshape(P, H // 2, DC),
        "wkckv": A(L0_xattn_w_kc_kv).transpose(1, 0, 2),
        "wo": A(L0_xattn_Wo).reshape(D, H, HK).transpose(2, 1, 0),
        "gate": A(L0_ffn_gate_w).T.reshape(KD, P, E).transpose(1, 0, 2).reshape(P, KD * E),
        "ffw": np.concatenate([gup, down, sel], axis=2),
        "consts": consts,
    }
    nc = bacc.Bacc("TRN2", target_bir_lowering=False, num_devices=1)
    feeds, args = {}, []
    for name, a in arrays.items():
        a = np.ascontiguousarray(a)
        feeds["in_" + name] = a
        args.append(nc.dram_tensor("in_" + name, a.shape, mybir.dt.from_np(a.dtype), kind="ExternalInput").ap())
    out = nc.dram_tensor("out_0", (P, TT, D), mybir.dt.float32, kind="ExternalOutput").ap()
    build(nc, *args, out)
    r = run_bass_kernel_spmd(nc, [feeds], core_ids=[0])
    return r.results[0]["out_0"].transpose(1, 0, 2).reshape(B, S, D)
```

```python
from contextlib import ExitStack

import numpy as np

import concourse.bass as bass
from concourse import mybir
from concourse.alu_op_type import AluOpType as ALU

B, S, D = 4, 256, 256
L, DC = 1601, 64
H, HK, DQ, R = 16, 128, 192, 64
E, I = 16, 176
P = 128
T = B * S
TT = T // P
KD = D // P
KT = -(-L // P)
LAST = L - (KT - 1) * P
UNITS = 4
G = B * UNITS
C = 4 * S
QT = C // P
CW = 402
NCHUNK = QT * 2
SHARED = 2 * I
NE = E * I // P
assert NE * P == E * I and NE % 2 == 0
NS = -(-SHARED // P)
assert NS == 3
NF = NS + NE
FW = 2 * KD * P + D + P
EPS = 1e-5
CROW = 32
CROWS = CROW + E


def build(nc, x, ctxk, rope, wqkv, bqk, bvo, wout, wq, wkcq, wqr, wkr, wkckv, wo, gate, ffw, consts, out):
    f32, f32r = mybir.dt.float32, mybir.dt.float32r
    ACT, AX = mybir.ActivationFunctionType, mybir.AxisListType
    es = ExitStack()
    with es:
        def sb(name, shape, dt=f32):
            return es.enter_context(nc.sbuf_tensor(name, shape, dt))

        def sem(name):
            return es.enter_context(nc.semaphore(name))

        x_sb = sb("x_sb", [P, TT, D])
        hT = sb("hT", [P, KD, T])
        A_sb = sb("A_sb", [P, KD, UNITS * 256])
        Bo_sb = sb("Bo_sb", [P, 8, D])
        ident = sb("ident", [P, P])
        rank = sb("rank", [P, TT, E])
        ones64 = sb("ones64", [P, 64])
        bqk_sb = sb("bqk_sb", [P, 4])
        bvo_sb = sb("bvo_sb", [P, 2, D])
        gate_sb = sb("gate_sb", [P, KD * E])
        xn = sb("xn", [P, 2, 4, D])
        stats = sb("stats", [P, 4, 6])
        mv = sb("mv", [P, 4, 2])
        lnw = sb("lnw", [P, 5, 4])
        smx = sb("smx", [P, 2, 4, 2])
        big = sb("big", [P, 25088])

        def part(lo, hi, rows=P, **dims):
            a = big[0:rows, lo:hi]
            return a.rearrange("p (a n) -> p a n", **dims) if dims else a

        wq_sb = part(0, 4096, a=H)
        wkcq_sb = part(4096, 7168, a=H)
        qkT = part(7168, 11264, a=4)
        wo_sb = part(7168, 11264, a=H)
        wqkv_sb = part(11264, 12800, a=KD)
        wout_sb = part(12800, 13312, a=KD)
        v_sb = part(13312, 15360, a=TT)
        pr = big[:, 15360:16384].rearrange("p (s q k) -> p s q k", s=2, q=2)
        prT = part(16384, 16896, a=2)
        cxT = big[:, 16896:17920].rearrange("p (s k n) -> p s k n", s=2, k=KD)
        wkr_sb = part(17920, 18432, a=H // 2)
        wkckv_sb = part(18944, 19968, HK, a=H)
        wqr_sb = big[0:96, 19968:22016].rearrange("p (h b r) -> p h b r", h=H, b=2)
        DT = big[0:96, 22016:24064].rearrange("p (s b n) -> p s b n", s=4, b=2)
        ET = part(24064, 25088, a=4)
        ctxn = part(0, 8192, a=G)
        probs = part(8192, 12288, a=4)
        accD = part(12288, 14336, a=2)
        accP = big[:, 14336:15360]
        nctx = big[:, 15360:15872]
        est = big[:, 15872:16384]
        corr = big[:, 16384:16896]
        kraw = sb("kraw", [P, KT, DC])
        kcos = sb("kcos", [P, 2, KT, DC])
        kt2 = sb("kt2", [P, KT, DC])
        kvn = sb("kvn", [P, 2, KT, DC])
        mxp = sb("mxp", [P, QT, 2])
        mx = sb("mx", [P, QT])
        mrow = sb("mrow", [QT, 2, 2, P], f32r)
        arr = sb("arr", [P, 11264], f32r)
        Q1 = arr[:, 0:2048].rearrange("p (s n) -> p s n", s=2)
        Q2 = arr[:, 2048:4096].rearrange("p (s n) -> p s n", s=2)
        kcat = arr[:, 4096:7424].rearrange("p (s n) -> p s n", s=2)
        khs = arr[:, 7424:10752].rearrange("p (s n) -> p s n", s=2)
        xhi = arr[:, 0:2048].rearrange("p (k n) -> p k n", k=KD)
        xlo = arr[:, 2048:4096].rearrange("p (k n) -> p k n", k=KD)
        whi = arr[:, 4096:4096 + 2 * FW].rearrange("p (s n) -> p s n", s=2)
        wlo = arr[:, 4096 + 2 * FW:4096 + 4 * FW].rearrange("p (s n) -> p s n", s=2)
        hhi = arr[:, 7680:8704].rearrange("p (s n) -> p s n", s=2)
        hlo = arr[:, 8704:9728].rearrange("p (s n) -> p s n", s=2)
        cT = arr[0:CROWS, 9728:10752]
        comb = arr[:, 10816:10816 + TT * CROWS].rearrange("p (t e) -> p t e", t=TT)
        ghi = arr[:, 10752:10784]
        glo = arr[:, 10784:10816]
        wring = part(8192, 8192 + 2 * FW, a=2)
        silu = big[:, 12288:13312].rearrange("p (s n) -> p s n", s=2)
        hsu = part(19000, 21048, a=4)
        hun = part(9984, 11008, a=2)
        hful = big[:, 14336:15360].rearrange("p (s n) -> p s n", s=2)
        rt = big[:, 17000:17000 + 6 * TT * E].rearrange("p (a t e) -> p a t e", a=6, t=TT)
        rs = sb("rs", [P, 6, TT])
        cmb = part(18000, 18000 + TT * E, a=TT)
        lgT = part(21100, 21100 + T, E)

        ps = es.enter_context(nc.psum_tensor("ps", [P, 8, 512], f32))

        loads = {}

        def arrived(eng, name):
            eng.wait_ge(loads[name], 16)

        names = ["x0", "x1", "consts", "wqkv", "bias", "wout", "wkr", "wkckv", "wqr", "gate", "rope"]
        names += [f"wkcq{i}" for i in range(4)] + [f"wq{i}" for i in range(4)] + [f"wo{i}" for i in range(4)]
        for n in names:
            loads[n] = sem("ld_" + n)
        ld_ctx = sem("ld_ctx")
        ld_ffw = [sem(f"ld_ffw{i}") for i in range(2)]

        early = """LN1.0 LE1.0 D.0 LT1.0 LT1.1 D.1 LN1.1 D.2 LE1.1 D.3 QK.0 QK.1 QK.2 QK.3 LT1.2 V.0 LT1.3 S.0 V.1 S.1
                   QK.4 QK.5 N.0 T.0 QK.6 N.1 T.1 C.0 QK.7 C.1 V.2 O.0 S.2 O.1 N.2 S.3 V.3 N.3 T.2 E.0 D.4 T.3 C.2
                   K.0 E.1 C.3 D.5 K.1 O.2 D.6 K.2 O.3 LN2.0 D.7 E.2 K.3 E.3 A.0 LE2.0 A.1 D.8"""
        late = """D.9 LN2.1 D.10 LT2.0 LT2.1 LE2.1 A.2 QP.0 E.4 A.3 D.11 M.0 D.12 M.1 E.5 M.2 D.13 M.3 A.4 M.4 E.6 M.5 A.5
                  M.6 D.14 M.7 LT2.2 M.8 D.15 M.9 LT2.3 W.0 M.10 E.7 M.11 M.12 A.6 M.13 A.7 M.14 M.15 MX.0 W.1 W.2
                  MT.0 MR.0 QP.1 W.3"""
        early, late = ([(a, int(b)) for a, b in (w.split(".") for w in text.split())] for text in (early, late))
        jobs = early + late
        OTHER = ("LN1", "LN2", "LE1", "LE2", "QP", "M", "MX", "MT", "MR", "N")
        evac_by = {"LT1": "act", "QK": "act", "V": "dve", "S": "act", "T": "act", "C": "dve", "O": "dve", "D": "act",
                   "E": "act", "A": "act", "W": "act", "LT2": "act", "K": "dve"}
        bank_jobs = [j for j in jobs if j[0] not in OTHER]
        bank_of, filled, done, before, user = {}, {}, {}, {}, {}
        count = {"act": 0, "dve": 0}
        for i, j in enumerate(bank_jobs):
            bank_of[j] = i % 8 if j in early else i % 3
            filled[j], before[j] = i + 1, user.get(bank_of[j])
            user[bank_of[j]] = j
            if j in early:
                early_user = dict(user)
            count[evac_by[j[0]]] += 1
            done[j] = count[evac_by[j[0]]]
        s_bank = sem("s_bank")
        s_evac = {"act": sem("s_evac_act"), "dve": sem("s_evac_dve")}

        def evacuated(eng, j):
            eng.wait_ge(s_evac[evac_by[j[0]]], done[j])

        s_link = sem("s_link")
        s_alink = sem("s_alink")
        s_ln_var = sem("s_ln_var")
        s_ln_est = sem("s_ln_est")
        s_xn = sem("s_xn")
        s_smax = sem("s_smax")
        s_probs = sem("s_probs")
        s_const = sem("s_const")
        s_rope = sem("s_rope")
        s_kraw = sem("s_kraw")
        s_plink = sem("s_plink")
        s_ktr = sem("s_ktr")
        s_khi = sem("s_khi")
        s_klo = sem("s_klo")
        s_qp = sem("s_qp")
        s_qhi = sem("s_qhi")
        s_qlo = sem("s_qlo")
        s_mch = sem("s_mch")
        s_mrd = sem("s_mrd")
        s_mx = sem("s_mx")
        s_mt = sem("s_mt")
        s_mrow = sem("s_mrow")
        s_mq = sem("s_mq")
        s_sc = sem("s_sc")
        s_exp = sem("s_exp")
        s_pv = sem("s_pv")
        s_addD = sem("s_addD")
        s_addP = sem("s_addP")
        s_acc = sem("s_acc")
        s_ctx = sem("s_ctx")
        s_sum = sem("s_sum")
        s_est = sem("s_est")
        s_rec = sem("s_rec")
        s_norm = sem("s_norm")
        s_o2 = sem("s_o2")
        s_x2 = sem("s_x2")
        s_l3 = sem("s_l3")
        s_xhi = sem("s_xhi")
        s_xlo = sem("s_xlo")
        s_gs = sem("s_gs")
        s_lg = sem("s_lg")
        s_lgs = sem("s_lgs")
        s_lgt = sem("s_lgt")
        s_rsub = sem("s_rsub")
        s_rexp = sem("s_rexp")
        s_comb = sem("s_comb")
        s_ct = sem("s_ct")
        s_ctc = sem("s_ctc")
        s_whi = sem("s_whi")
        s_wlo = sem("s_wlo")
        s_g = sem("s_g")
        s_u = sem("s_u")
        s_c = sem("s_c")
        s_silu = sem("s_silu")
        s_hu = sem("s_hu")
        s_hc = sem("s_hc")
        s_hhi = sem("s_hhi")
        s_hlo = sem("s_hlo")
        s_dn = sem("s_dn")
        s_fin = sem("s_fin")
        s_out = sem("s_out")

        NH = 2 * NF
        FIRST = (0, 2, 1, 3)
        GATE_BANK = {0: 4, 1: 4, 2: 6, 3: 6}
        N0 = 2 * NS
        PAIRS = NE // 2 - 1
        CHUNKS = (0, 2, 2, 1, 2, 1, 2, 1, 2, 2, 1, 0, 0)
        SLOTS = {0: (), 1: (1,), 2: (1, 2)}
        KPREP_AT = {(1, 5): 0, (1, 8): 1, (2, 5): 2, (2, 8): 3}
        assert sum(CHUNKS) == NCHUNK

        def chunks_beside(kt):
            return range(sum(CHUNKS[:kt]), sum(CHUNKS[:kt + 1]))

        def prepares_keys(g, kt):
            return g // UNITS + 1 < B and (g % UNITS, kt) in KPREP_AT

        def kgroup(i):
            return range(4 * i, min(4 * i + 4, KT))

        def releasedD(kt):
            return max(1, kt // 2)

        def releasedP(kt):
            return max(1, (kt - 1) // 2)

        block = es.enter_context(nc.Block())

        @block.sync
        def _(sp):
            def load(name, dst, src):
                sp.dma_start(dst, src).then_inc(loads[name], 16)

            load("x0", x_sb[:, 0:4, :], x[:, 0:4, :])
            sp.dma_start(ident[:, :], consts[:, 0:P]).then_inc(loads["consts"], 16)
            sp.dma_start(rank[:, :, :], consts[:, P:2 * P].rearrange("p (t e) -> p t e", t=TT)).then_inc(loads["consts"], 16)
            load("wkcq0", wkcq_sb[:, 0:4, :], wkcq[:, 0:4, :])
            load("wq0", wq_sb[:, 0:4, :], wq[:, 0:4, :])
            load("wqkv", wqkv_sb[:, :, :], wqkv)
            load("x1", x_sb[:, 4:8, :], x[:, 4:8, :])
            sp.dma_start(bqk_sb[:, :], bqk).then_inc(loads["bias"], 16)
            sp.dma_start(bvo_sb[:, :, :], bvo).then_inc(loads["bias"], 16)
            load("wqr", wqr_sb[:, :, :, :], wqr)
            load("wout", wout_sb[:, :, :], wout)
            load("wkr", wkr_sb[:, :, :], wkr)
            for i in range(1, 4):
                hs = slice(4 * i, 4 * i + 4)
                load(f"wkcq{i}", wkcq_sb[:, hs, :], wkcq[:, hs, :])
                load(f"wq{i}", wq_sb[:, hs, :], wq[:, hs, :])
            sp.dma_start(kraw[:, :, :], ctxk[0]).then_inc(ld_ctx, 16)
            load("rope", kcos[:, :, :, :], rope)
            load("wkckv", wkckv_sb[:, :, :], wkckv)
            load("gate", gate_sb[:, :], gate)
            sp.wait_ge(s_bank, filled[("S", B - 1)])
            for i in range(4):
                hs = slice(4 * i, 4 * i + 4)
                load(f"wo{i}", wo_sb[:, hs, :], wo[:, hs, :])
            for g in range(-1, G - 1):
                if g >= 0 and g % UNITS == 0 and g // UNITS + 1 < B:
                    sp.wait_ge(s_kraw, g // UNITS + 1)
                    sp.dma_start(kraw[:, :, :], ctxk[g // UNITS + 1]).then_inc(ld_ctx, 16)
                n = g + 1
                sp.wait_ge(s_mrow, n + 1)
                if n >= 2:
                    sp.wait_ge(s_sc, 2 * KT * (n - 1))
                for half in range(2):
                    sp.dma_start(Q2[64 + half:65 + half, n % 2, :].rearrange("o (t q) -> o t q", t=QT).bitcast(f32),
                                 mrow[:, n % 2, half, :].bitcast(f32)).then_inc(s_mq, 16)
            sp.wait_ge(s_pv, KT * G)
            sp.wait_ge(s_acc, G)

            def load_chunk(c, slot, recycled=True):
                if recycled:
                    sp.wait_ge(s_whi, c - 1)
                    sp.wait_ge(s_wlo, c - 1)
                sp.dma_start(wring[:, slot, :], ffw[bass.ds(c, 1)].rearrange("o p n -> p (o n)")).then_inc(ld_ffw[slot], 16)

            load_chunk(0, 0, False)
            load_chunk(1, 1, False)
            with sp.Fori(0, PAIRS + 1) as i:
                for slot in range(2):
                    load_chunk(i * 2 + 2 + slot, slot)
            load_chunk(NF - 1, 0)
            for i in range(4):
                sp.wait_ge(s_fin, i + 1)
                sp.dma_start(out[:, 2 * i:2 * i + 2, :], x_sb[:, 2 * i:2 * i + 2, :]).then_inc(s_out, 16)
            sp.wait_ge(s_out, 64)

        @block.tensor
        def _(pe):
            mm = nc.tensor.matmul

            def fresh_bank(j):
                if before[j]:
                    evacuated(pe, before[j])

            def key_transposes(out_bank, b, i):
                for n, kt in enumerate(kgroup(i)):
                    last = nc.tensor.transpose(ps[0:DC, out_bank, n * P:(n + 1) * P], kvn[:, b % 2, kt, :], ident[:, :])
                return last

            def scores(g, kt, between):
                n, b, m = KT * g + kt, g // UNITS, P if kt < KT - 1 else LAST
                if kt == 0:
                    pe.wait_ge(s_qlo, 2 * g + 2)
                for half in range(2):
                    cols = slice(half * 512, half * 512 + 512)
                    if n:
                        pe.wait_ge(s_exp, 2 * n - 1 + half)
                    else:
                        evacuated(pe, user[half])
                    mm(ps[0:m, half, :], kcat[:, b % 2, kt * P:kt * P + m], Q1[:, g % 2, cols], start=True, stop=False)
                    if kt == 0 and half == 0:
                        pe.wait_ge(s_mq, 32 * (g + 1))
                    mm(ps[0:m, half, :], khs[:, b % 2, kt * P:kt * P + m], Q2[:, g % 2, cols],
                       start=False, stop=True).then_inc(s_sc, 1)
                    between(half)

            def context(n, between=lambda slot: None):
                g, kt = n // KT, n % KT
                m = P if kt < KT - 1 else LAST
                if n == 0:
                    evacuated(pe, user[2])
                if kt == 0 and g:
                    pe.wait_ge(s_ctx, g)
                for r in range(2):
                    pe.wait_ge(s_exp, 2 * n + r + 1)
                    last = mm(ps[64 * r:64 * r + 64, 2, :], kvn[0:m, (g // UNITS) % 2, kt, :],
                              probs[0:m, n % 4, r * 512:r * 512 + 512], start=kt == 0, stop=kt == KT - 1)
                last.then_inc(s_pv, 1)
                between(2)

            def project_queries(g):
                b, u = g // UNITS, g % UNITS
                if g >= 1:
                    pe.wait_ge(s_mrd, NCHUNK * g)
                if g == 0:
                    evacuated(pe, ("LT2", 1))
                    for bank in range(3, 8):
                        evacuated(pe, early_user[bank])
                if g == 1:
                    pe.wait_ge(s_qlo, 2)
                for t in range(2):
                    for k in range(KD):
                        last = mm(ps[:, 6, t * S:(t + 1) * S], A_sb[:, k, u * 256 + t * P:u * 256 + (t + 1) * P],
                                  hT[:, k, b * S:(b + 1) * S], start=k == 0, stop=k == KD - 1)
                last.then_inc(s_qp, 1)

            def max_chunk(g, i):
                c = NCHUNK * g + i
                if i == 0:
                    pe.wait_ge(s_qlo, 2 * g + 1)
                if i == 1:
                    pe.wait_ge(s_qlo, 2 * g + 2)
                if i >= 2 or g:
                    pe.wait_ge(s_mrd, c - 1)
                t, half = divmod(i, 2)
                for q in range(2):
                    at = (2 * half + q) * CW
                    last = mm(ps[:, 4 + 2 * (c % 2) + q, 0:CW], Q1[:, g % 2, t * P:(t + 1) * P],
                              kcat[:, (g // UNITS) % 2, at:at + CW], start=True, stop=True)
                last.then_inc(s_mch, 1)

            def transpose_max(g):
                pe.wait_ge(s_mx, g + 1)
                nc.tensor.transpose(ps[0:QT, 3, 0:P], mx[:, :], ident[:, :]).then_inc(s_mt, 1)

            def add_up(g):
                pe.wait_ge(s_acc, g + 1)
                if g + 1 < G:
                    pe.wait_ge(s_mrow, g + 2)
                for r in range(2):
                    last = mm(ps[64 * r:64 * r + 64, 3, :], ones64[:, :], accD[:, g % 2, r * 512:r * 512 + 512],
                              start=True, stop=True)
                last.then_inc(s_sum, 1)

            for kind, i in jobs:
                j = (kind, i)
                if kind == "QP":
                    evacuated(pe, ("A", 2 * i + 1))
                    project_queries(i)
                elif kind == "M":
                    max_chunk(0, i)
                elif kind == "MT":
                    transpose_max(0)
                if kind in OTHER:
                    continue
                bk = bank_of[j]
                fresh_bank(j)
                if kind in ("LT1", "LT2"):
                    k, half = i % 2, i // 2
                    if j == ("LT1", 0):
                        pe.wait_ge(loads["consts"], 32)
                    pe.wait_ge(s_xn, (half + 1) if kind == "LT1" else half + 3)
                    for t in range(4):
                        last = nc.tensor.transpose(ps[:, bk, t * P:(t + 1) * P], xn[:, half, t, k * P:(k + 1) * P], ident[:, :])
                elif kind == "QK":
                    m, half = i % 4, i // 4
                    if i == 0:
                        arrived(pe, "wqkv")
                    evacuated(pe, ("LT1", 2 * half + 1))
                    for k in range(KD):
                        last = mm(ps[:, bk, :], wqkv_sb[:, k, m * P:(m + 1) * P], hT[:, k, half * 512:half * 512 + 512],
                                  start=k == 0, stop=k == KD - 1)
                elif kind == "V":
                    for t in range(2):
                        tok = (2 * i + t) * P
                        for k in range(KD):
                            last = mm(ps[:, bk, t * D:(t + 1) * D], hT[:, k, tok:tok + P], wqkv_sb[:, k, 2 * D:3 * D],
                                      start=k == 0, stop=k == KD - 1)
                elif kind == "S":
                    evacuated(pe, ("QK", 4 * (i // 2) + 3))
                    for q in range(2):
                        tok = i * S + q * P
                        for k in range(KD):
                            last = mm(ps[:, bk, q * S:(q + 1) * S], qkT[:, k, tok:tok + P], qkT[:, KD + k, i * S:(i + 1) * S],
                                      start=k == 0, stop=k == KD - 1)
                elif kind == "T":
                    pe.wait_ge(s_probs, i + 1)
                    for k in range(2):
                        for q in range(2):
                            last = nc.tensor.transpose(ps[:, bk, k * S + q * P:k * S + (q + 1) * P],
                                                       pr[:, i % 2, q, k * P:(k + 1) * P], ident[:, :])
                elif kind == "C":
                    evacuated(pe, ("T", i))
                    evacuated(pe, ("V", i))
                    for m in range(KD):
                        for k in range(2):
                            last = mm(ps[:, bk, m * S:(m + 1) * S], v_sb[:, 2 * i + k, m * P:(m + 1) * P], prT[:, k, :],
                                      start=k == 0, stop=k == 1)
                elif kind == "O":
                    evacuated(pe, ("C", i))
                    if i == 0:
                        arrived(pe, "wout")
                    for t in range(2):
                        for k in range(KD):
                            last = mm(ps[:, bk, t * D:(t + 1) * D], cxT[:, i % 2, k, t * P:(t + 1) * P], wout_sb[:, k, :],
                                      start=k == 0, stop=k == KD - 1)
                elif kind == "D":
                    if i % 4 == 0:
                        arrived(pe, f"wkcq{i // 4}")
                        arrived(pe, f"wq{i // 4}")
                    for b in range(2):
                        last = mm(ps[0:96, bk, b * D:(b + 1) * D], wkcq_sb[:, i, 96 * b:96 * b + 96], wq_sb[:, i, :],
                                  start=True, stop=True)
                elif kind == "E":
                    if i == 0:
                        arrived(pe, "wqr")
                    evacuated(pe, ("D", 2 * i + 1))
                    for b in range(2):
                        for r in range(2):
                            last = mm(ps[R * r:R * r + R, bk, 0:D], wqr_sb[:, 2 * i + r, b, :], DT[:, (2 * i + r) % 4, b, :],
                                      start=b == 0, stop=b == 1)
                elif kind == "A":
                    if i == 0:
                        arrived(pe, "wkr")
                    u, t = divmod(i, 2)
                    evacuated(pe, ("E", 2 * u + 1))
                    rows = slice(R * t, R * t + R)
                    for k in range(KD):
                        for r in range(2):
                            last = mm(ps[:, bk, k * P + r * DC:k * P + (r + 1) * DC], ET[rows, (2 * u + r) % 4, k * P:(k + 1) * P],
                                      wkr_sb[rows, 2 * u + r, :], start=True, stop=True)
                elif kind == "W":
                    if i == 0:
                        arrived(pe, "wkckv")
                    arrived(pe, f"wo{i}")
                    for t in range(2):
                        for r in range(2):
                            hh = 4 * i + 2 * r + t
                            last = mm(ps[64 * r:64 * r + 64, bk, t * D:(t + 1) * D], wkckv_sb[:, hh, :], wo_sb[:, hh, :],
                                      start=True, stop=True)
                elif kind == "K":
                    if i == 0:
                        pe.wait_ge(s_rope, 1)
                    last = key_transposes(bk, 0, i)
                last.then_inc(s_bank, 1)

            for g in range(G):
                for kt in range(KT):
                    def between(slot, g=g, kt=kt):
                        if g + 1 < G and slot in SLOTS[CHUNKS[kt]]:
                            max_chunk(g + 1, chunks_beside(kt)[SLOTS[CHUNKS[kt]].index(slot)])

                    scores(g, kt, between)
                    if kt == KT - 1 and g + 2 < G:
                        project_queries(g + 2)
                    if KT * g + kt > 0:
                        context(KT * g + kt - 1, between)
                    if kt == 2 and g:
                        add_up(g - 1)
                    if prepares_keys(g, kt):
                        i = KPREP_AT[g % UNITS, kt]
                        nb = g // UNITS + 1
                        if i == 0:
                            pe.wait_ge(s_rope, nb + 1)
                        pe.wait_ge(s_rec, g)
                        if i:
                            pe.wait_ge(s_klo, 4 * (nb - 1) + i)
                        key_transposes(3, nb, i).then_inc(s_ktr, 1)
                    if g + 1 < G and kt == 11:
                        if g:
                            pe.wait_ge(s_rec, g)
                        if g % UNITS in (1, 2) and g // UNITS + 1 < B:
                            pe.wait_ge(s_klo, 4 * (g // UNITS) + 2 * (g % UNITS))
                        transpose_max(g + 1)
            context(KT * G - 1)

            def project_context(i):
                pe.wait_ge(s_norm, UNITS * (i + 1))
                for t2 in range(2):
                    for p8 in range(8):
                        u, t = divmod(p8, 2)
                        last = mm(ps[:, i, t2 * D:(t2 + 1) * D], ctxn[:, UNITS * i + u, t * S + t2 * P:t * S + (t2 + 1) * P],
                                  Bo_sb[:, p8, :], start=p8 == 0, stop=p8 == 7)
                last.then_inc(s_o2, 1)

            def transpose_tokens(half):
                pe.wait_ge(s_xn, 5 + half)
                if half:
                    pe.wait_ge(s_x2, 4)
                for k in range(KD):
                    for t in range(4):
                        last = nc.tensor.transpose(ps[:, (4, 2)[half] + k, t * P:(t + 1) * P], xn[:, half, t, k * P:(k + 1) * P],
                                                   ident[:, :])
                    last.then_inc(s_l3, 1)

            def router(half):
                pe.wait_ge(s_xhi, 2 * half + 2)
                pe.wait_ge(s_xlo, 2 * half + 2)
                pe.wait_ge(s_gs, 2)
                terms = [(w, a, k) for k in range(KD) for w, a in ((ghi, xhi), (ghi, xlo), (glo, xhi))]
                for n, (w, a, k) in enumerate(terms):
                    last = mm(ps[0:E, half, :], w[:, k * E:(k + 1) * E], a[:, k, half * 512:half * 512 + 512],
                              start=n == 0, stop=n == len(terms) - 1)
                last.then_inc(s_lg, 1)

            def product(gu, slot, half, bank):
                tok = slice(half * 512, half * 512 + 512)
                terms = [(w, a, k) for k in range(KD) for w, a in ((whi, xhi), (whi, xlo), (wlo, xhi))]
                for m, (w, a, k) in enumerate(terms):
                    at = (k * 2 + gu) * P
                    last = mm(ps[:, bank, :], w[:, slot, at:at + P], a[:, k, tok], start=m == 0, stop=m == len(terms) - 1)
                last.then_inc((s_g, s_u)[gu], 1)

            def gate_up(n, slot, half):
                for gu in range(2):
                    pe.wait_ge((s_silu, s_hu)[gu], n)
                    product(gu, slot, half, 4 + gu)

            def combine_rows(n, slot, half, first=False):
                if not first:
                    pe.wait_ge(s_hc, n - 1 - N0)
                mm(ps[:, 6 + half, :], whi[0:CROWS, slot, FW - P:FW], cT[:, half * 512:half * 512 + 512],
                   start=True, stop=True).then_inc(s_c, 1)

            def down(n, slot, half, parity, first=False, final=False):
                pe.wait_ge(s_hhi, n + 1)
                pe.wait_ge(s_hlo, n + 1)
                at = 2 * KD * P
                for t in range(4):
                    tile = 4 * half + t
                    o = ps[:, tile // 2, (tile % 2) * D:(tile % 2 + 1) * D]
                    for m, (a, w) in enumerate(((hhi, whi), (hhi, wlo), (hlo, whi))):
                        last = mm(o, a[:, parity, t * P:(t + 1) * P], w[:, slot, at:at + D],
                                  start=first and m == 0 and tile % 2 == 0, stop=final and m == 2, skip_group_check=True)
                last.then_inc(s_dn, 1)

            pe.wait_ge(s_exp, 2 * KT * G)
            project_context(0)
            add_up(G - 1)
            project_context(1)
            pe.wait_ge(s_ctx, G)
            project_context(2)
            transpose_tokens(0)
            pe.wait_ge(s_rec, G)
            project_context(3)
            pe.wait_ge(s_xhi, 2)
            pe.wait_ge(s_xlo, 2)
            pe.wait_ge(s_whi, 1)
            pe.wait_ge(s_wlo, 1)
            product(0, 0, 0, 4)
            product(1, 0, 0, 5)
            pe.wait_ge(s_whi, 2)
            pe.wait_ge(s_wlo, 2)
            product(0, 1, 0, 6)
            product(1, 1, 0, 7)
            transpose_tokens(1)
            router(0)
            router(1)
            pe.wait_ge(s_silu, 1)
            product(0, 0, 1, 4)
            pe.wait_ge(s_lgs, 2)
            for t in range(TT):
                last = nc.tensor.transpose(ps[:, 2, t * E:(t + 1) * E], lgT[:, t * P:(t + 1) * P], ident[0:E, 0:E])
            last.then_inc(s_lgt, 1)
            pe.wait_ge(s_hu, 1)
            product(1, 0, 1, 5)
            down(0, 0, 0, 0, first=True)
            pe.wait_ge(s_silu, 2)
            product(0, 1, 1, 6)
            pe.wait_ge(s_rsub, 1)
            down(1, 0, 1, 1, first=True)
            pe.wait_ge(s_hu, 2)
            product(1, 1, 1, 7)
            down(2, 1, 0, 0)

            def half_chunks(c, slot, first=False):
                for half in range(2):
                    n = c * 2 + half
                    if half == 0:
                        pe.wait_ge(s_whi, c + 1)
                        pe.wait_ge(s_wlo, c + 1)
                    gate_up(n, slot, half)
                    combine_rows(n, slot, half, first=first)
                    down(n - 1, slot if half else 1 - slot, 1 - half, 1 - half)

            pe.wait_ge(s_whi, 3)
            pe.wait_ge(s_wlo, 3)
            gate_up(4, 0, 0)
            down(3, 1, 1, 1)
            gate_up(5, 0, 1)
            pe.wait_ge(s_silu, 4)
            pe.wait_ge(s_hu, 4)
            pe.wait_ge(s_comb, 1)
            for half in range(2):
                for t in range(4):
                    last = nc.tensor.transpose(ps[0:CROWS, 6 + half, t * P:(t + 1) * P], comb[:, 4 * half + t, :].bitcast(f32),
                                               ident[:, :])
                last.then_inc(s_ct, 1)
            down(4, 0, 0, 0)
            pe.wait_ge(s_ctc, 2)
            half_chunks(3, 1, first=True)
            with pe.Fori(0, PAIRS) as i:
                for slot in range(2):
                    half_chunks(i * 2 + 4 + slot, slot)
            half_chunks(NF - 1, 0)
            down(NH - 1, 0, 1, 1, final=True)

        @block.scalar
        def _(act):
            acts = nc.scalar.activation
            chain = [0]
            nc.scalar.preload_act_table_set("natural_log_exp_and_others")

            def link(ins):
                chain[0] += 1
                ins.then_inc(s_alink, 1)
                act.wait_ge(s_alink, chain[0])

            def ln_estimate(n):
                act.wait_ge(s_ln_var, n + 1)
                link(acts(lnw[:, 1, :], lnw[:, 0, :], ACT.Ln))
                acts(lnw[:, 2, :], lnw[:, 1, :], ACT.Exp, scale=-0.5).then_inc(s_ln_est, 1)

            def exponentials(g, kt):
                n, m = KT * g + kt, P if kt < KT - 1 else LAST
                if n >= 4:
                    act.wait_ge(s_pv, n - 3)
                    g4, kt4 = divmod(n - 4, KT)
                    if kt4 % 2 == 0:
                        act.wait_ge(s_addD, 6 * g4 + releasedD(kt4))
                    else:
                        act.wait_ge(s_addP, 5 * g4 + releasedP(kt4))
                for half in range(2):
                    act.wait_ge(s_sc, 2 * n + half + 1)
                    acts(probs[0:m, n % 4, half * 512:half * 512 + 512], ps[0:m, half, :], ACT.Exp).then_inc(s_exp, 1)

            def query_high(g):
                act.wait_ge(s_qp, g + 1)
                if g >= 2:
                    act.wait_ge(s_sc, 2 * KT * (g - 1))
                for r in range(2):
                    last = acts(Q1[0:64, g % 2, 512 * r:512 * r + 512], ps[64 * r:64 * r + 64, 6, :], ACT.Copy)
                last.then_inc(s_qhi, 1)

            def key_high(b, i):
                act.wait_ge(s_ktr, 4 * (b - 1) + i + 1)
                if i == 0 and b >= 2:
                    act.wait_ge(s_sc, 2 * KT * UNITS * (b - 1))
                w = len(kgroup(i)) * P
                at = slice(4 * P * i, 4 * P * i + w)
                acts(kcat[0:64, b % 2, at], ps[0:64, 3, 0:w], ACT.Copy).then_inc(s_khi, 1)
                acts(khs[0:64, b % 2, at], ps[0:64, 3, 0:w], ACT.Copy).then_inc(s_khi, 1)

            def read_context(g):
                act.wait_ge(s_pv, KT * (g + 1))
                if g:
                    act.wait_ge(s_norm, g)
                acts(nctx, ps[:, 2, :], ACT.Copy, scale=-1.0).then_inc(s_ctx, 1)

            def estimate(g):
                act.wait_ge(s_sum, g + 1)
                if g:
                    act.wait_ge(s_rec, g)
                link(acts(est, ps[:, 3, :], ACT.Ln))
                acts(est, est, ACT.Exp, scale=-1.0).then_inc(s_est, 1)

            for kind, i in jobs:
                j = (kind, i)
                if kind in ("LE1", "LE2"):
                    ln_estimate(i + (2 if kind == "LE2" else 0))
                    continue
                if kind == "QP":
                    query_high(i)
                if kind in OTHER:
                    continue
                if kind == "K":
                    act.wait_ge(s_bank, filled[j])
                    w = len(kgroup(i)) * P
                    if i == 0:
                        act.wait_ge(s_const, 1)
                    at = slice(4 * P * i, 4 * P * i + w)
                    acts(kcat[0:64, 0, at], ps[0:64, bank_of[j], 0:w], ACT.Copy).then_inc(s_khi, 1)
                    acts(khs[0:64, 0, at], ps[0:64, bank_of[j], 0:w], ACT.Copy).then_inc(s_khi, 1)
                    continue
                if evac_by[kind] != "act":
                    continue
                act.wait_ge(s_bank, filled[j])
                bk = ps[:, bank_of[j], :]
                if kind in ("LT1", "LT2"):
                    k, half = i % 2, i // 2
                    last = acts(hT[:, k, half * 512:half * 512 + 512], bk, ACT.Copy)
                elif kind == "QK":
                    m, half = i % 4, i // 4
                    if i == 0:
                        act.wait_ge(loads["bias"], 32)
                    last = acts(qkT[:, m, half * 512:half * 512 + 512], bk, ACT.Identity, bias=bqk_sb[:, m:m + 1])
                elif kind == "S":
                    act.wait_ge(s_smax, i + 1)
                    if i >= 2:
                        act.wait_ge(s_bank, filled[("T", i - 2)])
                    for q in range(2):
                        last = acts(pr[:, i % 2, q, :], bk[:, q * S:(q + 1) * S], ACT.Exp, scale=D ** -0.5,
                                    bias=smx[:, i % 2, 1, q:q + 1], accum_out=smx[:, i % 2, 2, q:q + 1])
                elif kind == "T":
                    if i:
                        act.wait_ge(s_bank, filled[("C", i - 1)])
                    last = acts(prT[:, :, :], bk.rearrange("p (k q) -> p k q", k=2), ACT.Copy)
                elif kind == "D":
                    if i >= 4:
                        act.wait_ge(s_bank, filled[("E", i // 2 - 2)])
                    last = acts(DT[:, i % 4, :, :], bk[0:96].rearrange("p (b n) -> p b n", b=2), ACT.Copy)
                elif kind == "E":
                    if i >= 4:
                        act.wait_ge(s_bank, filled[("A", 2 * (i // 2 - 2) + 1)])
                    last = acts(ET[:, i % 4, :], bk[:, 0:D], ACT.Copy)
                elif kind == "A":
                    last = acts(A_sb[:, :, i * P:(i + 1) * P], bk[:, 0:2 * P].rearrange("p (k n) -> p k n", k=2), ACT.Copy)
                elif kind == "W":
                    last = acts(Bo_sb[:, 2 * i:2 * i + 2, :], bk.rearrange("p (t n) -> p t n", t=2), ACT.Copy)
                last.then_inc(s_evac["act"], 1)

            for g in range(G):
                for kt in range(KT):
                    exponentials(g, kt)
                    if kt == 0 and g:
                        read_context(g - 1)
                    if kt == 3 and g:
                        estimate(g - 1)
                    if kt == KT - 1 and g + 2 < G:
                        query_high(g + 2)
                    if prepares_keys(g, kt):
                        key_high(g // UNITS + 1, KPREP_AT[g % UNITS, kt])
            read_context(G - 1)
            estimate(G - 1)

            def tokens_high(half):
                for k in range(KD):
                    act.wait_ge(s_l3, 2 * half + k + 1)
                    acts(xhi[:, k, half * 512:half * 512 + 512], ps[:, (4, 2)[half] + k, :], ACT.Copy).then_inc(s_xhi, 1)

            def weights_high(c, slot, turn):
                act.wait_ge(ld_ffw[slot], (turn + 1) * 16)
                acts(whi[:, slot, :], wring[:, slot, :], ACT.Copy).then_inc(s_whi, 1)

            def silu_first(i):
                n = FIRST[i]
                act.wait_ge(s_g, i + 1)
                if n >= 2:
                    act.wait_ge(s_hu, FIRST.index(n - 2) + 1)
                acts(silu[:, n % 2, :], ps[:, GATE_BANK[n], :], ACT.Silu).then_inc(s_silu, 1)

            def silu_of(n, parity):
                act.wait_ge(s_g, n + 1)
                act.wait_ge(s_hu, n - 1)
                acts(silu[:, parity, :], ps[:, 4, :], ACT.Silu).then_inc(s_silu, 1)

            def hidden_high_first(n):
                act.wait_ge(s_hu, FIRST.index(n) + 1)
                if n >= 2:
                    act.wait_ge(s_dn, n - 1)
                acts(hhi[:, n % 2, :], hsu[:, n, :], ACT.Copy).then_inc(s_hhi, 1)

            def hidden_high(n, parity, combined=True):
                if combined:
                    act.wait_ge(s_hc, n + 1 - N0)
                else:
                    act.wait_ge(s_hu, n + 1)
                act.wait_ge(s_dn, n - 1)
                acts(hhi[:, parity, :], hful[:, parity, :], ACT.Copy).then_inc(s_hhi, 1)

            ln_estimate(4)
            tokens_high(0)
            weights_high(0, 0, 0)
            weights_high(1, 1, 0)
            ln_estimate(5)
            silu_first(0)
            silu_first(1)
            tokens_high(1)
            def logits_out(half):
                act.wait_ge(s_lg, half + 1)
                acts(lgT[:, half * 512:half * 512 + 512], ps[0:E, half, :], ACT.Copy).then_inc(s_lgs, 1)

            logits_out(0)
            hidden_high_first(0)
            logits_out(1)
            silu_first(2)
            act.wait_ge(s_rsub, 1)
            acts(rt[:, 1, :, :], rt[:, 0, :, :], ACT.Exp).then_inc(s_rexp, 1)
            hidden_high_first(1)
            hidden_high_first(2)
            silu_first(3)
            act.wait_ge(s_dn, 2)
            weights_high(2, 0, 1)
            hidden_high_first(3)

            def half_chunks_act(c, slot, turn, combined=True, last=False):
                for half in range(2):
                    n = c * 2 + half
                    silu_of(n, half)
                    hidden_high(n, half, combined=combined)
                    if half == 0 and not last:
                        act.wait_ge(s_dn, c * 2)
                        weights_high(c + 1, 1 - slot, turn)

            half_chunks_act(2, 0, 1, combined=False)
            for half in range(2):
                act.wait_ge(s_ct, half + 1)
                acts(cT[:, half * 512:half * 512 + 512], ps[0:CROWS, 6 + half, :], ACT.Copy).then_inc(s_ctc, 1)
            half_chunks_act(3, 1, 2)
            with act.Fori(0, PAIRS) as i:
                for slot in range(2):
                    half_chunks_act(i * 2 + 4 + slot, slot, i + (2 + slot))
            half_chunks_act(NF - 1, 0, None, last=True)

        @block.gpsimd
        def _(pool):
            chain = [0]

            def link(ins):
                chain[0] += 1
                ins.then_inc(s_plink, 1)
                pool.wait_ge(s_plink, chain[0])

            link(nc.gpsimd.memset(ones64[:, :], 1.0))
            link(nc.gpsimd.memset(Q2[64:128, :, :].bitcast(f32), 0.0))
            link(nc.gpsimd.memset(khs[64:128, :, :].bitcast(f32), 0.0))
            nc.gpsimd.memset(khs[64:66, :, :].bitcast(f32), 1.0).then_inc(s_const, 1)
            pool.wait_ge(s_const, 1)

            def rotate(b):
                if b == 0:
                    arrived(pool, "rope")
                pool.wait_ge(ld_ctx, 16 * (b + 1))
                if b >= 2:
                    pool.wait_ge(s_pv, KT * UNITS * (b - 1))
                    pool.wait_ge(s_klo, 4 * (b - 1))
                hd = DC // 2
                nc.gpsimd.tensor_tensor(kvn[:, b % 2, :, :], kraw[:, :, :], kcos[:, 0], ALU.mult)
                nc.gpsimd.tensor_tensor(kt2[:, :, 0:hd], kraw[:, :, hd:DC], kcos[:, 1, :, 0:hd], ALU.mult)
                ins = nc.gpsimd.tensor_tensor(kt2[:, :, hd:DC], kraw[:, :, 0:hd], kcos[:, 1, :, hd:DC], ALU.mult)
                ins.then_inc(s_kraw, 1)
                pool.wait_ge(s_kraw, b + 1)
                nc.gpsimd.tensor_tensor(kvn[:, b % 2, :, :], kvn[:, b % 2, :, :], kt2[:, :, :], ALU.add).then_inc(s_rope, 1)

            rotate(0)

            def add_odd(g, kt):
                n = KT * g + kt
                pool.wait_ge(s_exp, 2 * n + 2)
                if kt == 3:
                    if g:
                        pool.wait_ge(s_acc, g)
                    nc.gpsimd.tensor_tensor(accP, probs[:, (n - 2) % 4, :], probs[:, n % 4, :], ALU.add).then_inc(s_addP, 1)
                elif kt > 3:
                    pool.wait_ge(s_addP, 5 * g + releasedP(kt) - 1)
                    nc.gpsimd.tensor_tensor(accP, accP, probs[:, n % 4, :], ALU.add).then_inc(s_addP, 1)

            def combine(g):
                pool.wait_ge(s_addD, 6 * (g + 1))
                pool.wait_ge(s_addP, 5 * (g + 1))
                a = accD[:, g % 2, :]
                nc.gpsimd.tensor_tensor(a, a, accP, ALU.add).then_inc(s_acc, 1)

            def norm(g):
                pool.wait_ge(s_rec, g + 1)
                pool.wait_ge(s_ctx, g + 1)
                nc.gpsimd.tensor_tensor(ctxn[:, g, :], corr, nctx, ALU.mult).then_inc(s_norm, 1)

            for g in range(G):
                if g:
                    combine(g - 1)
                for kt in range(1, KT, 2):
                    add_odd(g, kt)
                    if kt == 5 and g:
                        norm(g - 1)
                if g % UNITS == 0 and g // UNITS + 1 < B:
                    rotate(g // UNITS + 1)
            norm(G - 1)

            def weights_low(c, slot, turn):
                pool.wait_ge(ld_ffw[slot], (turn + 1) * 16)
                pool.wait_ge(s_whi, c + 1)
                nc.gpsimd.tensor_tensor(wlo[:, slot, 0:FW - P], wring[:, slot, 0:FW - P],
                                        whi[:, slot, 0:FW - P].bitcast(f32), ALU.subtract).then_inc(s_wlo, 1)

            weights_low(0, 0, 0)
            weights_low(1, 1, 0)
            with pool.Fori(0, PAIRS + 1) as i:
                for slot in range(2):
                    weights_low(i * 2 + 2 + slot, slot, i + 1)
            weights_low(NF - 1, 0, NF // 2)

        @block.vector
        def _(dve):
            V = nc.vector
            chain = [0]

            def link(ins):
                chain[0] += 1
                ins.then_inc(s_link, 1)
                dve.wait_ge(s_link, chain[0])

            def layer_norm(n, half):
                for t in range(4):
                    ins = V.bn_stats(stats[:, t, :], x_sb[:, 4 * half + t, :])
                link(ins)
                for t in range(4):
                    ins = V.bn_aggr(mv[:, t, :], stats[:, t, :])
                link(ins)
                V.tensor_scalar(lnw[:, 0, :], mv[:, :, 1], EPS, None, ALU.add).then_inc(s_ln_var, 1)
                dve.wait_ge(s_ln_est, n + 1)
                link(V.tensor_tensor(lnw[:, 3, :], lnw[:, 2, :], lnw[:, 2, :], ALU.mult))
                link(V.tensor_tensor(lnw[:, 3, :], lnw[:, 3, :], lnw[:, 0, :], ALU.mult))
                link(V.tensor_scalar(lnw[:, 3, :], lnw[:, 3, :], -0.5, 1.5, ALU.mult, ALU.add))
                link(V.tensor_tensor(lnw[:, 4, :], lnw[:, 3, :], lnw[:, 2, :], ALU.mult))
                if n >= 2:
                    dve.wait_ge(s_bank, filled[("LT1" if n < 4 else "LT2", 2 * half + 1)])
                for t in range(4):
                    ins = V.tensor_scalar(xn[:, half, t, :], x_sb[:, 4 * half + t, :], mv[:, t, 0:1], lnw[:, 4, t:t + 1],
                                          ALU.subtract, ALU.mult)
                ins.then_inc(s_xn, 1)

            def query_low(g):
                dve.wait_ge(s_qhi, g + 1)
                if g == 0:
                    dve.wait_ge(s_const, 1)
                V.tensor_copy(Q1[64:128, g % 2, :], Q1[0:64, g % 2, :].bitcast(f32)).then_inc(s_qlo, 1)
                for r in range(2):
                    last = V.tensor_tensor(Q2[0:64, g % 2, 512 * r:512 * r + 512], ps[64 * r:64 * r + 64, 6, :],
                                           Q1[0:64, g % 2, 512 * r:512 * r + 512].bitcast(f32), ALU.subtract)
                last.then_inc(s_qlo, 1)

            def key_low(b, i):
                dve.wait_ge(s_khi, 8 * b + 2 * (i + 1))
                w = len(kgroup(i)) * P
                at = slice(4 * P * i, 4 * P * i + w)
                V.tensor_tensor(kcat[64:128, b % 2, at], ps[0:64, 3, 0:w], kcat[0:64, b % 2, at].bitcast(f32),
                                ALU.subtract).then_inc(s_klo, 1)

            def max_chunk(g, i):
                dve.wait_ge(s_mch, NCHUNK * g + i + 1)
                if i == 0 and g:
                    dve.wait_ge(s_mx, g)
                t, half = divmod(i, 2)
                V.reduce_max(mxp[:, t, half:half + 1], ps[:, 4 + 2 * half:6 + 2 * half, 0:CW], AX.XY).then_inc(s_mrd, 1)

            def reduce_chunks(g):
                dve.wait_ge(s_mrd, NCHUNK * (g + 1))
                if g:
                    dve.wait_ge(s_mt, g)
                V.reduce_max(mx[:, :], mxp[:, :, :], AX.X).then_inc(s_mx, 1)

            def max_rows(g):
                dve.wait_ge(s_mt, g + 1)
                if g >= 2:
                    dve.wait_ge(s_mq, 32 * (g - 1))
                link(V.tensor_scalar(mrow[:, g % 2, 0, :], ps[0:QT, 3, 0:P], -1.0, None, ALU.mult))
                V.scalar_tensor_tensor(out=mrow[:, g % 2, 1, :], in0=ps[0:QT, 3, 0:P], scalar=-1.0,
                                       in1=mrow[:, g % 2, 0, :].bitcast(f32), op0=ALU.mult, op1=ALU.subtract).then_inc(s_mrow, 1)

            def add_even(g, kt):
                n, m = KT * g + kt, P if kt < KT - 1 else LAST
                if kt == 0:
                    return
                dve.wait_ge(s_exp, 2 * n + 2)
                a = accD[:, g % 2, :]
                if kt == 2:
                    if g >= 2:
                        dve.wait_ge(s_sum, g - 1)
                    V.tensor_tensor(a, probs[:, (n - 2) % 4, :], probs[:, n % 4, :], ALU.add).then_inc(s_addD, 1)
                else:
                    dve.wait_ge(s_addD, 6 * g + releasedD(kt) - 1)
                    V.tensor_tensor(a[0:m], a[0:m], probs[0:m, n % 4, :], ALU.add).then_inc(s_addD, 1)

            def reciprocal_sum(g):
                dve.wait_ge(s_est, g + 1)
                if g:
                    dve.wait_ge(s_norm, g)
                link(V.tensor_tensor(corr, est, ps[:, 3, :], ALU.mult))
                V.scalar_tensor_tensor(out=corr, in0=corr, scalar=-2.0, in1=est, op0=ALU.add, op1=ALU.mult).then_inc(s_rec, 1)

            for kind, i in jobs:
                j = (kind, i)
                if kind == "LN1":
                    arrived(dve, f"x{i}")
                    layer_norm(i, i)
                elif kind == "LN2":
                    layer_norm(2 + i, i)
                elif kind == "QP":
                    query_low(i)
                elif kind == "M":
                    max_chunk(0, i)
                elif kind == "MX":
                    reduce_chunks(0)
                elif kind == "MR":
                    max_rows(0)
                elif kind in ("MT", "LE1", "LE2"):
                    pass
                elif kind == "S":
                    dve.wait_ge(s_bank, filled[j])
                    if i >= 2:
                        dve.wait_ge(s_probs, i - 1)
                    link(V.reduce_max(smx[:, i % 2, 0, :], ps[:, bank_of[j], :].rearrange("p (q k) -> p q k", q=2), AX.X))
                    V.tensor_scalar(smx[:, i % 2, 1, :], smx[:, i % 2, 0, :], -D ** -0.5, None, ALU.mult).then_inc(s_smax, 1)
                elif kind == "N":
                    evacuated(dve, ("S", i))
                    link(V.reciprocal(smx[:, i % 2, 3, :], smx[:, i % 2, 2, :]))
                    for q in range(2):
                        ins = V.tensor_scalar(pr[:, i % 2, q, :], pr[:, i % 2, q, :], smx[:, i % 2, 3, q:q + 1], None, ALU.mult)
                    ins.then_inc(s_probs, 1)
                elif kind == "K":
                    w = len(kgroup(i)) * P
                    at = slice(4 * P * i, 4 * P * i + w)
                    dve.wait_ge(s_khi, 2 * (i + 1))
                    V.tensor_tensor(kcat[64:128, 0, at], ps[0:64, bank_of[j], 0:w], kcat[0:64, 0, at].bitcast(f32),
                                    ALU.subtract).then_inc(s_evac["dve"], 1)
                elif evac_by[kind] == "dve":
                    dve.wait_ge(s_bank, filled[j])
                    bk = ps[:, bank_of[j], :]
                    if kind == "V":
                        if i == 0:
                            dve.wait_ge(loads["bias"], 32)
                        ins = V.tensor_tensor(v_sb[:, 2 * i:2 * i + 2, :], bk.rearrange("p (t n) -> p t n", t=2),
                                              bvo_sb[:, 0:1, :].broadcast_to([P, 2, D]), ALU.add)
                    elif kind == "C":
                        if i >= 2:
                            dve.wait_ge(s_bank, filled[("O", i - 2)])
                        ins = V.tensor_copy(cxT[:, i % 2, :, :], bk.rearrange("p (k n) -> p k n", k=2))
                    elif kind == "O":
                        xt = x_sb[:, 2 * i:2 * i + 2, :]
                        link(V.tensor_tensor(xt, xt, bk.rearrange("p (t n) -> p t n", t=2), ALU.add))
                        ins = V.tensor_tensor(xt, xt, bvo_sb[:, 1:2, :].broadcast_to([P, 2, D]), ALU.add)
                    ins.then_inc(s_evac["dve"], 1)
                    if kind == "O":
                        evacuated(dve, j)

            for g in range(G):
                for kt in range(KT):
                    if kt == 4 and g:
                        reciprocal_sum(g - 1)
                    todo = list(chunks_beside(kt)) if g + 1 < G else []
                    for i in todo[:1]:
                        max_chunk(g + 1, i)
                    if prepares_keys(g, kt - 1):
                        key_low(g // UNITS + 1, KPREP_AT[g % UNITS, kt - 1])
                    if kt % 2 == 0:
                        add_even(g, kt)
                    for i in todo[1:]:
                        max_chunk(g + 1, i)
                    if kt == 10 and g + 1 < G:
                        reduce_chunks(g + 1)
                    if kt == 11 and g + 1 < G:
                        max_rows(g + 1)
                    if kt == KT - 1 and g + 2 < G:
                        query_low(g + 2)
            dve.wait_ge(s_addD, 6 * G)
            dve.wait_ge(s_addP, 5 * G)
            V.tensor_tensor(accD[:, (G - 1) % 2, :], accD[:, (G - 1) % 2, :], accP, ALU.add).then_inc(s_acc, 1)

            arrived(dve, "gate")
            dve.wait_ge(s_sc, 2 * KT * G)
            V.tensor_copy(ghi, gate_sb[:, :]).then_inc(s_gs, 1)
            dve.wait_ge(s_gs, 1)
            V.tensor_tensor(glo, gate_sb[:, :], ghi.bitcast(f32), ALU.subtract).then_inc(s_gs, 1)
            link(V.memset(comb.bitcast(f32), 0.0))

            def residual(i):
                dve.wait_ge(s_o2, i + 1)
                xt = x_sb[:, 2 * i:2 * i + 2, :]
                V.tensor_tensor(xt, xt, ps[:, i, :].rearrange("p (t n) -> p t n", t=2), ALU.add).then_inc(s_x2, 1)

            def tokens_low(half):
                at = slice(half * 512, half * 512 + 512)
                for k in range(KD):
                    dve.wait_ge(s_xhi, 2 * half + k + 1)
                    V.tensor_tensor(xlo[:, k, at], ps[:, (4, 2)[half] + k, :], xhi[:, k, at].bitcast(f32),
                                    ALU.subtract).then_inc(s_xlo, 1)

            def silu_up_first(i):
                n = FIRST[i]
                dve.wait_ge(s_u, i + 1)
                dve.wait_ge(s_silu, i + 1)
                V.tensor_tensor(hsu[:, n, :], silu[:, n % 2, :], ps[:, GATE_BANK[n] + 1, :], ALU.mult).then_inc(s_hu, 1)

            def silu_up(n, parity, shared=False, first=False):
                dve.wait_ge(s_u, n + 1)
                dve.wait_ge(s_silu, n + 1)
                if not shared and not first:
                    dve.wait_ge(s_hc, n - 1 - N0)
                dst = hful[:, parity, :] if shared else hun[:, parity, :]
                V.tensor_tensor(dst, silu[:, parity, :], ps[:, 5, :], ALU.mult).then_inc(s_hu, 1)

            def weigh(n, parity):
                dve.wait_ge(s_c, n + 1 - N0)
                dve.wait_ge(s_hu, n + 1)
                dve.wait_ge(s_hhi, n - 1)
                dve.wait_ge(s_hlo, n - 1)
                V.tensor_tensor(hful[:, parity, :], hun[:, parity, :], ps[:, 6 + parity, :], ALU.mult).then_inc(s_hc, 1)

            def hidden_low_first(n):
                dve.wait_ge(s_hhi, n + 1)
                dve.wait_ge(s_hu, FIRST.index(n) + 1)
                if n >= 2:
                    dve.wait_ge(s_dn, n - 1)
                V.tensor_tensor(hlo[:, n % 2, :], hsu[:, n, :], hhi[:, n % 2, :].bitcast(f32), ALU.subtract).then_inc(s_hlo, 1)

            def hidden_low(n, parity):
                dve.wait_ge(s_hhi, n + 1)
                dve.wait_ge(s_dn, n - 1)
                V.tensor_tensor(hlo[:, parity, :], hful[:, parity, :], hhi[:, parity, :].bitcast(f32),
                                ALU.subtract).then_inc(s_hlo, 1)

            residual(0)
            reciprocal_sum(G - 1)
            residual(1)
            dve.wait_ge(s_x2, 2)
            layer_norm(4, 0)
            tokens_low(0)
            residual(2)
            residual(3)
            dve.wait_ge(s_x2, 4)
            layer_norm(5, 1)
            silu_up_first(0)
            tokens_low(1)
            silu_up_first(1)
            hidden_low_first(0)

            def wide(a):
                return a.rearrange("p (t o) -> p t o", o=1).broadcast_to([P, TT, E])

            dve.wait_ge(s_lgt, 1)
            lg = ps[:, 2, 0:TT * E].rearrange("p (t e) -> p t e", t=TT)
            link(V.reduce_max(rs[:, 0, :], lg, AX.X))
            V.tensor_tensor(rt[:, 0], lg, wide(rs[:, 0, :]), ALU.subtract).then_inc(s_rsub, 1)
            V.memset(rt[:, 5], 0.0)
            silu_up_first(2)
            dve.wait_ge(s_rexp, 1)
            link(V.reduce_sum(rs[:, 1, :], rt[:, 1], AX.X))
            link(V.reciprocal(rs[:, 2, :], rs[:, 1, :]))
            link(V.tensor_tensor(rt[:, 1], rt[:, 1], wide(rs[:, 2, :]), ALU.mult))
            hidden_low_first(1)
            hidden_low_first(2)
            dve.wait_ge(loads["consts"], 32)
            cur = rt[:, 1]
            for turn in range(2):
                link(V.reduce_max(rs[:, 3, :], cur, AX.X))
                link(V.tensor_tensor(rt[:, 3], cur, wide(rs[:, 3, :]), ALU.is_equal))
                link(V.tensor_tensor(rt[:, 3], rt[:, 3], rank[:, :, :], ALU.mult))
                link(V.reduce_max(rs[:, 4, :], rt[:, 3], AX.X))
                link(V.tensor_tensor(rt[:, 4], rt[:, 3], wide(rs[:, 4, :]), ALU.is_equal))
                ins = V.tensor_tensor(rt[:, 5], rt[:, 5], rt[:, 4], ALU.add)
                if turn == 0:
                    silu_up_first(3)
                    ins = V.scalar_tensor_tensor(out=rt[:, 2], in0=rt[:, 4], scalar=-4.0, in1=rt[:, 1], op0=ALU.mult, op1=ALU.add)
                link(ins)
                cur = rt[:, 2]
            link(V.tensor_tensor(cmb[:, :, :], rt[:, 1], rt[:, 5], ALU.mult))
            link(V.tensor_copy(comb[:, :, 0:E], cmb[:, :, :]))
            V.tensor_tensor(comb[:, :, CROW:CROWS], cmb[:, :, :], comb[:, :, 0:E].bitcast(f32), ALU.subtract).then_inc(s_comb, 1)
            hidden_low_first(3)
            for n in (4, 5):
                silu_up(n, n % 2, shared=True)
                dve.wait_ge(s_hu, n + 1)
                hidden_low(n, n % 2)

            def weighed(n, half, first=False):
                silu_up(n, half, first=first)
                weigh(n, half)
                hidden_low(n, half)

            for half in range(2):
                weighed(N0 + half, half, first=True)
            with dve.Fori(0, PAIRS) as i:
                for slot in range(2):
                    for half in range(2):
                        weighed(i * 4 + (N0 + 2 + 2 * slot + half), half)
            for half in range(2):
                weighed(NH - 2 + half, half)
            for i in range(4):
                dve.wait_ge(s_dn, NH - 1 + i // 2)
                xt = x_sb[:, 2 * i:2 * i + 2, :]
                V.tensor_tensor(xt, xt, ps[:, i, :].rearrange("p (t n) -> p t n", t=2), ALU.add).then_inc(s_fin, 1)


def _tables():
    f = np.float32
    inv = (f(1.0) / f(10000.0) ** (np.arange(0, DC, 2, dtype=f) / f(DC))).astype(f)
    ang = np.arange(L, dtype=f)[:, None] * inv[None, :]
    sin = np.repeat(np.sin(ang), 2, axis=-1)
    cos = np.repeat(np.cos(ang), 2, axis=-1)
    sin[:, :DC // 2] = -sin[:, :DC // 2]
    sel = np.zeros((NF, P, P), f)
    for i in range(E * I):
        c, p = divmod(NS * P + i, P)
        sel[c, i // I, p] = sel[c, CROW + i // I, p] = 1.0
    rank = np.tile((E - np.arange(E)).astype(f), (P, TT))
    consts = np.concatenate([np.eye(P, dtype=f), rank], axis=1)
    return cos, sin, sel, consts


def _by_key(a):
    idx = np.minimum(np.arange(KT * P), L - 1)
    a = a[..., idx, :]
    a = a.reshape(*a.shape[:-2], KT, P, DC)
    return np.ascontiguousarray(np.swapaxes(a, -3, -2))


def _rows(a, n):
    return np.ascontiguousarray(a.reshape(n, P, -1).transpose(1, 0, 2))


def kernel(x, ctx_512, L0_attn_w_qkv, L0_attn_b_qkv, L0_attn_w_out, L0_attn_b_out, L0_xattn_Wq, L0_xattn_w_kc_q,
           L0_xattn_w_kc_kv, L0_xattn_W_qr, L0_xattn_W_kr, L0_xattn_Wo, L0_ffn_gate_w, L0_ffn_w_gate_up,
           L0_ffn_w_down, L0_ffn_shared_gate_up, L0_ffn_shared_down):
    import concourse.bacc as bacc
    from concourse.bass_utils import run_bass_kernel_spmd

    A = np.asarray
    cos, sin, sel, consts = _tables()
    gu = A(L0_ffn_w_gate_up)
    pad = NS * P - SHARED
    sgu, sdn = A(L0_ffn_shared_gate_up), A(L0_ffn_shared_down)

    def hidden(first, shared):
        a = np.concatenate([shared, np.zeros((D, pad), shared.dtype), first.transpose(1, 0, 2).reshape(D, E * I)], axis=1)
        return a.reshape(KD, P, NF, P).transpose(2, 1, 0, 3)

    gates = hidden(gu[:, :, :I], sgu[:, :SHARED])
    ups = hidden(gu[:, :, I:], sgu[:, SHARED:])
    gup = np.stack([gates, ups], axis=3).reshape(NF, P, 2 * KD * P)
    down = np.concatenate([sdn, np.zeros((pad, D), sdn.dtype), A(L0_ffn_w_down).reshape(E * I, D)]).reshape(NF, P, D)
    arrays = {
        "x": A(x).reshape(TT, P, D).transpose(1, 0, 2),
        "ctxk": _by_key(A(ctx_512)),
        "rope": np.stack([_by_key(cos), _by_key(sin)], axis=1),
        "wqkv": _rows(A(L0_attn_w_qkv).T, KD),
        "bqk": A(L0_attn_b_qkv)[:2 * D].reshape(4, P).T,
        "bvo": np.broadcast_to(np.stack([A(L0_attn_b_qkv)[2 * D:], A(L0_attn_b_out)])[None], (P, 2, D)),
        "wout": _rows(A(L0_attn_w_out).T, KD),
        "wq": A(L0_xattn_Wq).reshape(H, HK, D).transpose(1, 0, 2),
        "wkcq": A(L0_xattn_w_kc_q).transpose(1, 0, 2),
        "wqr": A(L0_xattn_W_qr).reshape(H, 2, 96, R).transpose(2, 0, 1, 3),
        "wkr": A(L0_xattn_W_kr).reshape(H // 2, 2, DC, R).transpose(1, 3, 0, 2).reshape(P, H // 2, DC),
        "wkckv": A(L0_xattn_w_kc_kv).transpose(1, 0, 2),
        "wo": A(L0_xattn_Wo).reshape(D, H, HK).transpose(2, 1, 0),
        "gate": A(L0_ffn_gate_w).T.reshape(KD, P, E).transpose(1, 0, 2).reshape(P, KD * E),
        "ffw": np.concatenate([gup, down, sel], axis=2),
        "consts": consts,
    }
    nc = bacc.Bacc("TRN2", target_bir_lowering=False, num_devices=1)
    feeds, args = {}, []
    for name, a in arrays.items():
        a = np.ascontiguousarray(a)
        feeds["in_" + name] = a
        args.append(nc.dram_tensor("in_" + name, a.shape, mybir.dt.from_np(a.dtype), kind="ExternalInput").ap())
    out = nc.dram_tensor("out_0", (P, TT, D), mybir.dt.float32, kind="ExternalOutput").ap()
    build(nc, *args, out)
    r = run_bass_kernel_spmd(nc, [feeds], core_ids=[0])
    return r.results[0]["out_0"].transpose(1, 0, 2).reshape(B, S, D)
```
